# Optimizing a Trainium2 kernel written in Bass

```python
import numpy as np
import jax
import jax.numpy as jnp

def _softmax(x, axis=-1):
    return jax.nn.softmax(x, axis=axis)

def _gelu(x):
    return jax.nn.gelu(x, approximate=True)

def _silu(x):
    return jax.nn.silu(x)

def _sigmoid(x):
    return jax.nn.sigmoid(x)

def _layernorm(x, axis=-1, eps=1e-05):
    m = jnp.mean(x, axis=axis, keepdims=True)
    v = jnp.var(x, axis=axis, keepdims=True)
    return (x - m) / jnp.sqrt(v + eps)

def _scatter_add(tgt, idx, src, axis=0):
    return tgt.at[idx].add(src)

def _segment_sum(src, seg, n):
    return jax.ops.segment_sum(src, seg, n)
kernel_name = 'mk_xattn_seq_d4_seqx_r4_3c86b7'

def setup_inputs(seed: int=0):
    np.random.seed(seed)
    _w = jnp.asarray

    def _rec_inputs():
        import jax
        import jax.numpy as jnp
        _rk = jax.random.key(seed)
        x = -0.000125 + 0.9999 * jax.random.normal(jax.random.fold_in(_rk, 1), (8, 112, 512), jnp.float32)
        _lenS = 112 - jax.random.randint(jax.random.fold_in(_rk, 7), (8,), 0, max(1, 112 // 4) + 1, jnp.int32)
        _lenS2 = 375 - jax.random.randint(jax.random.fold_in(_rk, 8), (8,), 0, max(1, 375 // 4) + 1, jnp.int32)
        _ctx_2048P = jax.random.normal(jax.random.fold_in(_rk, 11), (8, 16, 512), jnp.float32)
        _ctx_2048c = jax.random.dirichlet(jax.random.fold_in(_rk, 511), 0.3 * jnp.ones((16,), jnp.float32), (8, 375))
        _ctx_2048t = jnp.einsum('bsk,bkd->bsd', _ctx_2048c, _ctx_2048P)
        _ctx_2048t = _ctx_2048t * jax.lax.rsqrt(jnp.mean(jnp.square(_ctx_2048t)) + 1e-12) * 0.953939
        ctx_2048 = -0.00401388 + 1.00018 * (_ctx_2048t + 0.3 * jax.random.normal(jax.random.fold_in(_rk, 611), (8, 375, 512), jnp.float32))
        return (x, ctx_2048)
    x, ctx_2048 = _rec_inputs()

    def _L0_xattn_setup():
        import jax, jax.numpy as jnp
        import numpy as np
        H = 512
        B, L, S = (4, 1024, 10)
        key = jax.random.key(seed)
        k1, k2, k3, k4, k5, k6 = jax.random.split(key, 6)
        scale = 1.0 / np.sqrt(H)
        return {'h_english': jax.random.normal(k1, (B, L, H), dtype=jnp.float32), 'h_lojban': jax.random.normal(k2, (B, S, H), dtype=jnp.float32), 'w_q': jax.random.normal(k3, (H, H), dtype=jnp.float32) * scale, 'w_k': jax.random.normal(k4, (H, H), dtype=jnp.float32) * scale, 'w_v': jax.random.normal(k5, (H, H), dtype=jnp.float32) * scale, 'w_o': jax.random.normal(k6, (H, H), dtype=jnp.float32) * scale, 'alpha': jnp.float32(0.1)}
    _L0_xattn_all = _L0_xattn_setup()
    _L0_xattn_in = {k: v for k, v in _L0_xattn_all.items() if k in ('w_q', 'w_k', 'w_v', 'w_o', 'alpha')}
    del _L0_xattn_all

    def _L1_xattn_setup():
        import jax, jax.numpy as jnp
        import numpy as np
        N_HEAD = 32
        EPS = 1e-05

        def _ln(x, w, b):
            m = jnp.mean(x, axis=-1, keepdims=True)
            v = jnp.mean((x - m) ** 2, axis=-1, keepdims=True)
            return (x - m) * jax.lax.rsqrt(v + EPS) * w + b

        def _forward(x, state, i, ln1_w, ln1_b, ln2_w, ln2_b, maa_x, maa_w, maa_k, maa_v, maa_r, maa_g, maa_w1, maa_w2, time_decay, decay_w1, decay_w2, faaaa, Wr, Wk, Wv, Wg, Wo, gn_w, gn_b, fmaa_k, fmaa_r, fWk, fWr, fWv):
            B, L, C = x.shape
            H = N_HEAD
            S = C // H
            i0 = (2 + S) * i
            xa = _ln(x, ln1_w, ln1_b)
            sx = jnp.concatenate([state[:, i0 + 1][:, None], xa[:, :-1]], axis=1) - xa
            xxx = xa + sx * maa_x
            t = jnp.tanh(xxx @ maa_w1).reshape(B, L, 5, -1)
            m = jnp.einsum('blfd,fdc->blfc', t, maa_w2)
            mw, mk, mv, mr, mg = (m[:, :, j] for j in range(5))
            xw = xa + sx * (maa_w + mw)
            xk = xa + sx * (maa_k + mk)
            xv = xa + sx * (maa_v + mv)
            xr = xa + sx * (maa_r + mr)
            xg = xa + sx * (maa_g + mg)
            w = time_decay + jnp.tanh(xw @ decay_w1) @ decay_w2
            w = jnp.exp(-jnp.exp(w)).reshape(B, L, H, S)
            r = (xr @ Wr.T).reshape(B, L, H, S)
            k = (xk @ Wk.T).reshape(B, L, H, S)
            v = (xv @ Wv.T).reshape(B, L, H, S)
            g = jax.nn.silu(xg @ Wg.T)
            s0 = state[:, i0 + 2:i0 + 2 + S].reshape(B, H, S, S)

            def step(s, inp):
                k_l, v_l, w_l, r_l = inp
                a = k_l[..., :, None] * v_l[..., None, :]
                out = jnp.einsum('bhs,bhst->bht', r_l, faaaa * a + s)
                s_new = a + w_l[..., None] * s
                return (s_new, out)
            seq = tuple((z.transpose(1, 0, 2, 3) for z in (k, v, w, r)))
            _, outs = jax.lax.scan(step, s0, seq)
            y = outs.transpose(1, 0, 2, 3)
            gm = jnp.mean(y, axis=-1, keepdims=True)
            gv = jnp.mean((y - gm) ** 2, axis=-1, keepdims=True)
            y = ((y - gm) * jax.lax.rsqrt(gv + EPS)).reshape(B, L, C) * gn_w + gn_b
            x = x + y * g @ Wo.T
            xc = _ln(x, ln2_w, ln2_b)
            sxc = jnp.concatenate([state[:, i0][:, None], xc[:, :-1]], axis=1) - xc
            xk2 = xc + sxc * fmaa_k
            xr2 = xc + sxc * fmaa_r
            rr = jax.nn.sigmoid(xr2 @ fWr.T)
            kk = jnp.square(jax.nn.relu(xk2 @ fWk.T))
            x = x + rr * (kk @ fWv.T)
            return x
        key = jax.random.key(seed)
        B, L, C, H = (8, 128, 512, N_HEAD)
        S = C // H
        DM, DD = (32, 64)
        ks = jax.random.split(key, 32)
        n = lambda k, shp, s=1.0: jax.random.normal(k, shp, dtype=jnp.float32) * s
        u = lambda k, shp: jax.random.uniform(k, shp, dtype=jnp.float32)
        inp = {'x': n(ks[0], (B, L, C)), 'state': n(ks[1], (B, 2 + S, C), 0.1), 'i': 0, 'ln1_w': jnp.ones((C,), jnp.float32), 'ln1_b': jnp.zeros((C,), jnp.float32), 'ln2_w': jnp.ones((C,), jnp.float32), 'ln2_b': jnp.zeros((C,), jnp.float32), 'maa_x': u(ks[2], (C,)), 'maa_w': u(ks[3], (C,)), 'maa_k': u(ks[4], (C,)), 'maa_v': u(ks[5], (C,)), 'maa_r': u(ks[6], (C,)), 'maa_g': u(ks[7], (C,)), 'maa_w1': n(ks[8], (C, 5 * DM), 0.02), 'maa_w2': n(ks[9], (5, DM, C), 0.02), 'time_decay': n(ks[10], (C,), 0.5), 'decay_w1': n(ks[11], (C, DD), 0.02), 'decay_w2': n(ks[12], (DD, C), 0.02), 'faaaa': n(ks[13], (H, S, 1), 0.1), 'Wr': n(ks[14], (C, C), 0.02), 'Wk': n(ks[15], (C, C), 0.02), 'Wv': n(ks[16], (C, C), 0.02), 'Wg': n(ks[17], (C, C), 0.02), 'Wo': n(ks[18], (C, C), 0.02), 'gn_w': jnp.ones((C,), jnp.float32), 'gn_b': jnp.zeros((C,), jnp.float32), 'fmaa_k': u(ks[19], (C,)), 'fmaa_r': u(ks[20], (C,)), 'fWk': n(ks[21], (C, C), 0.02), 'fWr': n(ks[22], (C, C), 0.02), 'fWv': n(ks[23], (C, C), 0.02)}
        return inp
    _L1_xattn_all = _L1_xattn_setup()
    _L1_xattn_in = {k: v for k, v in _L1_xattn_all.items() if k in ('ln1_w', 'ln1_b', 'ln2_w', 'ln2_b', 'maa_x', 'maa_w', 'maa_k', 'maa_v', 'maa_r', 'maa_g', 'maa_w1', 'maa_w2', 'time_decay', 'decay_w1', 'decay_w2', 'faaaa', 'Wr', 'Wk', 'Wv', 'Wg', 'Wo', 'gn_w', 'gn_b', 'fmaa_k', 'fmaa_r', 'fWk', 'fWr', 'fWv')}
    del _L1_xattn_all

    def _L2_xattn_setup():
        import jax, jax.numpy as jnp
        import numpy as np
        E, H, L, B = (512, 32, 256, 4)
        S = E // H
        DM, DD = (32, 64)

        def _ln(x, w, b, eps=1e-05):
            m = x.mean(-1, keepdims=True)
            v = ((x - m) ** 2).mean(-1, keepdims=True)
            return (x - m) / jnp.sqrt(v + eps) * w + b

        def _block(x, state, ln1_w, ln1_b, ln2_w, ln2_b, maa_x, maa_w1, maa_w2, maa_stack, time_decay, td_w1, td_w2, u, Wr, Wk, Wv, Wg, Wo, gn_w, gn_b, ffn_maa_k, ffn_maa_r, Wfk, Wfr, Wfv):
            b, l, e = x.shape
            h = u.shape[0]
            s_ = e // h
            xa = _ln(x, ln1_w, ln1_b)
            sx = jnp.concatenate([state[:, 1:2] - xa[:, :1], xa[:, :-1] - xa[:, 1:]], axis=1)
            xxx = jnp.tanh((xa + sx * maa_x) @ maa_w1).reshape(b, l, 5, DM)
            xxx = jnp.einsum('blfd,fde->blfe', xxx, maa_w2)
            xm = xa[:, :, None] + sx[:, :, None] * (maa_stack + xxx)
            xk, xw, xv, xr, xg = (xm[:, :, j] for j in range(5))
            w = jnp.exp(-jnp.exp(time_decay + jnp.tanh(xw @ td_w1) @ td_w2)).reshape(b, l, h, s_)
            r = (xr @ Wr.T).reshape(b, l, h, s_)
            k = (xk @ Wk.T).reshape(b, l, h, s_)
            v = (xv @ Wv.T).reshape(b, l, h, s_)
            g = jax.nn.silu(xg @ Wg.T)
            s0 = state[:, 2:2 + s_].reshape(b, h, s_, s_)

            def step(s, rkvw):
                r_t, k_t, v_t, w_t = rkvw
                a = k_t[..., :, None] * v_t[..., None, :]
                out = jnp.einsum('bhi,bhij->bhj', r_t, u * a + s)
                s = a + w_t[..., :, None] * s
                return (s, out)
            rkvw = tuple((jnp.moveaxis(t, 1, 0) for t in (r, k, v, w)))
            _, out = jax.lax.scan(step, s0, rkvw)
            out = jnp.moveaxis(out, 0, 1).reshape(b, l, e)
            og = out.reshape(b, l, h, s_)
            m = og.mean(-1, keepdims=True)
            va = ((og - m) ** 2).mean(-1, keepdims=True)
            og = ((og - m) / jnp.sqrt(va + 1e-05)).reshape(b, l, e) * gn_w + gn_b
            x1 = x + og * g @ Wo.T
            xc = _ln(x1, ln2_w, ln2_b)
            sx2 = jnp.concatenate([state[:, 0:1] - xc[:, :1], xc[:, :-1] - xc[:, 1:]], axis=1)
            xk2 = xc + sx2 * ffn_maa_k
            xr2 = xc + sx2 * ffn_maa_r
            rr = jax.nn.sigmoid(xr2 @ Wfr.T)
            kk = jnp.square(jax.nn.relu(xk2 @ Wfk.T))
            return x1 + rr * (kk @ Wfv.T)
        key = jax.random.key(seed)
        ks = jax.random.split(key, 24)
        sc = 0.02
        d = {'x': jax.random.normal(ks[0], (B, L, E), jnp.float32), 'state': jax.random.normal(ks[1], (B, 2 + S, E), jnp.float32) * 0.1, 'ln1_w': jnp.ones((E,), jnp.float32), 'ln1_b': jnp.zeros((E,), jnp.float32), 'ln2_w': jnp.ones((E,), jnp.float32), 'ln2_b': jnp.zeros((E,), jnp.float32), 'maa_x': jax.random.normal(ks[2], (E,), jnp.float32) * 0.1, 'maa_w1': jax.random.normal(ks[3], (E, 5 * DM), jnp.float32) * sc, 'maa_w2': jax.random.normal(ks[4], (5, DM, E), jnp.float32) * sc, 'maa_stack': jax.random.normal(ks[5], (1, 5, E), jnp.float32) * 0.1, 'time_decay': jax.random.normal(ks[6], (E,), jnp.float32) * 0.5, 'td_w1': jax.random.normal(ks[7], (E, DD), jnp.float32) * sc, 'td_w2': jax.random.normal(ks[8], (DD, E), jnp.float32) * sc, 'u': jax.random.normal(ks[9], (H, S, 1), jnp.float32) * 0.1, 'Wr': jax.random.normal(ks[10], (E, E), jnp.float32) * sc, 'Wk': jax.random.normal(ks[11], (E, E), jnp.float32) * sc, 'Wv': jax.random.normal(ks[12], (E, E), jnp.float32) * sc, 'Wg': jax.random.normal(ks[13], (E, E), jnp.float32) * sc, 'Wo': jax.random.normal(ks[14], (E, E), jnp.float32) * sc, 'gn_w': jnp.ones((E,), jnp.float32), 'gn_b': jnp.zeros((E,), jnp.float32), 'ffn_maa_k': jax.random.normal(ks[15], (E,), jnp.float32) * 0.1, 'ffn_maa_r': jax.random.normal(ks[16], (E,), jnp.float32) * 0.1, 'Wfk': jax.random.normal(ks[17], (E, E), jnp.float32) * sc, 'Wfr': jax.random.normal(ks[18], (E, E), jnp.float32) * sc, 'Wfv': jax.random.normal(ks[19], (E, E), jnp.float32) * sc}
        return d
    _L2_xattn_all = _L2_xattn_setup()
    _L2_xattn_in = {k: v for k, v in _L2_xattn_all.items() if k in ('ln1_w', 'ln1_b', 'ln2_w', 'ln2_b', 'maa_x', 'maa_w1', 'maa_w2', 'maa_stack', 'time_decay', 'td_w1', 'td_w2', 'u', 'Wr', 'Wk', 'Wv', 'Wg', 'Wo', 'gn_w', 'gn_b', 'ffn_maa_k', 'ffn_maa_r', 'Wfk', 'Wfr', 'Wfv')}
    del _L2_xattn_all

    def _L3_xattn_setup():
        import jax, jax.numpy as jnp
        import numpy as np
        B, Q, S1, S2 = (4, 64, 512, 512)
        D, H, K, F = (512, 16, 128, 2048)
        LN_EPS = 1e-05

        def _layer_norm(x, scale, offset):
            mu = jnp.mean(x, axis=-1, keepdims=True)
            var = jnp.var(x, axis=-1, keepdims=True)
            return (x - mu) * jax.lax.rsqrt(var + LN_EPS) * scale + offset

        def _cross_attention(q_in, kv_in, wq, bq, wk, bk, wv, bv, wo, bo, bias_k, bias_v):
            b, q_len, _ = q_in.shape
            t = kv_in.shape[1]
            qh = (q_in @ wq + bq).reshape(b, q_len, H, K)
            kh = (kv_in @ wk + bk).reshape(b, t, H, K)
            vh = (kv_in @ wv + bv).reshape(b, t, H, K)
            kh = jnp.concatenate([kh, jnp.broadcast_to(bias_k, (b, 1, H, K))], axis=1)
            vh = jnp.concatenate([vh, jnp.broadcast_to(bias_v, (b, 1, H, K))], axis=1)
            scale = jnp.sqrt(jnp.asarray(K, q_in.dtype))
            logits = jnp.einsum('bqhk,bthk->bhqt', qh, kh) / scale
            weights = jax.nn.softmax(logits, axis=-1)
            ctx = jnp.einsum('bhqt,bthk->bqhk', weights, vh).reshape(b, q_len, H * K)
            return ctx @ wo + bo

        def _forward(x, xf_1, xf_2, ln1_scale, ln1_offset, wq1, bq1, wk1, bk1, wv1, bv1, wo1, bo1, bias_k1, bias_v1, ln2_scale, ln2_offset, wq2, bq2, wk2, bk2, wv2, bv2, wo2, bo2, bias_k2, bias_v2, ln_mlp_scale, ln_mlp_offset, w_fc1, b_fc1, w_fc2, b_fc2):
            res = x
            h = _layer_norm(x, ln1_scale, ln1_offset)
            x = res + _cross_attention(h, xf_1, wq1, bq1, wk1, bk1, wv1, bv1, wo1, bo1, bias_k1, bias_v1)
            res = x
            h = _layer_norm(x, ln2_scale, ln2_offset)
            x = res + _cross_attention(h, xf_2, wq2, bq2, wk2, bk2, wv2, bv2, wo2, bo2, bias_k2, bias_v2)
            h = _layer_norm(x, ln_mlp_scale, ln_mlp_offset)
            h = jax.nn.gelu(h @ w_fc1 + b_fc1, approximate=False) @ w_fc2 + b_fc2
            return x + h
        key = jax.random.key(seed)
        ks = iter(jax.random.split(key, 64))

        def rn(shape, s=0.02):
            return jax.random.normal(next(ks), shape, jnp.float32) * s
        inp = {'x': rn((B, Q, D), 1.0), 'xf_1': rn((B, S1, D), 1.0), 'xf_2': rn((B, S2, D), 1.0)}
        for i in (1, 2):
            inp[f'ln{i}_scale'] = jnp.ones((D,), jnp.float32)
            inp[f'ln{i}_offset'] = jnp.zeros((D,), jnp.float32)
            inp[f'wq{i}'] = rn((D, H * K))
            inp[f'bq{i}'] = jnp.zeros((H * K,), jnp.float32)
            inp[f'wk{i}'] = rn((D, H * K))
            inp[f'bk{i}'] = jnp.zeros((H * K,), jnp.float32)
            inp[f'wv{i}'] = rn((D, H * K))
            inp[f'bv{i}'] = jnp.zeros((H * K,), jnp.float32)
            inp[f'wo{i}'] = rn((H * K, D))
            inp[f'bo{i}'] = jnp.zeros((D,), jnp.float32)
            inp[f'bias_k{i}'] = rn((1, 1, H, K))
            inp[f'bias_v{i}'] = rn((1, 1, H, K))
        inp['ln_mlp_scale'] = jnp.ones((D,), jnp.float32)
        inp['ln_mlp_offset'] = jnp.zeros((D,), jnp.float32)
        inp['w_fc1'] = rn((D, F))
        inp['b_fc1'] = jnp.zeros((F,), jnp.float32)
        inp['w_fc2'] = rn((F, D))
        inp['b_fc2'] = jnp.zeros((D,), jnp.float32)
        return inp
    _L3_xattn_all = _L3_xattn_setup()
    _L3_xattn_in = {k: v for k, v in _L3_xattn_all.items() if k in ('ln1_scale', 'ln1_offset', 'wq1', 'bq1', 'wk1', 'bk1', 'wv1', 'bv1', 'wo1', 'bo1', 'bias_k1', 'bias_v1', 'ln2_scale', 'ln2_offset', 'wq2', 'bq2', 'wk2', 'bk2', 'wv2', 'bv2', 'wo2', 'bo2', 'bias_k2', 'bias_v2', 'ln_mlp_scale', 'ln_mlp_offset', 'w_fc1', 'b_fc1', 'w_fc2', 'b_fc2')}
    del _L3_xattn_all
    return {'x': x, 'ctx_2048': ctx_2048, 'L0_xattn_w_q': _L0_xattn_in['w_q'], 'L0_xattn_w_k': _L0_xattn_in['w_k'], 'L0_xattn_w_v': _L0_xattn_in['w_v'], 'L0_xattn_w_o': _L0_xattn_in['w_o'], 'L0_xattn_alpha': _L0_xattn_in['alpha'], 'L1_xattn_ln1_w': _L1_xattn_in['ln1_w'], 'L1_xattn_ln1_b': _L1_xattn_in['ln1_b'], 'L1_xattn_ln2_w': _L1_xattn_in['ln2_w'], 'L1_xattn_ln2_b': _L1_xattn_in['ln2_b'], 'L1_xattn_maa_x': _L1_xattn_in['maa_x'], 'L1_xattn_maa_w': _L1_xattn_in['maa_w'], 'L1_xattn_maa_k': _L1_xattn_in['maa_k'], 'L1_xattn_maa_v': _L1_xattn_in['maa_v'], 'L1_xattn_maa_r': _L1_xattn_in['maa_r'], 'L1_xattn_maa_g': _L1_xattn_in['maa_g'], 'L1_xattn_maa_w1': _L1_xattn_in['maa_w1'], 'L1_xattn_maa_w2': _L1_xattn_in['maa_w2'], 'L1_xattn_time_decay': _L1_xattn_in['time_decay'], 'L1_xattn_decay_w1': _L1_xattn_in['decay_w1'], 'L1_xattn_decay_w2': _L1_xattn_in['decay_w2'], 'L1_xattn_faaaa': _L1_xattn_in['faaaa'], 'L1_xattn_Wr': _L1_xattn_in['Wr'], 'L1_xattn_Wk': _L1_xattn_in['Wk'], 'L1_xattn_Wv': _L1_xattn_in['Wv'], 'L1_xattn_Wg': _L1_xattn_in['Wg'], 'L1_xattn_Wo': _L1_xattn_in['Wo'], 'L1_xattn_gn_w': _L1_xattn_in['gn_w'], 'L1_xattn_gn_b': _L1_xattn_in['gn_b'], 'L1_xattn_fmaa_k': _L1_xattn_in['fmaa_k'], 'L1_xattn_fmaa_r': _L1_xattn_in['fmaa_r'], 'L1_xattn_fWk': _L1_xattn_in['fWk'], 'L1_xattn_fWr': _L1_xattn_in['fWr'], 'L1_xattn_fWv': _L1_xattn_in['fWv'], 'L2_xattn_ln1_w': _L2_xattn_in['ln1_w'], 'L2_xattn_ln1_b': _L2_xattn_in['ln1_b'], 'L2_xattn_ln2_w': _L2_xattn_in['ln2_w'], 'L2_xattn_ln2_b': _L2_xattn_in['ln2_b'], 'L2_xattn_maa_x': _L2_xattn_in['maa_x'], 'L2_xattn_maa_w1': _L2_xattn_in['maa_w1'], 'L2_xattn_maa_w2': _L2_xattn_in['maa_w2'], 'L2_xattn_maa_stack': _L2_xattn_in['maa_stack'], 'L2_xattn_time_decay': _L2_xattn_in['time_decay'], 'L2_xattn_td_w1': _L2_xattn_in['td_w1'], 'L2_xattn_td_w2': _L2_xattn_in['td_w2'], 'L2_xattn_u': _L2_xattn_in['u'], 'L2_xattn_Wr': _L2_xattn_in['Wr'], 'L2_xattn_Wk': _L2_xattn_in['Wk'], 'L2_xattn_Wv': _L2_xattn_in['Wv'], 'L2_xattn_Wg': _L2_xattn_in['Wg'], 'L2_xattn_Wo': _L2_xattn_in['Wo'], 'L2_xattn_gn_w': _L2_xattn_in['gn_w'], 'L2_xattn_gn_b': _L2_xattn_in['gn_b'], 'L2_xattn_ffn_maa_k': _L2_xattn_in['ffn_maa_k'], 'L2_xattn_ffn_maa_r': _L2_xattn_in['ffn_maa_r'], 'L2_xattn_Wfk': _L2_xattn_in['Wfk'], 'L2_xattn_Wfr': _L2_xattn_in['Wfr'], 'L2_xattn_Wfv': _L2_xattn_in['Wfv'], 'L3_xattn_ln1_scale': _L3_xattn_in['ln1_scale'], 'L3_xattn_ln1_offset': _L3_xattn_in['ln1_offset'], 'L3_xattn_wq1': _L3_xattn_in['wq1'], 'L3_xattn_bq1': _L3_xattn_in['bq1'], 'L3_xattn_wk1': _L3_xattn_in['wk1'], 'L3_xattn_bk1': _L3_xattn_in['bk1'], 'L3_xattn_wv1': _L3_xattn_in['wv1'], 'L3_xattn_bv1': _L3_xattn_in['bv1'], 'L3_xattn_wo1': _L3_xattn_in['wo1'], 'L3_xattn_bo1': _L3_xattn_in['bo1'], 'L3_xattn_bias_k1': _L3_xattn_in['bias_k1'], 'L3_xattn_bias_v1': _L3_xattn_in['bias_v1'], 'L3_xattn_ln2_scale': _L3_xattn_in['ln2_scale'], 'L3_xattn_ln2_offset': _L3_xattn_in['ln2_offset'], 'L3_xattn_wq2': _L3_xattn_in['wq2'], 'L3_xattn_bq2': _L3_xattn_in['bq2'], 'L3_xattn_wk2': _L3_xattn_in['wk2'], 'L3_xattn_bk2': _L3_xattn_in['bk2'], 'L3_xattn_wv2': _L3_xattn_in['wv2'], 'L3_xattn_bv2': _L3_xattn_in['bv2'], 'L3_xattn_wo2': _L3_xattn_in['wo2'], 'L3_xattn_bo2': _L3_xattn_in['bo2'], 'L3_xattn_bias_k2': _L3_xattn_in['bias_k2'], 'L3_xattn_bias_v2': _L3_xattn_in['bias_v2'], 'L3_xattn_ln_mlp_scale': _L3_xattn_in['ln_mlp_scale'], 'L3_xattn_ln_mlp_offset': _L3_xattn_in['ln_mlp_offset'], 'L3_xattn_w_fc1': _L3_xattn_in['w_fc1'], 'L3_xattn_b_fc1': _L3_xattn_in['b_fc1'], 'L3_xattn_w_fc2': _L3_xattn_in['w_fc2'], 'L3_xattn_b_fc2': _L3_xattn_in['b_fc2']}

def reference(x, ctx_2048, L0_xattn_w_q, L0_xattn_w_k, L0_xattn_w_v, L0_xattn_w_o, L0_xattn_alpha, L1_xattn_ln1_w, L1_xattn_ln1_b, L1_xattn_ln2_w, L1_xattn_ln2_b, L1_xattn_maa_x, L1_xattn_maa_w, L1_xattn_maa_k, L1_xattn_maa_v, L1_xattn_maa_r, L1_xattn_maa_g, L1_xattn_maa_w1, L1_xattn_maa_w2, L1_xattn_time_decay, L1_xattn_decay_w1, L1_xattn_decay_w2, L1_xattn_faaaa, L1_xattn_Wr, L1_xattn_Wk, L1_xattn_Wv, L1_xattn_Wg, L1_xattn_Wo, L1_xattn_gn_w, L1_xattn_gn_b, L1_xattn_fmaa_k, L1_xattn_fmaa_r, L1_xattn_fWk, L1_xattn_fWr, L1_xattn_fWv, L2_xattn_ln1_w, L2_xattn_ln1_b, L2_xattn_ln2_w, L2_xattn_ln2_b, L2_xattn_maa_x, L2_xattn_maa_w1, L2_xattn_maa_w2, L2_xattn_maa_stack, L2_xattn_time_decay, L2_xattn_td_w1, L2_xattn_td_w2, L2_xattn_u, L2_xattn_Wr, L2_xattn_Wk, L2_xattn_Wv, L2_xattn_Wg, L2_xattn_Wo, L2_xattn_gn_w, L2_xattn_gn_b, L2_xattn_ffn_maa_k, L2_xattn_ffn_maa_r, L2_xattn_Wfk, L2_xattn_Wfr, L2_xattn_Wfv, L3_xattn_ln1_scale, L3_xattn_ln1_offset, L3_xattn_wq1, L3_xattn_bq1, L3_xattn_wk1, L3_xattn_bk1, L3_xattn_wv1, L3_xattn_bv1, L3_xattn_wo1, L3_xattn_bo1, L3_xattn_bias_k1, L3_xattn_bias_v1, L3_xattn_ln2_scale, L3_xattn_ln2_offset, L3_xattn_wq2, L3_xattn_bq2, L3_xattn_wk2, L3_xattn_bk2, L3_xattn_wv2, L3_xattn_bv2, L3_xattn_wo2, L3_xattn_bo2, L3_xattn_bias_k2, L3_xattn_bias_v2, L3_xattn_ln_mlp_scale, L3_xattn_ln_mlp_offset, L3_xattn_w_fc1, L3_xattn_b_fc1, L3_xattn_w_fc2, L3_xattn_b_fc2):
    import jax
    import jax.numpy as jnp

    def _L0_xattn_ref(h_english, h_lojban, w_q, w_k, w_v, w_o, alpha):
        import jax, jax.numpy as jnp
        import numpy as np
        H = 512
        B, L, S = (4, 1024, 10)
        h = h_english.shape[-1]
        q = jnp.einsum('blh,oh->blo', h_english, w_q)
        k = jnp.einsum('bsh,oh->bso', h_lojban, w_k)
        v = jnp.einsum('bsh,oh->bso', h_lojban, w_v)
        scores = jnp.einsum('blh,bsh->bls', q, k) / jnp.sqrt(jnp.float32(h))
        probs = jax.nn.softmax(scores, axis=-1)
        context = jnp.einsum('bls,bsh->blh', probs, v)
        delta = jnp.einsum('blh,oh->blo', context, w_o)
        return h_english + alpha * delta

    def _L1_xattn_ref(x, state, i, ln1_w, ln1_b, ln2_w, ln2_b, maa_x, maa_w, maa_k, maa_v, maa_r, maa_g, maa_w1, maa_w2, time_decay, decay_w1, decay_w2, faaaa, Wr, Wk, Wv, Wg, Wo, gn_w, gn_b, fmaa_k, fmaa_r, fWk, fWr, fWv):
        import jax, jax.numpy as jnp
        import numpy as np
        N_HEAD = 32
        EPS = 1e-05

        def _ln(x, w, b):
            m = jnp.mean(x, axis=-1, keepdims=True)
            v = jnp.mean((x - m) ** 2, axis=-1, keepdims=True)
            return (x - m) * jax.lax.rsqrt(v + EPS) * w + b

        def _forward(x, state, i, ln1_w, ln1_b, ln2_w, ln2_b, maa_x, maa_w, maa_k, maa_v, maa_r, maa_g, maa_w1, maa_w2, time_decay, decay_w1, decay_w2, faaaa, Wr, Wk, Wv, Wg, Wo, gn_w, gn_b, fmaa_k, fmaa_r, fWk, fWr, fWv):
            B, L, C = x.shape
            H = N_HEAD
            S = C // H
            i0 = (2 + S) * i
            xa = _ln(x, ln1_w, ln1_b)
            sx = jnp.concatenate([state[:, i0 + 1][:, None], xa[:, :-1]], axis=1) - xa
            xxx = xa + sx * maa_x
            t = jnp.tanh(xxx @ maa_w1).reshape(B, L, 5, -1)
            m = jnp.einsum('blfd,fdc->blfc', t, maa_w2)
            mw, mk, mv, mr, mg = (m[:, :, j] for j in range(5))
            xw = xa + sx * (maa_w + mw)
            xk = xa + sx * (maa_k + mk)
            xv = xa + sx * (maa_v + mv)
            xr = xa + sx * (maa_r + mr)
            xg = xa + sx * (maa_g + mg)
            w = time_decay + jnp.tanh(xw @ decay_w1) @ decay_w2
            w = jnp.exp(-jnp.exp(w)).reshape(B, L, H, S)
            r = (xr @ Wr.T).reshape(B, L, H, S)
            k = (xk @ Wk.T).reshape(B, L, H, S)
            v = (xv @ Wv.T).reshape(B, L, H, S)
            g = jax.nn.silu(xg @ Wg.T)
            s0 = state[:, i0 + 2:i0 + 2 + S].reshape(B, H, S, S)

            def step(s, inp):
                k_l, v_l, w_l, r_l = inp
                a = k_l[..., :, None] * v_l[..., None, :]
                out = jnp.einsum('bhs,bhst->bht', r_l, faaaa * a + s)
                s_new = a + w_l[..., None] * s
                return (s_new, out)
            seq = tuple((z.transpose(1, 0, 2, 3) for z in (k, v, w, r)))
            _, outs = jax.lax.scan(step, s0, seq)
            y = outs.transpose(1, 0, 2, 3)
            gm = jnp.mean(y, axis=-1, keepdims=True)
            gv = jnp.mean((y - gm) ** 2, axis=-1, keepdims=True)
            y = ((y - gm) * jax.lax.rsqrt(gv + EPS)).reshape(B, L, C) * gn_w + gn_b
            x = x + y * g @ Wo.T
            xc = _ln(x, ln2_w, ln2_b)
            sxc = jnp.concatenate([state[:, i0][:, None], xc[:, :-1]], axis=1) - xc
            xk2 = xc + sxc * fmaa_k
            xr2 = xc + sxc * fmaa_r
            rr = jax.nn.sigmoid(xr2 @ fWr.T)
            kk = jnp.square(jax.nn.relu(xk2 @ fWk.T))
            x = x + rr * (kk @ fWv.T)
            return x
        return _forward(x, state, i, ln1_w, ln1_b, ln2_w, ln2_b, maa_x, maa_w, maa_k, maa_v, maa_r, maa_g, maa_w1, maa_w2, time_decay, decay_w1, decay_w2, faaaa, Wr, Wk, Wv, Wg, Wo, gn_w, gn_b, fmaa_k, fmaa_r, fWk, fWr, fWv)

    def _L2_xattn_ref(x, state, ln1_w, ln1_b, ln2_w, ln2_b, maa_x, maa_w1, maa_w2, maa_stack, time_decay, td_w1, td_w2, u, Wr, Wk, Wv, Wg, Wo, gn_w, gn_b, ffn_maa_k, ffn_maa_r, Wfk, Wfr, Wfv):
        import jax, jax.numpy as jnp
        import numpy as np
        E, H, L, B = (512, 32, 256, 4)
        S = E // H
        DM, DD = (32, 64)

        def _ln(x, w, b, eps=1e-05):
            m = x.mean(-1, keepdims=True)
            v = ((x - m) ** 2).mean(-1, keepdims=True)
            return (x - m) / jnp.sqrt(v + eps) * w + b

        def _block(x, state, ln1_w, ln1_b, ln2_w, ln2_b, maa_x, maa_w1, maa_w2, maa_stack, time_decay, td_w1, td_w2, u, Wr, Wk, Wv, Wg, Wo, gn_w, gn_b, ffn_maa_k, ffn_maa_r, Wfk, Wfr, Wfv):
            b, l, e = x.shape
            h = u.shape[0]
            s_ = e // h
            xa = _ln(x, ln1_w, ln1_b)
            sx = jnp.concatenate([state[:, 1:2] - xa[:, :1], xa[:, :-1] - xa[:, 1:]], axis=1)
            xxx = jnp.tanh((xa + sx * maa_x) @ maa_w1).reshape(b, l, 5, DM)
            xxx = jnp.einsum('blfd,fde->blfe', xxx, maa_w2)
            xm = xa[:, :, None] + sx[:, :, None] * (maa_stack + xxx)
            xk, xw, xv, xr, xg = (xm[:, :, j] for j in range(5))
            w = jnp.exp(-jnp.exp(time_decay + jnp.tanh(xw @ td_w1) @ td_w2)).reshape(b, l, h, s_)
            r = (xr @ Wr.T).reshape(b, l, h, s_)
            k = (xk @ Wk.T).reshape(b, l, h, s_)
            v = (xv @ Wv.T).reshape(b, l, h, s_)
            g = jax.nn.silu(xg @ Wg.T)
            s0 = state[:, 2:2 + s_].reshape(b, h, s_, s_)

            def step(s, rkvw):
                r_t, k_t, v_t, w_t = rkvw
                a = k_t[..., :, None] * v_t[..., None, :]
                out = jnp.einsum('bhi,bhij->bhj', r_t, u * a + s)
                s = a + w_t[..., :, None] * s
                return (s, out)
            rkvw = tuple((jnp.moveaxis(t, 1, 0) for t in (r, k, v, w)))
            _, out = jax.lax.scan(step, s0, rkvw)
            out = jnp.moveaxis(out, 0, 1).reshape(b, l, e)
            og = out.reshape(b, l, h, s_)
            m = og.mean(-1, keepdims=True)
            va = ((og - m) ** 2).mean(-1, keepdims=True)
            og = ((og - m) / jnp.sqrt(va + 1e-05)).reshape(b, l, e) * gn_w + gn_b
            x1 = x + og * g @ Wo.T
            xc = _ln(x1, ln2_w, ln2_b)
            sx2 = jnp.concatenate([state[:, 0:1] - xc[:, :1], xc[:, :-1] - xc[:, 1:]], axis=1)
            xk2 = xc + sx2 * ffn_maa_k
            xr2 = xc + sx2 * ffn_maa_r
            rr = jax.nn.sigmoid(xr2 @ Wfr.T)
            kk = jnp.square(jax.nn.relu(xk2 @ Wfk.T))
            return x1 + rr * (kk @ Wfv.T)
        return _block(x, state, ln1_w, ln1_b, ln2_w, ln2_b, maa_x, maa_w1, maa_w2, maa_stack, time_decay, td_w1, td_w2, u, Wr, Wk, Wv, Wg, Wo, gn_w, gn_b, ffn_maa_k, ffn_maa_r, Wfk, Wfr, Wfv)

    def _L3_xattn_ref(x, xf_1, xf_2, ln1_scale, ln1_offset, wq1, bq1, wk1, bk1, wv1, bv1, wo1, bo1, bias_k1, bias_v1, ln2_scale, ln2_offset, wq2, bq2, wk2, bk2, wv2, bv2, wo2, bo2, bias_k2, bias_v2, ln_mlp_scale, ln_mlp_offset, w_fc1, b_fc1, w_fc2, b_fc2):
        import jax, jax.numpy as jnp
        import numpy as np
        B, Q, S1, S2 = (4, 64, 512, 512)
        D, H, K, F = (512, 16, 128, 2048)
        LN_EPS = 1e-05

        def _layer_norm(x, scale, offset):
            mu = jnp.mean(x, axis=-1, keepdims=True)
            var = jnp.var(x, axis=-1, keepdims=True)
            return (x - mu) * jax.lax.rsqrt(var + LN_EPS) * scale + offset

        def _cross_attention(q_in, kv_in, wq, bq, wk, bk, wv, bv, wo, bo, bias_k, bias_v):
            b, q_len, _ = q_in.shape
            t = kv_in.shape[1]
            qh = (q_in @ wq + bq).reshape(b, q_len, H, K)
            kh = (kv_in @ wk + bk).reshape(b, t, H, K)
            vh = (kv_in @ wv + bv).reshape(b, t, H, K)
            kh = jnp.concatenate([kh, jnp.broadcast_to(bias_k, (b, 1, H, K))], axis=1)
            vh = jnp.concatenate([vh, jnp.broadcast_to(bias_v, (b, 1, H, K))], axis=1)
            scale = jnp.sqrt(jnp.asarray(K, q_in.dtype))
            logits = jnp.einsum('bqhk,bthk->bhqt', qh, kh) / scale
            weights = jax.nn.softmax(logits, axis=-1)
            ctx = jnp.einsum('bhqt,bthk->bqhk', weights, vh).reshape(b, q_len, H * K)
            return ctx @ wo + bo

        def _forward(x, xf_1, xf_2, ln1_scale, ln1_offset, wq1, bq1, wk1, bk1, wv1, bv1, wo1, bo1, bias_k1, bias_v1, ln2_scale, ln2_offset, wq2, bq2, wk2, bk2, wv2, bv2, wo2, bo2, bias_k2, bias_v2, ln_mlp_scale, ln_mlp_offset, w_fc1, b_fc1, w_fc2, b_fc2):
            res = x
            h = _layer_norm(x, ln1_scale, ln1_offset)
            x = res + _cross_attention(h, xf_1, wq1, bq1, wk1, bk1, wv1, bv1, wo1, bo1, bias_k1, bias_v1)
            res = x
            h = _layer_norm(x, ln2_scale, ln2_offset)
            x = res + _cross_attention(h, xf_2, wq2, bq2, wk2, bk2, wv2, bv2, wo2, bo2, bias_k2, bias_v2)
            h = _layer_norm(x, ln_mlp_scale, ln_mlp_offset)
            h = jax.nn.gelu(h @ w_fc1 + b_fc1, approximate=False) @ w_fc2 + b_fc2
            return x + h
        return _forward(x, xf_1, xf_2, ln1_scale, ln1_offset, wq1, bq1, wk1, bk1, wv1, bv1, wo1, bo1, bias_k1, bias_v1, ln2_scale, ln2_offset, wq2, bq2, wk2, bk2, wv2, bv2, wo2, bo2, bias_k2, bias_v2, ln_mlp_scale, ln_mlp_offset, w_fc1, b_fc1, w_fc2, b_fc2)
    x = _L0_xattn_ref(x, ctx_2048, L0_xattn_w_q, L0_xattn_w_k, L0_xattn_w_v, L0_xattn_w_o, L0_xattn_alpha)
    x = _L1_xattn_ref(x, ctx_2048, 0, L1_xattn_ln1_w, L1_xattn_ln1_b, L1_xattn_ln2_w, L1_xattn_ln2_b, L1_xattn_maa_x, L1_xattn_maa_w, L1_xattn_maa_k, L1_xattn_maa_v, L1_xattn_maa_r, L1_xattn_maa_g, L1_xattn_maa_w1, L1_xattn_maa_w2, L1_xattn_time_decay, L1_xattn_decay_w1, L1_xattn_decay_w2, L1_xattn_faaaa, L1_xattn_Wr, L1_xattn_Wk, L1_xattn_Wv, L1_xattn_Wg, L1_xattn_Wo, L1_xattn_gn_w, L1_xattn_gn_b, L1_xattn_fmaa_k, L1_xattn_fmaa_r, L1_xattn_fWk, L1_xattn_fWr, L1_xattn_fWv)
    x = _L2_xattn_ref(x, ctx_2048, L2_xattn_ln1_w, L2_xattn_ln1_b, L2_xattn_ln2_w, L2_xattn_ln2_b, L2_xattn_maa_x, L2_xattn_maa_w1, L2_xattn_maa_w2, L2_xattn_maa_stack, L2_xattn_time_decay, L2_xattn_td_w1, L2_xattn_td_w2, L2_xattn_u, L2_xattn_Wr, L2_xattn_Wk, L2_xattn_Wv, L2_xattn_Wg, L2_xattn_Wo, L2_xattn_gn_w, L2_xattn_gn_b, L2_xattn_ffn_maa_k, L2_xattn_ffn_maa_r, L2_xattn_Wfk, L2_xattn_Wfr, L2_xattn_Wfv)
    x = _L3_xattn_ref(x, ctx_2048, ctx_2048, L3_xattn_ln1_scale, L3_xattn_ln1_offset, L3_xattn_wq1, L3_xattn_bq1, L3_xattn_wk1, L3_xattn_bk1, L3_xattn_wv1, L3_xattn_bv1, L3_xattn_wo1, L3_xattn_bo1, L3_xattn_bias_k1, L3_xattn_bias_v1, L3_xattn_ln2_scale, L3_xattn_ln2_offset, L3_xattn_wq2, L3_xattn_bq2, L3_xattn_wk2, L3_xattn_bk2, L3_xattn_wv2, L3_xattn_bv2, L3_xattn_wo2, L3_xattn_bo2, L3_xattn_bias_k2, L3_xattn_bias_v2, L3_xattn_ln_mlp_scale, L3_xattn_ln_mlp_offset, L3_xattn_w_fc1, L3_xattn_b_fc1, L3_xattn_w_fc2, L3_xattn_b_fc2)
    return x

_drawn_inputs = setup_inputs


def setup_inputs(seed=0):
    import zlib

    import numpy as np

    out = dict(_drawn_inputs(seed))
    spreads = {'L1_xattn_ln1_w': (1.0, 0.2),
     'L1_xattn_ln1_b': (0.0, 0.287),
     'L1_xattn_ln2_w': (1.0, 0.6),
     'L1_xattn_ln2_b': (0.0, 0.8),
     'L1_xattn_gn_w': (1.0, 0.6),
     'L1_xattn_gn_b': (0.0, 0.8),
     'L2_xattn_ln1_w': (1.0, 0.2),
     'L2_xattn_ln1_b': (0.0, 0.303),
     'L2_xattn_ln2_w': (1.0, 0.6),
     'L2_xattn_ln2_b': (0.0, 0.8),
     'L2_xattn_gn_w': (1.0, 0.6),
     'L2_xattn_gn_b': (0.0, 0.714),
     'L3_xattn_ln1_scale': (1.0, 0.6),
     'L3_xattn_ln1_offset': (0.0, 0.8),
     'L3_xattn_bq1': (0.0, 0.8),
     'L3_xattn_bk1': (0.0, 2.0),
     'L3_xattn_bv1': (0.0, 0.1),
     'L3_xattn_bo1': (0.0, 0.1),
     'L3_xattn_ln2_scale': (1.0, 0.6),
     'L3_xattn_ln2_offset': (0.0, 0.8),
     'L3_xattn_bq2': (0.0, 0.8),
     'L3_xattn_bk2': (0.0, 2.0),
     'L3_xattn_bv2': (0.0, 0.1),
     'L3_xattn_bo2': (0.0, 0.1),
     'L3_xattn_ln_mlp_scale': (1.0, 0.2),
     'L3_xattn_ln_mlp_offset': (0.0, 0.375),
     'L3_xattn_b_fc1': (0.0, 0.1),
     'L3_xattn_b_fc2': (0.0, 0.1)}
    factors = {'L0_xattn_w_q': 2.789,
     'L0_xattn_w_k': 2.865,
     'L1_xattn_maa_x': 6.703,
     'L1_xattn_maa_w': 8.0,
     'L1_xattn_maa_w1': 3.5,
     'L1_xattn_maa_w2': 3.577,
     'L1_xattn_decay_w1': 8.0,
     'L1_xattn_decay_w2': 8.0,
     'L1_xattn_faaaa': 3.754,
     'L1_xattn_fmaa_k': 2.678,
     'L1_xattn_fmaa_r': 8.0,
     'L1_xattn_fWr': 7.677,
     'L2_xattn_maa_x': 8.0,
     'L2_xattn_maa_w1': 3.033,
     'L2_xattn_maa_w2': 3.091,
     'L2_xattn_td_w1': 8.0,
     'L2_xattn_td_w2': 8.0,
     'L2_xattn_u': 3.18,
     'L2_xattn_ffn_maa_k': 5.691,
     'L2_xattn_ffn_maa_r': 8.0,
     'L2_xattn_Wfr': 4.11,
     'L3_xattn_wq1': 3.901,
     'L3_xattn_wk1': 3.802,
     'L3_xattn_bias_k1': 64.0,
     'L3_xattn_bias_v1': 64.0,
     'L3_xattn_wq2': 3.918,
     'L3_xattn_wk2': 3.835,
     'L3_xattn_bias_k2': 64.0,
     'L3_xattn_bias_v2': 64.0}
    for name, (base, spread) in spreads.items():
        noise = np.random.default_rng([zlib.crc32(name.encode()), seed]).standard_normal(out[name].shape)
        drawn = base * np.exp(spread * noise) if base else spread * noise
        out[name] = jnp.asarray(drawn.astype(out[name].dtype))
    for name, factor in factors.items():
        out[name] = (out[name] * factor).astype(out[name].dtype)
    return out
```

```python
from contextlib import ExitStack

import numpy as np
import concourse.bass as bass
from concourse import mybir

F32 = mybir.dt.float32
F32R = mybir.dt.float32r
ACT = mybir.ActivationFunctionType
ALU = mybir.AluOpType
AXX = mybir.AxisListType.X

P = 128
B, L, D = 8, 112, 512
S = 375
SP = S + 1
CT = D // P
NH = 2
HB = B // NH
HN = HB * L
T = CT * HN
NS, HS = 32, 16
GJ = 4
DM, DD = 32, 64
XH, XK = 16, 128
HG = 4
NG = XH // HG
F = 2048
CH = [(0, 128), (128, 128), (256, 120)]
UNIT = CT * D
EPS = 1e-5

U_L0 = {n: i for i, n in enumerate(["q", "k", "v", "o"])}
R_ORDER = ["k", "v", "r", "g", "o", "fr", "fk", "fv"]


def unit_r(layer, name):
    return 4 + 8 * layer + R_ORDER.index(name)


def unit_x(att, name, g):
    return 20 + 16 * att + 4 * g + ["q", "k", "v", "o"].index(name)


def unit_m(which, g):
    return 52 + 4 * which + g


N_UNITS = 60

R_VECS = ["ln1_w", "ln1_b", "ln2_w", "ln2_b", "maa_x", "maa_w", "maa_k", "maa_v", "maa_r", "maa_g",
          "decay", "u", "gn_w", "gn_b", "fmaa_k", "fmaa_r"]


def vector_columns():
    col, n = {}, 0
    for layer in (0, 1):
        for v in R_VECS:
            col[f"R{layer}_{v}"] = n
            n += CT
    for att in (0, 1):
        for v, w in (("ln_w", CT), ("ln_b", CT), ("bq", XH), ("bk", XH), ("bv", XH), ("bias_k", XH), ("bo", CT)):
            col[f"X{att}_{v}"] = n
            n += w
    for v, w in (("ln_w", CT), ("ln_b", CT), ("b1", F // P), ("b2", CT), ("alpha", 1), ("eps", 1)):
        col[f"M_{v}"] = n
        n += w
    return col, n


COL, NCOL = vector_columns()


class Queue:

    def __init__(self, sem):
        self.sem, self.count, self.todo, self.waited = sem, 0, [], {}

    def wait(self, *marks):
        for m in marks:
            if m is None:
                continue
            if isinstance(m, list):
                self.wait(*m)
                continue
            sem, value = m
            if self.waited.get(id(sem), 0) < value:
                self.waited[id(sem)] = value
                self.todo.append(lambda e, s=sem, v=value: e.wait_ge(s, v))

    def run(self, instruction, *after):
        self.wait(*after)
        self.todo.append(instruction)

    def step(self, instruction, *after):
        self.wait(*after)
        self.count += 1
        self.todo.append(lambda e, f=instruction: f(e).then_inc(self.sem, 1))
        return (self.sem, self.count)

    def now(self):
        return (self.sem, self.count) if self.count else None

    def play(self, engine):
        for f in self.todo:
            f(engine)


class Loads:

    def __init__(self, sem):
        self.sem, self.count = sem, 0

    def load(self, queue, dst, src, *after):
        queue.wait(*after)
        self.count += 16
        queue.todo.append(lambda e: e.dma_start(dst, src).then_inc(self.sem, 16))
        return (self.sem, self.count)


def build(nc, xT, ctxT, ctx_tok, s0, shift, weights, mix1, mix2, dec1, dec2, cols, rows, consts, out):
    with ExitStack() as ctx:
        def sb(stack, name, shape, dt=F32):
            return stack.enter_context(nc.sbuf_tensor(name, shape, dt))

        def sem(name):
            return ctx.enter_context(nc.semaphore(name))

        PE, DVE, SC, GP, SY = (Queue(sem(n)) for n in ("pe_done", "dve_done", "act_done", "pool_done", "sp_done"))

        x = sb(ctx, "x", [P, CT, NH, HN])
        vec = sb(ctx, "vec", [P, NCOL])
        ident = sb(ctx, "ident", [P, P])
        ones = sb(ctx, "ones", [P, P])
        raw = sb(ctx, "raw", [P, UNIT])
        NW = 3
        w_hi = [sb(ctx, f"w_hi{i}", [P, CT, D], F32R) for i in range(NW)]
        w_lo = [sb(ctx, f"w_lo{i}", [P, CT, D], F32R) for i in range(NW)]
        std = sb(ctx, "std", [P, HN])
        ps = ctx.enter_context(nc.psum_tensor("ps", [P, 8, 512], F32))

        bank_free = [None] * 8

        order = []

        def enter(unit, slot):
            order.append((unit, slot))
            return slot

        for unit in ([U_L0[n] for n in ("q", "k", "v", "o")] * NH
                     + [unit_r(layer, n) for layer in (0, 1) for _ in range(NH) for n in R_ORDER]):
            enter(unit, len(order) % NW)
        sq_, sv, sk = (len(order) % NW, (len(order) + 1) % NW, (len(order) + 2) % NW)
        for hf in range(NH):
            for att in (0, 1):
                enter(unit_x(att, "q", 0), sq_), enter(unit_x(att, "v", 0), sv), enter(unit_x(att, "k", 0), sk)
                for g in range(NG):
                    if g + 1 < NG:
                        enter(unit_x(att, "v", g + 1), sq_)
                        enter(unit_x(att, "o", g), sv)
                        enter(unit_x(att, "q", g + 1), sk)
                        enter(unit_x(att, "k", g + 1), sv)
                        sq_, sv, sk = sk, sq_, sv
                    else:
                        enter(unit_x(att, "o", g), sv)
                        sv, sk = sk, sv
            spare = [sq_, sv, sk]
            for i in range(2 * NG):
                enter(unit_m(i % 2, i // 2), spare[i % NW])
            n = 2 * NG
            sq_, sv, sk = spare[n % NW], spare[(n + 1) % NW], spare[(n + 2) % NW]
        raw_dma = Loads(sem("raw_loaded"))
        raw_mark, raw_free = [None], [None]
        ready_of = [None] * len(order)
        slot_free = [None] * NW
        slot_busy = [False] * NW
        fetched, used = [0], [0]

        def load_raw(n):
            if n < len(order):
                raw_mark[0] = raw_dma.load(SY, raw[:, :], weights[order[n][0], :, :], raw_free[0])

        def fetch():
            while fetched[0] < len(order) and not slot_busy[order[fetched[0]][1]]:
                n = fetched[0]
                i = order[n][1]
                fetched[0] += 1
                slot_busy[i] = True
                flat_hi = w_hi[i][:, :, :].rearrange("p a b -> p (a b)")
                flat_lo = w_lo[i][:, :, :].rearrange("p a b -> p (a b)")
                hi = SC.step(lambda e, d=flat_hi: e.activation(d, raw[:, :], ACT.Copy), raw_mark[0], slot_free[i])
                lo = GP.step(lambda e, d=flat_lo, h=flat_hi: e.tensor_tensor(d, raw[:, :], h.bitcast(F32), ALU.subtract),
                             raw_mark[0], hi, slot_free[i])
                ready_of[n] = [hi, lo]
                raw_free[0] = [hi, lo]
                load_raw(n + 1)

        def use(unit):
            fetch()
            n = used[0]
            used[0] += 1
            assert order[n][0] == unit and n < fetched[0], (n, unit, order[n])
            return n

        def done(n, mark):
            i = order[n][1]
            slot_free[i], slot_busy[i] = mark, False
            fetch()

        def products(dst, terms, *after):
            PE.wait(*after)
            for i, (lhsT, rhs) in enumerate(terms[:-1]):
                PE.run(lambda e, a=lhsT, b=rhs, s=(i == 0): e.matmul(dst, a, b, start=s, stop=False))
            a, b = terms[-1]
            return PE.step(lambda e: e.matmul(dst, a, b, start=(len(terms) == 1), stop=True))

        def three(a, b):
            return [(a[0], b[0]), (a[0], b[1]), (a[1], b[0])]

        def linear(n, pair, ready, evacuate, banks):
            i = order[n][1]
            mark = None
            for co in range(CT):
                bank = banks[co % len(banks)]
                terms = []
                for ct in range(CT):
                    w = (w_hi[i][:, ct, co * P:(co + 1) * P], w_lo[i][:, ct, co * P:(co + 1) * P])
                    m = (pair[0][:, ct, :], pair[1][:, ct, :])
                    terms += three(w, m)
                mark = products(ps[:, bank, 0:HN], terms, ready_of[n], ready, bank_free[bank])
                bank_free[bank] = evacuate(co, ps[:, bank, 0:HN], mark)
            done(n, mark)
            return mark

        def split(pair, src, ready, free):
            hi = SC.step(lambda e: e.activation(pair[0][:, :, :], src, ACT.Copy), ready, free)
            lo = GP.step(lambda e: e.tensor_tensor(pair[1][:, :, :], src, pair[0][:, :, :].bitcast(F32), ALU.subtract),
                         hi, ready, free)
            return [hi, lo]

        def col(name, i=0):
            c = COL[name] + i
            return vec[:, c:c + 1]

        def over_tiles(ap2):
            return ap2.unsqueeze(1).broadcast_to([P, CT, HN])

        def layer_norm(src, cen, sq, ready, free, b0, b1):
            m = products(ps[:, b0, 0:HN], [(ones[:, :], src[:, ct, :]) for ct in range(CT)], ready, bank_free[b0])
            c = DVE.step(lambda e: e.tensor_tensor(cen, src, over_tiles(ps[:, b0, 0:HN]), ALU.subtract), m, ready, free)
            bank_free[b0] = c
            v = [None] * CT
            for ct in range(CT):
                s = SC.step(lambda e, ct=ct: e.activation(sq[ct % len(sq)], cen[:, ct, :], ACT.Square), c, free,
                            v[ct - len(sq)] if ct >= len(sq) else None)
                PE.wait(s, bank_free[b1])
                v[ct] = PE.step(lambda e, ct=ct: e.matmul(ps[:, b1, 0:HN], ones[:, :], sq[ct % len(sq)],
                                                          start=(ct == 0), stop=(ct == CT - 1)))
            r = SC.step(lambda e: e.activation(std[:, :], ps[:, b1, 0:HN], ACT.Sqrt, bias=col("M_eps")), v[-1], DVE.now())
            bank_free[b1] = r
            r = DVE.step(lambda e: e.reciprocal(std[:, :], std[:, :]), r)
            return DVE.step(lambda e: e.tensor_tensor(cen, cen, over_tiles(std[:, :]), ALU.mult), r)

        def barrier():
            marks = [q.now() for q in (PE, DVE, SC, GP)]
            for q in (PE, DVE, SC, GP, SY):
                q.wait(*marks)

        start = Loads(sem("start_loaded"))
        load_raw(0)
        first = start.load(SY, x[:, :, :, :], xT)
        first = start.load(SY, vec[:, :], cols)
        first = start.load(SY, ident[:, :], consts[:, 0:P])
        first = start.load(SY, ones[:, :], consts[:, P:2 * P])
        for q in (PE, DVE, SC, GP):
            q.wait(first)
        x_ready = [None] * NH

        with ExitStack() as early:
            def act(name, dt=F32):
                return sb(early, name, [P, CT, HN], dt)

            xa = sb(early, "xa", [P, CT, HB, L + 1])
            sx = act("sx")
            tmp_a, tmp_b = act("tmp_a"), act("tmp_b")
            pairs = [(act("p0_hi", F32R), act("p0_lo", F32R)), (act("p1_hi", F32R), act("p1_lo", F32R))]
            r_, k_, v_, w_ = act("r"), act("k"), act("v"), act("w")
            ring = [sb(early, f"ring{i}", [P, GJ, HN]) for i in range(3)]
            block16 = sb(early, "block16", [P, P])
            mean16 = sb(early, "mean16", [P, P])
            collect = sb(early, "collect", [P, P + HS - 1])
            pick = sb(early, "pick", [P, HS, P], F32R)
            mix1_w = sb(early, "mix1_w", [P, CT, 5 * DM])
            mix2_a = sb(early, "mix2_a", [P, D])
            mix2_b = sb(early, "mix2_b", [DM, D])
            dec1_w = sb(early, "dec1_w", [P, CT, DD])
            dec2_w = sb(early, "dec2_w", [DD, D])
            s0_t = sb(early, "s0_t", [P, CT, HS, B])
            shift_t = sb(early, "shift_t", [P, CT, 2, B])
            soft = sb(early, "soft", [P, 4])

            early_dma = Loads(sem("early_loaded"))
            c_ready = early_dma.load(SY, block16[:, :], consts[:, 2 * P:3 * P])
            c_ready = early_dma.load(SY, mean16[:, :], consts[:, 3 * P:4 * P])
            c_ready = early_dma.load(SY, collect[:, :], consts[:, 4 * P:5 * P + HS - 1])
            c_ready = early_dma.load(SY, xa[:, :, :, :].rearrange("p a b c -> p (a b c)")[:, 0:P * HS // 2], consts[:, 5 * P + HS - 1:13 * P + HS - 1])
            c_ready = early_dma.load(SY, tmp_a[:, :, :].rearrange("p a b -> p (a b)")[:, 0:P * HS // 2], consts[:, 13 * P + HS - 1:21 * P + HS - 1])
            c_ready = early_dma.load(SY, s0_t[:, :, :, :], s0)
            c_ready = early_dma.load(SY, shift_t[:, :, :, :], shift)
            for i, raw_part in enumerate((xa[:, :, :, :].rearrange("p a b c -> p (a b c)"), tmp_a[:, :, :].rearrange("p a b -> p (a b)"))):
                pick_ready = SC.step(lambda e, i=i, r=raw_part: e.activation(
                    pick[:, i * HS // 2:(i + 1) * HS // 2, :].rearrange("p a b -> p (a b)"), r[:, 0:P * HS // 2], ACT.Copy), c_ready)

            ctx_dma = [Loads(sem("ctx_loaded0")), Loads(sem("ctx_loaded1"))]
            ctx_buf = [(ring[0], ring[1]), (ring[2], k_)]
            ctx_free = [None, None]
            prob = v_[:, 0, :]
            probT = v_[:, 1:4, :]
            p_free = [None]
            def cross_attention_0(hf):
                xh = x[:, :, hf, :]
                ctx_views, ctx_mark = [], []

                def load_ctx(b):
                    i = b % 2
                    keyT = ctx_buf[i][0][:, :, :].rearrange("p a b -> p (a b)")[:, 0:CT * SP].rearrange(
                        "p (a b) -> p a b", a=CT)
                    tok = ctx_buf[i][1][:, :, :].rearrange("p a b -> p (a b)")[:, 0:3 * D].rearrange(
                        "p (a b) -> p a b", a=3)
                    ctx_dma[i].load(SY, keyT, ctxT[b], ctx_free[i])
                    ctx_mark.append(ctx_dma[i].load(SY, tok, ctx_tok[b]))
                    ctx_views.append((keyT, tok))

                load_ctx(hf * HB)
                load_ctx(hf * HB + 1)
                ready = split(pairs[0], xh, x_ready[hf], PE.now())

                def q_out(co, src, mark):
                    hi = SC.step(lambda e: e.activation(pairs[1][0][:, co, :], src, ACT.Copy), mark)
                    lo = DVE.step(lambda e: e.tensor_tensor(pairs[1][1][:, co, :], src,
                                                            pairs[1][0][:, co, :].bitcast(F32), ALU.subtract), hi)
                    q_marks.extend([hi, lo])
                    return [hi, lo]

                q_marks = []
                linear(use(U_L0["q"]), pairs[0], ready, q_out, [0, 1, 2, 3])
                g_marks = []

                def g_out(co, src, mark):
                    g_marks.append(SC.step(lambda e: e.activation(tmp_a[:, co, :], src, ACT.Copy), mark, PE.now()))
                    return g_marks[-1]

                linear(use(U_L0["k"]), pairs[1], q_marks, g_out, [4, 5, 6, 7])
                c_marks = []
                for bb in range(HB):
                    b = hf * HB + bb
                    keyT, tok = ctx_views[bb]
                    cols_b = slice(bb * L, (bb + 1) * L)
                    sc = ps[0:L, 0, 0:SP]
                    m = products(sc, [(tmp_a[:, ct, cols_b], keyT[:, ct, :]) for ct in range(CT)],
                                 g_marks, ctx_mark[bb], bank_free[0])
                    m = DVE.step(lambda e, sc=sc: e.tensor_reduce(soft[0:L, 0:1], sc[:, 0:S], AXX, ALU.max), m, p_free[0])
                    m = DVE.step(lambda e: e.tensor_scalar(soft[0:L, 1:2], soft[0:L, 0:1], -float(D) ** -0.5, None, ALU.mult), m)
                    m = SC.step(lambda e, sc=sc: e.activation(prob[0:L, 0:S], sc[:, 0:S], ACT.Exp, bias=soft[0:L, 1:2],
                                                       scale=float(D) ** -0.5, accum_out=soft[0:L, 2:3]), m, p_free[0])
                    bank_free[0] = m
                    m = DVE.step(lambda e: e.reciprocal(soft[0:L, 3:4], soft[0:L, 2:3]), m)
                    m = DVE.step(lambda e: e.tensor_scalar(prob[0:L, 0:S], prob[0:L, 0:S], soft[0:L, 3:4], None, ALU.mult), m)
                    PE.wait(m, bank_free[1])
                    for c, (t0, n) in enumerate(CH):
                        n = min(n, S - t0)
                        m = PE.step(lambda e, c=c, t0=t0, n=n: e.transpose(
                            ps[0:n, 1, c * L:(c + 1) * L], prob[0:L, t0:t0 + n], ident[0:L, 0:L]))
                    a = SC.step(lambda e: e.activation(probT[:, 0:2, 0:L], ps[:, 1, 0:2 * L].rearrange("p (c q) -> p c q", c=2), ACT.Copy), m)
                    a = SC.step(lambda e: e.activation(probT[0:119, 2, 0:L], ps[0:119, 1, 2 * L:3 * L], ACT.Copy), m)
                    bank_free[1] = a
                    PE.wait(a, bank_free[2])
                    for dt in range(CT):
                        m = products(ps[:, 2, dt * L:(dt + 1) * L],
                                     [(tok[0:min(n, S - t0), c, dt * P:(dt + 1) * P], probT[0:min(n, S - t0), c, 0:L])
                                      for c, (t0, n) in enumerate(CH)])
                    ctx_free[b % 2] = m
                    p_free[0] = m
                    m = DVE.step(lambda e, cols_b=cols_b: e.tensor_copy(tmp_b[:, :, cols_b],
                                                         ps[:, 2, 0:CT * L].rearrange("p (c q) -> p c q", c=CT)), m)
                    bank_free[2] = m
                    c_marks.append(m)
                    if bb + 2 < HB:
                        load_ctx(b + 2)
                ready = split(pairs[0], tmp_b[:, :, :], c_marks, PE.now())
                q_marks = []
                linear(use(U_L0["v"]), pairs[0], ready, q_out, [3, 4, 5, 6])
                x_marks = []

                def o_out(co, src, mark):
                    x_marks.append(DVE.step(lambda e: e.scalar_tensor_tensor(
                        xh[:, co, :], src, col("M_alpha"), xh[:, co, :], ALU.mult, ALU.add), mark))
                    return x_marks[-1]

                linear(use(U_L0["o"]), pairs[1], q_marks, o_out, [0, 1, 2, 7])
                x_ready[hf] = x_marks

            for hf in range(NH):
                cross_attention_0(hf)

            barrier()
            PE.wait(c_ready)
            DVE.wait(c_ready)
            GP.wait(c_ready)
            w4 = w_[:, :, :].rearrange("p c (b t) -> p c b t", b=HB)
            w_zero = DVE.step(lambda e: e.memset(w4[:, :, :, 0:1], 0.0))
            small_dma = Loads(sem("small_loaded"))
            xa_now = xa[:, :, :, 1:L + 1]
            xa_prev = xa[:, :, :, 0:L]
            by_seq = lambda ap: ap.rearrange("p c (b t) -> p c b t", b=HB)

            def normalise_and_shift(layer, hf, name, which, ready):
                prior = [PE.now(), DVE.now(), GP.now(), SC.now()]
                c = layer_norm(x[:, :, hf, :], tmp_a[:, :, :], [tmp_b[:, ct, :] for ct in range(CT)], ready, prior, 0, 1)
                st = GP.step(lambda e: e.tensor_copy(xa[:, :, :, 0], shift_t[:, :, which, hf * HB:(hf + 1) * HB]), prior)
                for ct in range(CT):
                    a = SC.step(lambda e, ct=ct: e.activation(
                        xa_now[:, ct, :, :], tmp_a[:, ct, :].rearrange("p (b t) -> p b t", b=HB), ACT.Identity,
                        bias=col(f"R{layer}_{name}_b", ct), scale=col(f"R{layer}_{name}_w", ct)), c, prior)
                for ct in range(CT):
                    s = DVE.step(lambda e, ct=ct: e.tensor_tensor(
                        sx[:, ct, :].rearrange("p (b t) -> p b t", b=HB), xa_prev[:, ct, :, :], xa_now[:, ct, :, :],
                        ALU.subtract), a, st)
                return [s, a, st]

            def recurrent_half(layer, hf, small):
                def V(v, ct):
                    return col(f"R{layer}_{v}", ct)

                xh = x[:, :, hf, :]
                xs = normalise_and_shift(layer, hf, "ln1", 1, x_ready[hf])
                for ct in range(CT):
                    m = DVE.step(lambda e, ct=ct: e.scalar_tensor_tensor(
                        tmp_b[:, ct, :].rearrange("p (b t) -> p b t", b=HB),
                        sx[:, ct, :].rearrange("p (b t) -> p b t", b=HB), V("maa_x", ct), xa_now[:, ct, :, :],
                        ALU.mult, ALU.add), xs)
                h1 = products(ps[:, 0, 0:HN], [(mix1_w[:, ct, 0:P], tmp_b[:, ct, :]) for ct in range(CT)],
                              m, small, bank_free[0])
                h1 = SC.step(lambda e: e.activation(tmp_a[:, 0, :], ps[:, 0, 0:HN], ACT.Tanh), h1)
                bank_free[0] = h1
                h2 = products(ps[0:DM, 1, 0:HN], [(mix1_w[:, ct, P:P + DM], tmp_b[:, ct, :]) for ct in range(CT)],
                              bank_free[1])
                h2 = SC.step(lambda e: e.activation(tmp_a[0:DM, 1, :], ps[0:DM, 1, 0:HN], ACT.Tanh), h2)
                bank_free[1] = h2
                hidden_ready = [h1, h2]
                names = ["w", "k", "v", "r", "g"] if layer == 0 else ["k", "w", "v", "r", "g"]
                tmpb_free = h2

                def mix(f, name, after):
                    marks = []
                    for ct in range(CT):
                        bank = ct
                        lhsT, rhs = ((mix2_a[f * DM:(f + 1) * DM, ct * P:(ct + 1) * P], tmp_a[f * DM:(f + 1) * DM, 0, :])
                                     if f < 4 else (mix2_b[:, ct * P:(ct + 1) * P], tmp_a[0:DM, 1, :]))
                        m = products(ps[:, bank, 0:HN], [(lhsT, rhs)], hidden_ready, bank_free[bank])
                        m = DVE.step(lambda e, ct=ct, bank=bank: e.scalar_tensor_tensor(
                            tmp_b[:, ct, :], ps[:, bank, 0:HN], V("maa_" + name, ct), sx[:, ct, :],
                            ALU.add, ALU.mult), m, after)
                        bank_free[bank] = m
                        marks.append(GP.step(lambda e, ct=ct: e.tensor_tensor(
                            tmp_b[:, ct, :].rearrange("p (b t) -> p b t", b=HB),
                            tmp_b[:, ct, :].rearrange("p (b t) -> p b t", b=HB), xa_now[:, ct, :, :], ALU.add), m))
                    return marks

                mixed = mix(names.index("w"), "w", [tmpb_free, PE.now()])
                m = products(ps[0:DD, 4, 0:HN], [(dec1_w[:, ct, :], tmp_b[:, ct, :]) for ct in range(CT)],
                             mixed, bank_free[4])
                tmpb_free = m
                m = SC.step(lambda e: e.activation(tmp_a[0:DD, 2, :], ps[0:DD, 4, 0:HN], ACT.Tanh), m)
                bank_free[4] = m
                w_marks = []
                for ct in range(CT):
                    bank = 4 + ct
                    q = products(ps[:, bank, 0:HN], [(dec2_w[:, ct * P:(ct + 1) * P], tmp_a[0:DD, 2, :])],
                                 m, bank_free[bank])
                    q = SC.step(lambda e, ct=ct, bank=bank: e.activation(
                        tmp_a[:, 3, :], ps[:, bank, 0:HN], ACT.Exp, bias=V("decay", ct)), q, w_marks)
                    bank_free[bank] = q
                    w_marks.append(SC.step(lambda e, ct=ct: e.activation(
                        w4[:, ct, :, 1:L], tmp_a[:, 3, :].rearrange("p (b t) -> p b t", b=HB)[:, :, 0:L - 1],
                        ACT.Exp, scale=-1.0), q, w_zero))

                dest = {"k": k_, "v": v_, "r": r_, "g": sx}
                got = {}
                for i, name in enumerate(("k", "v", "r", "g")):
                    mixed = mix(names.index(name), name, tmpb_free)
                    pair = pairs[i % 2]
                    ready = split(pair, tmp_b[:, :, :], mixed, PE.now())
                    tmpb_free = ready
                    marks = got[name] = []

                    def out_of(co, src, mark, name=name, marks=marks, mixed=mixed):
                        func = ACT.Silu if name == "g" else ACT.Copy
                        marks.append(SC.step(lambda e: e.activation(dest[name][:, co, :], src, func), mark, mixed))
                        return marks[-1]

                    linear(use(unit_r(layer, name)), pair, ready, out_of, [4, 5, 6, 7])
                v_pair = pairs[0]
                v_split = split(v_pair, v_[:, :, :], got["v"], PE.now())

                last = None
                y_marks = []
                ring_free = [PE.now()] * 3
                turn = 0
                for ct in range(CT):
                    m = DVE.step(lambda e, ct=ct: e.scalar_tensor_tensor(
                        tmp_b[:, ct, :], r_[:, ct, :], V("u", ct), k_[:, ct, :], ALU.mult, ALU.mult),
                        got["r"], got["k"], v_split, tmpb_free)
                    m = products(ps[:, 7, 0:HN], [(block16[:, :], tmp_b[:, ct, :])], m, bank_free[7])
                    own = DVE.step(lambda e, ct=ct: e.tensor_tensor(
                        tmp_b[:, ct, :], ps[:, 7, 0:HN], v_[:, ct, :], ALU.mult), m)
                    bank_free[7] = own
                    for jg in range(HS // GJ):
                        buf = ring[turn % 3]
                        free = ring_free[turn % 3]
                        buf4 = buf[:, :, :].rearrange("p j (b t) -> p j b t", b=HB)
                        st = GP.step(lambda e, ct=ct, jg=jg, hf=hf, buf4=buf4: e.tensor_copy(
                            buf4[:, :, :, 0], s0_t[:, ct, jg * GJ:(jg + 1) * GJ, hf * HB:(hf + 1) * HB]), free)
                        a_marks = []
                        for jp in range(GJ // 2):
                            b0 = 2 * ((turn * 2 + jp) % 3)
                            for q in range(2):
                                j = jg * GJ + jp * 2 + q
                                sel = pick[:, j, :]
                                m = products(ps[:, b0 + q, 0:HN],
                                             [(sel, v_pair[0][:, ct, :]), (sel, v_pair[1][:, ct, :])],
                                             v_split, pick_ready, bank_free[b0 + q])
                            m = DVE.step(lambda e, ct=ct, jp=jp, b0=b0, buf4=buf4: e.tensor_tensor(
                                buf4[:, 2 * jp:2 * jp + 2, :, 1:L],
                                ps[:, b0:b0 + 2, 0:HN].rearrange("p j (b t) -> p j b t", b=HB)[:, :, :, 0:L - 1],
                                k_[:, ct, :].rearrange("p (b t) -> p b t", b=HB)[:, :, 0:L - 1].unsqueeze(1)
                                .broadcast_to([P, 2, HB, L - 1]), ALU.mult), m, got["k"], free)
                            bank_free[b0] = bank_free[b0 + 1] = m
                            a_marks.append(m)
                        for jj in range(GJ):
                            m = DVE.step(lambda e, ct=ct, jj=jj, buf=buf: e.tensor_tensor_scan(
                                buf[:, jj, :], w_[:, ct, :], buf[:, jj, :], 0.0, ALU.mult, ALU.add),
                                a_marks, st, w_marks)
                        eng = GP if turn % 2 else DVE
                        m = eng.step(lambda e, ct=ct, buf=buf: e.tensor_tensor(
                            buf[:, :, :], buf[:, :, :], r_[:, ct, :].unsqueeze(1).broadcast_to([P, GJ, HN]),
                            ALU.mult), m, got["r"])
                        PE.wait(m, bank_free[6] if jg == 0 else None)
                        for jj in range(GJ):
                            j = jg * GJ + jj
                            PE.run(lambda e, j=j, jj=jj, buf=buf: e.matmul(
                                ps[:, 6, 0:HN], collect[:, HS - 1 - j:HS - 1 - j + P], buf[:, jj, :],
                                start=(j == 0), stop=(j == HS - 1))) if jj < GJ - 1 else None
                        last = PE.step(lambda e, j=j, buf=buf: e.matmul(
                            ps[:, 6, 0:HN], collect[:, HS - 1 - j:HS - 1 - j + P], buf[:, GJ - 1, :],
                            start=False, stop=(j == HS - 1)))
                        ring_free[turn % 3] = last
                        turn += 1
                    m = DVE.step(lambda e, ct=ct: e.tensor_tensor(
                        tmp_b[:, ct, :], tmp_b[:, ct, :], ps[:, 6, 0:HN], ALU.add), last, own)
                    bank_free[6] = m
                    g = products(ps[:, 7, 0:HN], [(mean16[:, :], tmp_b[:, ct, :])], m, bank_free[7])
                    m = DVE.step(lambda e, ct=ct: e.tensor_tensor(
                        tmp_b[:, ct, :], tmp_b[:, ct, :], ps[:, 7, 0:HN], ALU.subtract), g)
                    bank_free[7] = m
                    g = SC.step(lambda e, ct=ct: e.activation(tmp_a[:, ct, :], tmp_b[:, ct, :], ACT.Square), m, w_marks)
                    g = products(ps[:, 7, 0:HN], [(mean16[:, :], tmp_a[:, ct, :])], g, bank_free[7])
                    g = SC.step(lambda e, ct=ct: e.activation(tmp_a[:, ct, :], ps[:, 7, 0:HN], ACT.Sqrt,
                                                              bias=col("M_eps")), g)
                    bank_free[7] = g
                    g = DVE.step(lambda e, ct=ct: e.reciprocal(tmp_a[:, ct, :], tmp_a[:, ct, :]), g)
                    g = DVE.step(lambda e, ct=ct: e.tensor_tensor(
                        tmp_b[:, ct, :], tmp_b[:, ct, :], tmp_a[:, ct, :], ALU.mult), g)
                    g = SC.step(lambda e, ct=ct: e.activation(tmp_b[:, ct, :], tmp_b[:, ct, :], ACT.Identity,
                                                              bias=V("gn_b", ct), scale=V("gn_w", ct)), g)
                    y_marks.append(DVE.step(lambda e, ct=ct: e.tensor_tensor(
                        tmp_b[:, ct, :], tmp_b[:, ct, :], sx[:, ct, :], ALU.mult), g, got["g"]))
                ready = split(pairs[1], tmp_b[:, :, :], y_marks, PE.now())
                x_marks = []

                def add_x(co, src, mark):
                    x_marks.append(DVE.step(lambda e: e.tensor_tensor(xh[:, co, :], xh[:, co, :], src, ALU.add), mark))
                    return x_marks[-1]

                linear(use(unit_r(layer, "o")), pairs[1], ready, add_x, [0, 1, 2, 3])

                xs = normalise_and_shift(layer, hf, "ln2", 0, x_marks)
                rr, kk_ = tmp_a, r_
                for i, (name, unit) in enumerate((("fmaa_r", "fr"), ("fmaa_k", "fk"))):
                    free = [PE.now(), SC.now(), GP.now()]
                    for ct in range(CT):
                        m = DVE.step(lambda e, ct=ct, name=name: e.scalar_tensor_tensor(
                            tmp_b[:, ct, :].rearrange("p (b t) -> p b t", b=HB),
                            sx[:, ct, :].rearrange("p (b t) -> p b t", b=HB), V(name, ct), xa_now[:, ct, :, :],
                            ALU.mult, ALU.add), xs, free)
                    ready = split(pairs[i], tmp_b[:, :, :], m, PE.now())
                    marks = []

                    def f_out(co, src, mark, unit=unit, marks=marks):
                        if unit == "fr":
                            marks.append(SC.step(lambda e: e.activation(rr[:, co, :], src, ACT.Sigmoid), mark, xs))
                            return marks[-1]
                        a = SC.step(lambda e: e.activation(kk_[:, co, :], src, ACT.Relu), mark)
                        marks.append(DVE.step(lambda e: e.tensor_tensor(
                            kk_[:, co, :], kk_[:, co, :], kk_[:, co, :], ALU.mult), a))
                        return a

                    linear(use(unit_r(layer, unit)), pairs[i], ready, f_out, [4 * i, 4 * i + 1, 4 * i + 2, 4 * i + 3])
                    if unit == "fr":
                        rr_marks = marks
                ready = split(pairs[0], kk_[:, :, :], marks, PE.now())
                x_marks = []

                def fv_out(co, src, mark):
                    m = DVE.step(lambda e: e.tensor_tensor(rr[:, co, :], rr[:, co, :], src, ALU.mult), mark, rr_marks)
                    x_marks.append(GP.step(lambda e: e.tensor_tensor(
                        xh[:, co, :], xh[:, co, :], rr[:, co, :], ALU.add), m))
                    return m

                linear(use(unit_r(layer, "fv")), pairs[0], ready, fv_out, [0, 1, 2, 3])
                x_ready[hf] = x_marks

            for layer in (0, 1):
                small_dma.load(SY, mix1_w[:, :, :], mix1[layer], PE.now())
                small_dma.load(SY, mix2_a[:, :], mix2[layer, 0:P, :])
                small_dma.load(SY, mix2_b[:, :], mix2[layer, P:P + DM, :])
                small_dma.load(SY, dec1_w[:, :, :], dec1[layer])
                small = small_dma.load(SY, dec2_w[:, :], dec2[layer])
                for hf in range(NH):
                    recurrent_half(layer, hf, small)

            barrier()

        with ExitStack() as late:
            ctx_pair = (sb(late, "ctx_hi", [P, HB, CT, SP], F32R), sb(late, "ctx_lo", [P, HB, CT, SP], F32R))
            h_pair = (sb(late, "h_hi", [P, CT, HN], F32R), sb(late, "h_lo", [P, CT, HN], F32R))
            q_pair = (sb(late, "q_hi", [P, HG, HN], F32R), sb(late, "q_lo", [P, HG, HN], F32R))
            k_pair = (sb(late, "k_hi", [P, HG, SP], F32R), sb(late, "k_lo", [P, HG, SP], F32R))
            v_pairs = [(sb(late, f"v_hi{i}", [P, 3, D], F32R), sb(late, f"v_lo{i}", [P, 3, D], F32R)) for i in range(2)]
            pt_pairs = [(sb(late, f"pt_hi{i}", [P, 3, L], F32R), sb(late, f"pt_lo{i}", [P, 3, L], F32R)) for i in range(2)]
            row_pair = sb(late, "row_pair", [1, 2, D], F32R)
            row_raw = sb(late, "row_raw", [P, 2, D])
            scratch = sb(late, "scratch", [P, T])
            soft = sb(late, "soft3", [P, 16])
            cen = scratch[:, :].rearrange("p (a b) -> p a b", a=CT)
            stage = scratch[:, 0:CT * SP].rearrange("p (a b) -> p a b", a=CT)
            probs = [scratch[0:L, i * SP:(i + 1) * SP] for i in range(3)]
            o_raw = scratch[:, 3 * SP:3 * SP + HG * L].rearrange("p (h q) -> p h q", h=HG)
            squares = [row_raw[:, i, 0:HN] for i in range(2)]
            row_dma, ctx_dma = Loads(sem("rows_loaded")), Loads(sem("late_ctx_loaded"))
            vrow_dma = [Loads(sem("vrow_moved0")), Loads(sem("vrow_moved1"))]
            out_dma = Loads(sem("stored"))
            SCALE = float(XK) ** -0.5
            BIAS_P = CH[2][1] - 1
            k_free = [None] * HG
            v_free = [None] * 2
            pt_free = [None] * 2
            p_free = [None] * 3
            turn = [0, 0]

            def minus(dst, src, hi):
                return lambda e: e.tensor_tensor(dst, src, hi.bitcast(F32), ALU.subtract)

            def load_context(hf):
                marks = []
                prior = [q.now() for q in (PE, DVE, GP, SC)]
                for bb in range(HB):
                    m = ctx_dma.load(SY, stage, ctxT[hf * HB + bb], prior if bb == 0 else marks)
                    hi = SC.step(lambda e, bb=bb: e.activation(ctx_pair[0][:, bb, :, :], stage, ACT.Copy), m, prior)
                    lo = DVE.step(minus(ctx_pair[1][:, bb, :, :], stage, ctx_pair[0][:, bb, :, :]), hi, m, prior)
                    marks += [hi, lo]
                return marks

            def norm_to_pair(hf, name, ready):
                prior = [q.now() for q in (PE, DVE, GP, SC)]
                c = layer_norm(x[:, :, hf, :], cen, squares, ready, prior, 0, 1)
                for ct in range(CT):
                    a = SC.step(lambda e, ct=ct: e.activation(cen[:, ct, :], cen[:, ct, :], ACT.Identity,
                                                              bias=col(name + "_ln_b", ct), scale=col(name + "_ln_w", ct)), c)
                hi = SC.step(lambda e: e.activation(h_pair[0][:, :, :], cen, ACT.Copy), a, prior)
                lo = DVE.step(minus(h_pair[1][:, :, :], cen, h_pair[0][:, :, :]), hi, prior)
                return [hi, lo]

            def attention(hf, att, ctx_ready, x_marks):
                xh = x[:, :, hf, :]
                A = f"X{att}_"
                h_ready = norm_to_pair(hf, f"X{att}", x_marks)
                q_marks, k_marks, v_marks = [], [None] * HG, [None] * 2
                col_marks, row_marks = [None], [None, None]
                o_marks = []
                x_last = x_marks
                v_block, k_block = [None], [None]
                later = []
                item = [0]

                def put(lag, what):
                    later.append((item[0] + lag, len(later), what))

                def next_item(what):
                    what()
                    item[0] += 1
                    flush(item[0])

                def flush(upto):
                    due = sorted(x for x in later if x[0] <= upto)
                    later[:] = [x for x in later if x[0] > upto]
                    for _, _, what in due:
                        what()

                def q_projection(g):
                    n = use(unit_x(att, "q", g))
                    q_marks.clear()
                    old = list(o_marks)
                    o_marks.clear()

                    def out_q(co, src, mark, g=g):
                        b = col(A + "bq", HG * g + co)
                        hi = SC.step(lambda e: e.activation(q_pair[0][:, co, :], src, ACT.Identity, bias=b), mark, old)
                        lo = DVE.step(lambda e: e.scalar_tensor_tensor(
                            q_pair[1][:, co, :], src, b, q_pair[0][:, co, :].bitcast(F32), ALU.add, ALU.subtract), hi)
                        q_marks.extend([hi, lo])
                        return [hi, lo]

                    linear(n, h_pair, h_ready, out_q, [0, 1, 2])

                def bias_slots(g):
                    kb = vec[:, COL[A + "bias_k"] + HG * g:COL[A + "bias_k"] + HG * (g + 1)]
                    hi = SC.step(lambda e: e.activation(k_pair[0][:, :, S], kb, ACT.Copy), k_free)
                    lo = DVE.step(minus(k_pair[1][:, :, S], kb, k_pair[0][:, :, S]), hi, k_free)
                    col_marks[0] = [hi, lo]

                def bias_rows(g):
                    m = row_dma.load(SY, row_raw[0:1, :, :], rows[att, g], DVE.now(), SC.now(), PE.now())
                    d = DVE.step(lambda e: e.tensor_tensor(row_raw[0:1, 0, :], row_raw[0:1, 0, :], row_raw[0:1, 1, :],
                                                           ALU.subtract), m)
                    hi = SC.step(lambda e: e.activation(row_pair[:, 0, :], row_raw[0:1, 0, :], ACT.Copy), d, row_marks)
                    lo = DVE.step(minus(row_pair[:, 1, :], row_raw[0:1, 0, :], row_pair[:, 0, :]), hi)
                    return [hi, lo]

                def move_row(i, ready):
                    for part in range(2):
                        row_marks[i] = vrow_dma[i].load(
                            SY, v_pairs[i][part][BIAS_P:BIAS_P + 1, 2, :].bitcast(F32), row_pair[:, part, :].bitcast(F32),
                            ready, v_free[i])

                def value_tile(bb, c, last):
                    i = bb % 2
                    t0, n = CH[c]
                    bank = turn[1] % 3
                    turn[1] += 1
                    blk = v_block[0]
                    s = order[blk][1]
                    terms = []
                    for ct in range(CT):
                        terms += three((ctx_pair[0][:, bb, ct, t0:t0 + n], ctx_pair[1][:, bb, ct, t0:t0 + n]),
                                       (w_hi[s][:, ct, :], w_lo[s][:, ct, :]))
                    m = products(ps[0:n, bank, :], terms, ready_of[blk], ctx_ready, bank_free[bank])
                    if last:
                        done(blk, m)
                    n = min(n, S - t0)
                    hi = SC.step(lambda e: e.activation(v_pairs[i][0][0:n, c, :], ps[0:n, bank, :], ACT.Copy), m, v_free[i])
                    lo = DVE.step(minus(v_pairs[i][1][0:n, c, :], ps[0:n, bank, :], v_pairs[i][0][0:n, c, :]), hi, v_free[i])
                    bank_free[bank] = [hi, lo]
                    v_marks[i] = [hi, lo]

                def key_tile(bb, h, g, last):
                    bank = turn[1] % 3
                    turn[1] += 1
                    blk = k_block[0]
                    s = order[blk][1]
                    terms = []
                    for ct in range(CT):
                        terms += three((w_hi[s][:, ct, h * XK:(h + 1) * XK], w_lo[s][:, ct, h * XK:(h + 1) * XK]),
                                       (ctx_pair[0][:, bb, ct, :], ctx_pair[1][:, bb, ct, :]))
                    m = products(ps[:, bank, 0:SP], terms, ready_of[blk], ctx_ready, bank_free[bank])
                    if last:
                        done(blk, m)
                    b = col(A + "bk", HG * g + h)
                    hi = SC.step(lambda e: e.activation(k_pair[0][:, h, 0:S], ps[:, bank, 0:S], ACT.Identity, bias=b),
                                 m, k_free[h])
                    lo = DVE.step(lambda e: e.scalar_tensor_tensor(
                        k_pair[1][:, h, 0:S], ps[:, bank, 0:S], b, k_pair[0][:, h, 0:S].bitcast(F32),
                        ALU.add, ALU.subtract), hi, k_free[h])
                    bank_free[bank] = [hi, lo]
                    k_marks[h] = [hi, lo]
                    put(1, lambda: scores(bb, h, g))

                def scores(bb, h, g):
                    t = turn[0]
                    turn[0] += 1
                    bank, pr, st = 3 + t % 2, probs[t % 3], soft[0:L, 4 * (t % 4):4 * (t % 4) + 4]
                    cols_b = slice(bb * L, (bb + 1) * L)
                    m = products(ps[0:L, bank, 0:SP],
                                 three((q_pair[0][:, h, cols_b], q_pair[1][:, h, cols_b]),
                                       (k_pair[0][:, h, :], k_pair[1][:, h, :])),
                                 q_marks, k_marks[h], col_marks[0], bank_free[bank])
                    k_free[h] = m
                    src = ps[0:L, bank, 0:SP]
                    m = DVE.step(lambda e: e.tensor_reduce(st[:, 0:1], src, AXX, ALU.max), m)
                    m = DVE.step(lambda e: e.tensor_scalar(st[:, 1:2], st[:, 0:1], -SCALE, None, ALU.mult), m)
                    m = SC.step(lambda e: e.activation(pr, src, ACT.Exp, bias=st[:, 1:2], scale=SCALE,
                                                       accum_out=st[:, 2:3]), m, p_free[t % 3])
                    bank_free[bank] = m
                    m = DVE.step(lambda e: e.reciprocal(st[:, 3:4], st[:, 2:3]), m)
                    m = DVE.step(lambda e: e.tensor_scalar(pr, pr, st[:, 3:4], None, ALU.mult), m)
                    put(1, lambda: turn_probs(bb, h, g, t, m))

                def turn_probs(bb, h, g, t, ready):
                    bank, pt = 5 + t % 2, pt_pairs[t % 2]
                    PE.wait(ready, bank_free[bank])
                    for c, (t0, n) in enumerate(CH):
                        m = PE.step(lambda e, c=c, t0=t0, n=n: e.transpose(
                            ps[0:n, bank, c * L:(c + 1) * L], probs[t % 3][:, t0:t0 + n], ident[0:L, 0:L]))
                    p_free[t % 3] = m
                    marks = []
                    parts = [(pt[0][0:n, c0:c1, :], pt[1][0:n, c0:c1, :],
                              ps[0:n, bank, c0 * L:c1 * L].rearrange("p (c q) -> p c q", q=L))
                             for c0, c1, n in ((0, 2, P), (2, 3, CH[2][1]))]
                    for hi, _, src in parts:
                        m = SC.step(lambda e, d=hi, s=src: e.activation(d, s, ACT.Copy), m, pt_free[t % 2])
                    marks = [m]
                    for hi, lo, src in parts:
                        marks.append(DVE.step(minus(lo, src, hi), m, pt_free[t % 2]))
                    bank_free[bank] = marks
                    put(1, lambda: weigh(bb, h, g, t, marks))

                def weigh(bb, h, g, t, ready):
                    pt, v = pt_pairs[t % 2], v_pairs[bb % 2]
                    terms = []
                    for c, (_, n) in enumerate(CH):
                        terms += three((v[0][0:n, c, h * XK:(h + 1) * XK], v[1][0:n, c, h * XK:(h + 1) * XK]),
                                       (pt[0][0:n, c, :], pt[1][0:n, c, :]))
                    m = products(ps[:, 7, h * L:(h + 1) * L], terms, ready, v_marks[bb % 2], row_marks[bb % 2],
                                 bank_free[7] if h == 0 else None)
                    pt_free[t % 2] = m
                    if h == HG - 1:
                        v_free[bb % 2] = m
                        bv = vec[:, COL[A + "bv"] + HG * g:COL[A + "bv"] + HG * (g + 1)].unsqueeze(2).broadcast_to([P, HG, L])
                        r = DVE.step(lambda e: e.tensor_tensor(
                            o_raw, ps[:, 7, 0:HG * L].rearrange("p (h q) -> p h q", h=HG), bv, ALU.add), m, GP.now())
                        bank_free[7] = r
                        dst = [q_pair[i][:, :, bb * L:(bb + 1) * L] for i in range(2)]
                        hi = SC.step(lambda e: e.activation(dst[0], o_raw, ACT.Copy), r)
                        lo = GP.step(minus(dst[1], o_raw, dst[0]), hi)
                        o_marks.extend([hi, lo])

                def out_projection(g):
                    marks = []

                    def add_x(co, src, mark):
                        if g == 0:
                            m = DVE.step(lambda e: e.scalar_tensor_tensor(
                                xh[:, co, :], src, col(A + "bo", co), xh[:, co, :], ALU.add, ALU.add), mark)
                        else:
                            m = DVE.step(lambda e: e.tensor_tensor(xh[:, co, :], xh[:, co, :], src, ALU.add), mark)
                        marks.append(m)
                        return m

                    m = linear(use(unit_x(att, "o", g)), q_pair, o_marks, add_x, [0, 1, 2])
                    o_marks[:] = [m]
                    return marks

                q_projection(0)
                for g in range(NG):
                    for bb in range(HB):
                        if bb == 0:
                            v_block[0] = use(unit_x(att, "v", g))
                            rows_ready = bias_rows(g)
                            move_row(0, rows_ready)
                        for c in range(3):
                            next_item(lambda: value_tile(bb, c, bb == HB - 1 and c == 2))
                        if bb == 0:
                            if g:
                                flush(item[0] + 9)
                                x_marks = out_projection(g - 1)
                                q_projection(g)
                            move_row(1, rows_ready)
                            bias_slots(g)
                            k_block[0] = use(unit_x(att, "k", g))
                        for h in range(HG):
                            next_item(lambda: key_tile(bb, h, g, bb == HB - 1 and h == HG - 1))
                for _ in range(4):
                    item[0] += 1
                    flush(item[0])
                return out_projection(NG - 1)

            def mlp_group(hf, g, h_ready, m):
                xh = x[:, :, hf, :]
                g_marks = []
                prior = [m, PE.now()]

                def out_g(co, src, mark):
                    a = SC.step(lambda e: e.activation(cen[:, co, :], src, ACT.Gelu, bias=col("M_b1", CT * g + co)),
                                mark, prior)
                    hi = SC.step(lambda e: e.activation(q_pair[0][:, co, :], cen[:, co, :], ACT.Copy), a, prior)
                    lo = DVE.step(minus(q_pair[1][:, co, :], cen[:, co, :], q_pair[0][:, co, :]), hi, prior)
                    g_marks.extend([hi, lo])
                    return a

                linear(use(unit_m(0, g)), h_pair, h_ready, out_g, [0, 1, 2, 3])
                x_marks = []

                def add_mlp(co, src, mark):
                    if g == 0:
                        m = DVE.step(lambda e: e.scalar_tensor_tensor(
                            xh[:, co, :], src, col("M_b2", co), xh[:, co, :], ALU.add, ALU.add), mark)
                    else:
                        m = DVE.step(lambda e: e.tensor_tensor(xh[:, co, :], xh[:, co, :], src, ALU.add), mark)
                    x_marks.append(m)
                    return m

                m = [linear(use(unit_m(1, g)), q_pair, g_marks, add_mlp, [4, 5, 6, 7]), g_marks]
                return m, x_marks

            for hf in range(NH):
                ctx_ready = load_context(hf)
                x_marks = x_ready[hf]
                for att in (0, 1):
                    x_marks = attention(hf, att, ctx_ready, x_marks)
                h_ready = norm_to_pair(hf, "M", x_marks)
                m = h_ready
                for g in range(NG):
                    m, x_marks = mlp_group(hf, g, h_ready, m)
                stored = out_dma.load(SY, out[:, :, hf, :], x[:, :, hf, :], x_marks)
            SY.wait(stored)

            with nc.Block() as block:
                @block.sync
                def _(e):
                    SY.play(e)

                @block.tensor
                def _(e):
                    PE.play(e)

                @block.vector
                def _(e):
                    DVE.play(e)

                @block.scalar
                def _(e):
                    SC.play(e)

                @block.gpsimd
                def _(e):
                    GP.play(e)


def kernel(**inputs):
    import concourse.bacc as bacc
    from concourse.bass_utils import run_bass_kernel_spmd

    get = {k: np.asarray(v) for k, v in inputs.items()}

    def tiles(w):
        return w.reshape(CT, P, w.shape[-1]).transpose(1, 0, 2)

    def column(v):
        return v.reshape(-1, P).T

    xT = tiles(get["x"].reshape(B * L, D).T).reshape(P, CT, NH, HN)
    c = get["ctx_2048"]
    ctxT = np.zeros((B, P, CT, SP), np.float32)
    ctxT[:, :, :, 0:S] = c.transpose(0, 2, 1).reshape(B, CT, P, S).transpose(0, 2, 1, 3)
    ctx_tok = np.zeros((B, 3 * P, D), np.float32)
    ctx_tok[:, 0:S] = c
    ctx_tok = ctx_tok.reshape(B, 3, P, D).transpose(0, 2, 1, 3)
    s0 = c[:, 2:2 + HS].reshape(B, CT, P // HS, HS, HS).transpose(2, 3, 1, 4, 0).reshape(P, CT, HS, B)
    shift = c[:, 0:2].reshape(B, 2, CT, P).transpose(3, 2, 1, 0)

    blocks = [get["L0_xattn_w_q"].T, get["L0_xattn_w_k"], get["L0_xattn_w_v"].T, get["L0_xattn_w_o"].T]
    r_names = [
        dict(k="Wk", v="Wv", r="Wr", g="Wg", o="Wo", fr="fWr", fk="fWk", fv="fWv", mix1="maa_w1", mix2="maa_w2",
             dec1="decay_w1", dec2="decay_w2", decay="time_decay", u="faaaa", fmaa_k="fmaa_k", fmaa_r="fmaa_r"),
        dict(k="Wk", v="Wv", r="Wr", g="Wg", o="Wo", fr="Wfr", fk="Wfk", fv="Wfv", mix1="maa_w1", mix2="maa_w2",
             dec1="td_w1", dec2="td_w2", decay="time_decay", u="u", fmaa_k="ffn_maa_k", fmaa_r="ffn_maa_r"),
    ]
    vectors, mix1, mix2, dec1, dec2 = [], [], [], [], []
    for layer, names in enumerate(r_names):
        pre = f"L{layer + 1}_xattn_"
        blocks += [get[pre + names[n]].T for n in R_ORDER]
        mix1.append(tiles(get[pre + names["mix1"]]))
        mix2.append(get[pre + names["mix2"]].reshape(5 * DM, D))
        dec1.append(tiles(get[pre + names["dec1"]]))
        dec2.append(get[pre + names["dec2"]])
        for v in R_VECS:
            if layer == 1 and v[:4] == "maa_" and v != "maa_x":
                vectors.append(column(get[pre + "maa_stack"][0, "kwvrg".index(v[4])]))
            else:
                vectors.append(column(get[pre + names.get(v, v)].reshape(D)))
    rows = []
    for att in (0, 1):
        n = str(att + 1)
        X = lambda name: get["L3_xattn_" + name + n]
        for g in range(NG):
            s = slice(g * D, (g + 1) * D)
            blocks += [X("wq")[:, s], X("wk")[:, s], X("wv")[:, s], X("wo")[s]]
        vectors += [column(get[f"L3_xattn_ln{n}_scale"]), column(get[f"L3_xattn_ln{n}_offset"])]
        vectors += [column(X("bq")), column(X("bk")), column(X("bv")), column(X("bias_k").reshape(-1)), column(X("bo"))]
        rows.append(np.stack([X("bias_v").reshape(NG, D), X("bv").reshape(NG, D)], 1)[:, None])
    w1, w2 = get["L3_xattn_w_fc1"], get["L3_xattn_w_fc2"]
    blocks += [w1[:, g * D:(g + 1) * D] for g in range(NG)] + [w2[g * D:(g + 1) * D] for g in range(NG)]
    vectors += [column(get["L3_xattn_ln_mlp_scale"]), column(get["L3_xattn_ln_mlp_offset"])]
    vectors += [column(get["L3_xattn_b_fc1"]), column(get["L3_xattn_b_fc2"])]
    vectors += [np.broadcast_to(get["L0_xattn_alpha"].reshape(1, 1), (P, 1)), np.full((P, 1), EPS, np.float32)]
    weights = np.stack([tiles(b).reshape(P, UNIT) for b in blocks])

    head = np.arange(P) // HS
    same = (head[:, None] == head[None, :]).astype(np.float32)
    collect = np.zeros((P, P + HS - 1), np.float32)
    collect[np.arange(P), HS * head + HS - 1] = 1.0
    pick = np.zeros((P, HS, P), np.float32)
    for j in range(HS):
        pick[HS * head + j, j, np.arange(P)] = 1.0
    consts = np.concatenate([np.eye(P, dtype=np.float32), np.full((P, P), 1.0 / D, np.float32), same,
                             same / np.float32(HS), collect, pick.reshape(P, -1)], 1)

    arrays = {"xT": xT, "ctxT": ctxT, "ctx_tok": ctx_tok, "s0": s0, "shift": shift, "weights": weights,
              "mix1": np.stack(mix1), "mix2": np.stack(mix2), "dec1": np.stack(dec1), "dec2": np.stack(dec2),
              "cols": np.concatenate(vectors, 1), "rows": np.stack(rows), "consts": consts}
    arrays = {k: np.ascontiguousarray(v) for k, v in arrays.items()}
    nc = bacc.Bacc("TRN2", target_bir_lowering=False, num_devices=1)
    args = [nc.dram_tensor(k, v.shape, F32, kind="ExternalInput").ap() for k, v in arrays.items()]
    out = nc.dram_tensor("result", (P, CT, NH, HN), F32, kind="ExternalOutput").ap()
    build(nc, *args, out)
    got = run_bass_kernel_spmd(nc, [arrays], core_ids=[0]).results[0]["result"]
    return got.transpose(2, 3, 1, 0).reshape(B, L, D)
```

```python
from contextlib import ExitStack

import numpy as np
import concourse.bass as bass
from concourse import mybir

F32 = mybir.dt.float32
F32R = mybir.dt.float32r
ACT = mybir.ActivationFunctionType
ALU = mybir.AluOpType
AXX = mybir.AxisListType.X

P = 128
B, L, D = 8, 112, 512
S = 375
SP = S + 1
CT = D // P
NH = 2
HB = B // NH
HN = HB * L
T = CT * HN
NS, HS = 32, 16
GJ = 4
DM, DD = 32, 64
XH, XK = 16, 128
HG = 4
NG = XH // HG
F = 2048
CH = [(0, 128), (128, 128), (256, 120)]
UNIT = CT * D
EPS = 1e-5

U_L0 = {n: i for i, n in enumerate(["q", "k", "v", "o"])}
R_ORDER = ["k", "v", "r", "g", "o", "fk", "fr", "fv"]


def unit_r(layer, name):
    return 4 + 8 * layer + R_ORDER.index(name)


def unit_x(att, name, g):
    return 20 + 16 * att + 4 * g + ["q", "k", "v", "o"].index(name)


def unit_m(which, g):
    return 52 + 4 * which + g


N_UNITS = 60

R_VECS = ["ln1_w", "ln1_b", "ln2_w", "ln2_b", "maa_x", "maa_w", "maa_k", "maa_v", "maa_r", "maa_g",
          "decay", "u", "gn_w", "gn_b", "fmaa_k", "fmaa_r"]


def vector_columns():
    col, n = {}, 0
    for layer in (0, 1):
        for v in R_VECS:
            col[f"R{layer}_{v}"] = n
            n += CT
    for att in (0, 1):
        for v, w in (("ln_w", CT), ("ln_b", CT), ("bq", XH), ("bk", XH), ("bv", XH), ("bias_k", XH), ("bo", CT)):
            col[f"X{att}_{v}"] = n
            n += w
    for v, w in (("ln_w", CT), ("ln_b", CT), ("b1", F // P), ("b2", CT), ("alpha", 1), ("eps", 1)):
        col[f"M_{v}"] = n
        n += w
    return col, n


COL, NCOL = vector_columns()


class Queue:

    def __init__(self, sem):
        self.sem, self.count, self.todo, self.waited = sem, 0, [], {}

    def wait(self, *marks):
        for m in marks:
            if m is None:
                continue
            if isinstance(m, list):
                self.wait(*m)
                continue
            sem, value = m
            if self.waited.get(id(sem), 0) < value:
                self.waited[id(sem)] = value
                self.todo.append(lambda e, s=sem, v=value: e.wait_ge(s, v))

    def run(self, instruction, *after):
        self.wait(*after)
        self.todo.append(instruction)

    def step(self, instruction, *after):
        self.wait(*after)
        self.count += 1
        self.todo.append(lambda e, f=instruction: f(e).then_inc(self.sem, 1))
        return (self.sem, self.count)

    def now(self):
        return (self.sem, self.count) if self.count else None

    def play(self, engine):
        for f in self.todo:
            f(engine)


class Loads:

    def __init__(self, sem):
        self.sem, self.count = sem, 0

    def load(self, queue, dst, src, *after):
        queue.wait(*after)
        self.count += 16
        queue.todo.append(lambda e: e.dma_start(dst, src).then_inc(self.sem, 16))
        return (self.sem, self.count)


def build(nc, xT, ctxT, ctx_tok, s0, shift, weights, mix1, mix2, dec1, dec2, cols, rows, consts, out):
    with ExitStack() as ctx:
        def sb(stack, name, shape, dt=F32):
            return stack.enter_context(nc.sbuf_tensor(name, shape, dt))

        def sem(name):
            return ctx.enter_context(nc.semaphore(name))

        PE, DVE, SC, GP, SY = (Queue(sem(n)) for n in ("pe_done", "dve_done", "act_done", "pool_done", "sp_done"))

        x = sb(ctx, "x", [P, CT, NH, HN])
        vec = sb(ctx, "vec", [P, NCOL])
        ident = sb(ctx, "ident", [P, P])
        ones = sb(ctx, "ones", [P, P])
        raw = sb(ctx, "raw", [P, UNIT])
        NW = 3
        w_hi = [sb(ctx, f"w_hi{i}", [P, CT, D], F32R) for i in range(NW)]
        w_lo = [sb(ctx, f"w_lo{i}", [P, CT, D], F32R) for i in range(NW)]
        std = sb(ctx, "std", [P, HN])
        ps = ctx.enter_context(nc.psum_tensor("ps", [P, 8, 512], F32))

        bank_free = [None] * 8

        order = []

        def enter(unit, slot):
            order.append((unit, slot))
            return slot

        for unit in ([U_L0[n] for n in ("q", "k", "v", "o")] * NH
                     + [unit_r(layer, n) for layer in (0, 1) for _ in range(NH) for n in R_ORDER]):
            enter(unit, len(order) % NW)
        sq_, sv, sk = (len(order) % NW, (len(order) + 1) % NW, (len(order) + 2) % NW)
        for hf in range(NH):
            for att in (0, 1):
                enter(unit_x(att, "q", 0), sq_), enter(unit_x(att, "v", 0), sv), enter(unit_x(att, "k", 0), sk)
                for g in range(NG):
                    if g + 1 < NG:
                        enter(unit_x(att, "v", g + 1), sq_)
                        enter(unit_x(att, "o", g), sv)
                        enter(unit_x(att, "q", g + 1), sk)
                        enter(unit_x(att, "k", g + 1), sv)
                        sq_, sv, sk = sk, sq_, sv
                    else:
                        enter(unit_x(att, "o", g), sv)
                        sv, sk = sk, sv
            spare = [sq_, sv, sk]
            for i in range(2 * NG):
                enter(unit_m(i % 2, i // 2), spare[i % NW])
            n = 2 * NG
            sq_, sv, sk = spare[n % NW], spare[(n + 1) % NW], spare[(n + 2) % NW]
        raw_dma = Loads(sem("raw_loaded"))
        raw_mark, raw_free = [None], [None]
        ready_of = [None] * len(order)
        slot_free = [None] * NW
        slot_busy = [False] * NW
        fetched, used = [0], [0]

        def load_raw(n):
            if n < len(order):
                raw_mark[0] = raw_dma.load(SY, raw[:, :], weights[order[n][0], :, :], raw_free[0])

        def fetch():
            while fetched[0] < len(order) and not slot_busy[order[fetched[0]][1]]:
                n = fetched[0]
                i = order[n][1]
                fetched[0] += 1
                slot_busy[i] = True
                flat_hi = w_hi[i][:, :, :].rearrange("p a b -> p (a b)")
                flat_lo = w_lo[i][:, :, :].rearrange("p a b -> p (a b)")
                hi = SC.step(lambda e, d=flat_hi: e.activation(d, raw[:, :], ACT.Copy), raw_mark[0], slot_free[i])
                lo = GP.step(lambda e, d=flat_lo, h=flat_hi: e.tensor_tensor(d, raw[:, :], h.bitcast(F32), ALU.subtract),
                             raw_mark[0], hi, slot_free[i])
                ready_of[n] = [hi, lo]
                raw_free[0] = [hi, lo]
                load_raw(n + 1)

        def use(unit):
            fetch()
            n = used[0]
            used[0] += 1
            assert order[n][0] == unit and n < fetched[0], (n, unit, order[n])
            return n

        def done(n, mark):
            i = order[n][1]
            slot_free[i], slot_busy[i] = mark, False
            fetch()

        def products(dst, terms, *after, each=None):
            PE.wait(*after)
            for i, (lhsT, rhs) in enumerate(terms[:-1]):
                if each:
                    PE.wait(each[i])
                PE.run(lambda e, a=lhsT, b=rhs, s=(i == 0): e.matmul(dst, a, b, start=s, stop=False))
            if each:
                PE.wait(each[-1])
            a, b = terms[-1]
            return PE.step(lambda e: e.matmul(dst, a, b, start=(len(terms) == 1), stop=True))

        def three(a, b):
            return [(a[0], b[0]), (a[0], b[1]), (a[1], b[0])]

        def linear(n, pair, ready, evacuate, banks):
            i = order[n][1]
            mark = None
            for co in range(CT):
                bank = banks[co % len(banks)]
                terms = []
                for ct in range(CT):
                    w = (w_hi[i][:, ct, co * P:(co + 1) * P], w_lo[i][:, ct, co * P:(co + 1) * P])
                    m = (pair[0][:, ct, :], pair[1][:, ct, :])
                    terms += three(w, m)
                mark = products(ps[:, bank, 0:HN], terms, ready_of[n], ready, bank_free[bank])
                bank_free[bank] = evacuate(co, ps[:, bank, 0:HN], mark)
            done(n, mark)
            return mark

        def linear_by_input(n, pair, ready, evacuate, banks):
            i = order[n][1]
            marks = [None] * CT
            PE.wait(ready_of[n], [bank_free[b] for b in banks])
            for ct in range(CT):
                PE.wait(ready[ct])
                for co in range(CT):
                    dst = ps[:, banks[co], 0:HN]
                    w = (w_hi[i][:, ct, co * P:(co + 1) * P], w_lo[i][:, ct, co * P:(co + 1) * P])
                    terms = three(w, (pair[0][:, ct, :], pair[1][:, ct, :]))
                    for t, (a, b) in enumerate(terms):
                        first, last = ct == 0 and t == 0, ct == CT - 1 and t == 2
                        what = lambda e, d=dst, a=a, b=b, f=first, l=last: e.matmul(d, a, b, start=f, stop=l)
                        if last:
                            marks[co] = PE.step(what)
                        else:
                            PE.run(what)
            for co in range(CT):
                bank_free[banks[co]] = evacuate(co, ps[:, banks[co], 0:HN], marks[co])
            done(n, marks[-1])
            return marks[-1]

        def split_tile(pair, ct, src, ready, free):
            hi = SC.step(lambda e: e.activation(pair[0][:, ct, :], src, ACT.Copy), ready, free)
            lo = DVE.step(lambda e: e.tensor_tensor(pair[1][:, ct, :], src, pair[0][:, ct, :].bitcast(F32),
                                                    ALU.subtract), hi, ready, free)
            return [hi, lo]

        def split(pair, src, ready, free):
            hi = SC.step(lambda e: e.activation(pair[0][:, :, :], src, ACT.Copy), ready, free)
            lo = DVE.step(lambda e: e.tensor_tensor(pair[1][:, :, :], src, pair[0][:, :, :].bitcast(F32), ALU.subtract),
                          hi, ready, free)
            return [hi, lo]

        def col(name, i=0):
            c = COL[name] + i
            return vec[:, c:c + 1]

        def layer_norm(src, cen, sq, ready, free, b0, b1):
            m = products(ps[:, b0, 0:HN], [(ones[:, :], src[:, ct, :]) for ct in range(CT)], bank_free[b0],
                         each=ready)
            v = [None] * CT
            for ct in range(CT):
                c = DVE.step(lambda e, ct=ct: e.tensor_tensor(cen[:, ct, :], src[:, ct, :], ps[:, b0, 0:HN],
                                                              ALU.subtract), m, ready, free)
                s = SC.step(lambda e, ct=ct: e.activation(sq[ct % len(sq)], cen[:, ct, :], ACT.Square), c, free,
                            v[ct - len(sq)] if ct >= len(sq) else None)
                PE.wait(s, bank_free[b1])
                v[ct] = PE.step(lambda e, ct=ct: e.matmul(ps[:, b1, 0:HN], ones[:, :], sq[ct % len(sq)],
                                                          start=(ct == 0), stop=(ct == CT - 1)))
            bank_free[b0] = c
            r = SC.step(lambda e: e.activation(std[:, :], ps[:, b1, 0:HN], ACT.Sqrt, bias=col("M_eps")), v[-1], DVE.now())
            bank_free[b1] = r
            r = DVE.step(lambda e: e.reciprocal(std[:, :], std[:, :]), r)
            return [DVE.step(lambda e, ct=ct: e.tensor_tensor(cen[:, ct, :], cen[:, ct, :], std[:, :], ALU.mult), r)
                    for ct in range(CT)]

        def barrier():
            marks = [q.now() for q in (PE, DVE, SC, GP)]
            for q in (PE, DVE, SC, GP, SY):
                q.wait(*marks)

        start = Loads(sem("start_loaded"))
        load_raw(0)
        first = start.load(SY, x[:, :, :, :], xT)
        first = start.load(SY, vec[:, :], cols)
        first = start.load(SY, ident[:, :], consts[:, 0:P])
        first = start.load(SY, ones[:, :], consts[:, P:2 * P])
        for q in (PE, DVE, SC, GP):
            q.wait(first)
        x_ready = [[None] * CT] * NH

        with ExitStack() as early:
            def act(name, dt=F32):
                return sb(early, name, [P, CT, HN], dt)

            xa = sb(early, "xa", [P, CT, HB, L + 1])
            sx = act("sx")
            tmp_a, tmp_b = act("tmp_a"), act("tmp_b")
            pairs = [(act("p0_hi", F32R), act("p0_lo", F32R)), (act("p1_hi", F32R), act("p1_lo", F32R))]
            r_, k_, v_, w_ = act("r"), act("k"), act("v"), act("w")
            ring = [sb(early, f"ring{i}", [P, GJ, HN]) for i in range(3)]
            block16 = sb(early, "block16", [P, P])
            mean16 = sb(early, "mean16", [P, P])
            centre16 = sb(early, "centre16", [P, P])
            collect = sb(early, "collect", [P, P + HS - 1])
            pick = sb(early, "pick", [P, HS, P], F32R)
            mix1_w = sb(early, "mix1_w", [P, CT, 5 * DM])
            mix2_a = sb(early, "mix2_a", [P, D])
            mix2_b = sb(early, "mix2_b", [DM, D])
            dec1_w = sb(early, "dec1_w", [P, CT, DD])
            dec2_w = sb(early, "dec2_w", [DD, D])
            s0_t = sb(early, "s0_t", [P, CT, HS, B])
            shift_t = sb(early, "shift_t", [P, CT, 2, B])
            soft = sb(early, "soft", [P, 8])

            ctx_dma = [Loads(sem(f"ctx_loaded{i}")) for i in range(3)]
            ctx_buf = [(ring[0], ring[1]), (ring[2], k_), (r_, w_)]
            ctx_free = [None] * 3
            prob = [v_[:, i, :] for i in range(2)]
            probT = [v_[:, 2 + i, 0:3 * L].rearrange("p (c q) -> p c q", c=3) for i in range(2)]
            p_free, pt_free = [None] * 2, [None] * 2

            def cross_attention_0(hf):
                xh = x[:, :, hf, :]
                ctx_views, ctx_mark = [], []

                def load_ctx(b):
                    i = b % HB % 3
                    keyT = ctx_buf[i][0][:, :, :].rearrange("p a b -> p (a b)")[:, 0:CT * SP].rearrange(
                        "p (a b) -> p a b", a=CT)
                    tok = ctx_buf[i][1][:, :, :].rearrange("p a b -> p (a b)")[:, 0:3 * D].rearrange(
                        "p (a b) -> p a b", a=3)
                    ctx_dma[i].load(SY, keyT, ctxT[b], ctx_free[i])
                    ctx_mark.append(ctx_dma[i].load(SY, tok, ctx_tok[b]))
                    ctx_views.append((keyT, tok))

                load_ctx(hf * HB)
                load_ctx(hf * HB + 1)
                load_ctx(hf * HB + 2)
                ready = split(pairs[0], xh, x_ready[hf], PE.now())

                def q_out(co, src, mark):
                    hi = SC.step(lambda e: e.activation(pairs[1][0][:, co, :], src, ACT.Copy), mark)
                    lo = DVE.step(lambda e: e.tensor_tensor(pairs[1][1][:, co, :], src,
                                                            pairs[1][0][:, co, :].bitcast(F32), ALU.subtract), hi)
                    q_marks.extend([hi, lo])
                    return [hi, lo]

                q_marks = []
                linear(use(U_L0["q"]), pairs[0], ready, q_out, [0, 1, 2, 3])
                g_marks = []

                def g_out(co, src, mark):
                    g_marks.append(SC.step(lambda e: e.activation(tmp_a[:, co, :], src, ACT.Copy), mark, PE.now()))
                    return g_marks[-1]

                linear(use(U_L0["k"]), pairs[1], q_marks, g_out, [4, 5, 6, 7])
                c_marks = []
                scale = float(D) ** -0.5

                def score(bb):
                    keyT, _ = ctx_views[bb]
                    i = bb % 2
                    sc, st, pr = ps[0:L, i, 0:SP], soft[0:L, 4 * i:4 * i + 4], prob[i]
                    m = products(sc, [(tmp_a[:, ct, bb * L:(bb + 1) * L], keyT[:, ct, :]) for ct in range(CT)],
                                 g_marks, ctx_mark[bb], bank_free[i])
                    m = DVE.step(lambda e: e.tensor_reduce(st[:, 0:1], sc[:, 0:S], AXX, ALU.max), m, p_free[i])
                    m = DVE.step(lambda e: e.tensor_scalar(st[:, 1:2], st[:, 0:1], -scale, None, ALU.mult), m)
                    m = SC.step(lambda e: e.activation(pr[0:L, 0:S], sc[:, 0:S], ACT.Exp, bias=st[:, 1:2],
                                                       scale=scale, accum_out=st[:, 2:3]), m, p_free[i])
                    bank_free[i] = m
                    m = DVE.step(lambda e: e.reciprocal(st[:, 3:4], st[:, 2:3]), m)
                    return DVE.step(lambda e: e.tensor_scalar(pr[0:L, 0:S], pr[0:L, 0:S], st[:, 3:4], None, ALU.mult), m)

                def turn(bb, ready):
                    i = bb % 2
                    pr, pt = prob[i], probT[i]
                    PE.wait(ready, bank_free[2 + i])
                    for c, (t0, n) in enumerate(CH):
                        n = min(n, S - t0)
                        m = PE.step(lambda e, c=c, t0=t0, n=n: e.transpose(
                            ps[0:n, 2 + i, c * L:(c + 1) * L], pr[0:L, t0:t0 + n], ident[0:L, 0:L]))
                    p_free[i] = m
                    a = SC.step(lambda e: e.activation(
                        pt[:, 0:2, :], ps[:, 2 + i, 0:2 * L].rearrange("p (c q) -> p c q", c=2), ACT.Copy), m, pt_free[i])
                    a = SC.step(lambda e: e.activation(
                        pt[0:S - 2 * P, 2, :], ps[0:S - 2 * P, 2 + i, 2 * L:3 * L], ACT.Copy), m, pt_free[i])
                    bank_free[2 + i] = a
                    return a

                def weigh(bb, ready):
                    i = bb % 2
                    tok, pt, dst = ctx_views[bb][1], probT[i], tmp_b[:, :, bb * L:(bb + 1) * L]
                    PE.wait(ready, bank_free[4 + i])
                    for dt in range(CT):
                        m = products(ps[:, 4 + i, dt * L:(dt + 1) * L],
                                     [(tok[0:min(n, S - t0), c, dt * P:(dt + 1) * P], pt[0:min(n, S - t0), c, :])
                                      for c, (t0, n) in enumerate(CH)])
                    ctx_free[bb % 3] = pt_free[i] = m
                    m = DVE.step(lambda e: e.tensor_copy(
                        dst, ps[:, 4 + i, 0:CT * L].rearrange("p (c q) -> p c q", c=CT)), m)
                    bank_free[4 + i] = m
                    c_marks.append(m)
                    if bb + 3 < HB:
                        load_ctx(hf * HB + bb + 3)

                scored, turned = {}, {}
                for step in range(HB + 2):
                    if step < HB:
                        scored[step] = score(step)
                    if 1 <= step <= HB:
                        turned[step - 1] = turn(step - 1, scored[step - 1])
                    if step == 1 or step == 0:
                        continue
                    weigh(step - 2, turned[step - 2])
                ready = split(pairs[0], tmp_b[:, :, :], c_marks, PE.now())
                q_marks = []
                linear(use(U_L0["v"]), pairs[0], ready, q_out, [3, 4, 5, 6])
                x_marks = []

                def o_out(co, src, mark):
                    x_marks.append(DVE.step(lambda e: e.scalar_tensor_tensor(
                        xh[:, co, :], src, col("M_alpha"), xh[:, co, :], ALU.mult, ALU.add), mark))
                    return x_marks[-1]

                linear(use(U_L0["o"]), pairs[1], q_marks, o_out, [0, 1, 2, 7])
                x_ready[hf] = x_marks

            cross_attention_0(0)
            early_dma = Loads(sem("early_loaded"))
            at = 4 * P
            halves = (xa[:, :, :, :].rearrange("p a b c -> p (a b c)")[:, 0:P * HS // 2],
                      sx[:, :, :].rearrange("p a b -> p (a b)")[:, 0:P * HS // 2])
            early_dma.load(SY, block16[:, :], consts[:, 2 * P:3 * P])
            early_dma.load(SY, mean16[:, :], consts[:, 3 * P:4 * P])
            early_dma.load(SY, centre16[:, :], consts[:, at:at + P])
            early_dma.load(SY, collect[:, :], consts[:, at + P:at + 2 * P + HS - 1])
            at += 2 * P + HS - 1
            for i, dst in enumerate(halves):
                early_dma.load(SY, dst, consts[:, at + i * P * HS // 2:at + (i + 1) * P * HS // 2])
            early_dma.load(SY, s0_t[:, :, :, :], s0)
            c_ready = early_dma.load(SY, shift_t[:, :, :, :], shift)
            cross_attention_0(1)
            for i, src in enumerate(halves):
                pick_ready = SC.step(lambda e, i=i, r=src: e.activation(
                    pick[:, i * HS // 2:(i + 1) * HS // 2, :].rearrange("p a b -> p (a b)"), r, ACT.Copy), c_ready)

            barrier()
            PE.wait(c_ready)
            DVE.wait(c_ready)
            GP.wait(c_ready)
            w4 = w_[:, :, :].rearrange("p c (b t) -> p c b t", b=HB)
            w_zero = DVE.step(lambda e: e.memset(w4[:, :, :, 0:1], 0.0))
            small_dma = Loads(sem("small_loaded"))
            xa_now = xa[:, :, :, 1:L + 1]
            xa_prev = xa[:, :, :, 0:L]
            by_seq = lambda ap: ap.rearrange("p c (b t) -> p c b t", b=HB)

            def seq(tile):
                return tile.rearrange("p (b t) -> p b t", b=HB)

            def normalise_and_shift(layer, hf, name, which, ready):
                prior = [PE.now(), DVE.now(), GP.now(), SC.now()]
                st = GP.step(lambda e: e.tensor_copy(xa[:, :, :, 0], shift_t[:, :, which, hf * HB:(hf + 1) * HB]), prior)
                c = layer_norm(x[:, :, hf, :], tmp_a[:, :, :], [tmp_b[:, ct, :] for ct in range(CT)], ready, prior, 0, 1)
                marks = []
                for ct in range(CT):
                    a = SC.step(lambda e, ct=ct: e.activation(
                        xa_now[:, ct, :, :], seq(tmp_a[:, ct, :]), ACT.Identity,
                        bias=col(f"R{layer}_{name}_b", ct), scale=col(f"R{layer}_{name}_w", ct)), c[ct], prior)
                    s = DVE.step(lambda e, ct=ct: e.tensor_tensor(
                        seq(sx[:, ct, :]), xa_prev[:, ct, :, :], xa_now[:, ct, :, :], ALU.subtract), a, st)
                    marks.append([s, a, st])
                return marks

            def recurrent_half(layer, hf, small):
                def V(v, ct):
                    return col(f"R{layer}_{v}", ct)

                def shifted(dst, name, ct, xs, *free):
                    return DVE.step(lambda e: e.scalar_tensor_tensor(
                        seq(dst[:, ct, :]), seq(sx[:, ct, :]), V(name, ct), xa_now[:, ct, :, :],
                        ALU.mult, ALU.add), xs[ct], *free)

                xh = x[:, :, hf, :]
                xs = normalise_and_shift(layer, hf, "ln1", 1, x_ready[hf])
                xxx = tmp_b
                m = [shifted(xxx, "maa_x", ct, xs, PE.now()) for ct in range(CT)]
                affine_done = SC.now()
                h1 = products(ps[:, 2, 0:HN], [(mix1_w[:, ct, 0:P], xxx[:, ct, :]) for ct in range(CT)],
                              small, bank_free[2], each=m)
                h1 = SC.step(lambda e: e.activation(tmp_a[:, 0, :], ps[:, 2, 0:HN], ACT.Tanh), h1, affine_done)
                bank_free[2] = h1
                h2 = products(ps[0:DM, 3, 0:HN], [(mix1_w[:, ct, P:P + DM], xxx[:, ct, :]) for ct in range(CT)],
                              bank_free[3])
                h2 = SC.step(lambda e: e.activation(tmp_a[0:DM, 1, :], ps[0:DM, 3, 0:HN], ACT.Tanh), h2, affine_done)
                bank_free[3] = h2
                names = ["w", "k", "v", "r", "g"] if layer == 0 else ["k", "w", "v", "r", "g"]

                def mix(name, dst, free):
                    f = names.index(name)
                    marks = []
                    for ct in range(CT):
                        lhsT, rhs = ((mix2_a[f * DM:(f + 1) * DM, ct * P:(ct + 1) * P], tmp_a[f * DM:(f + 1) * DM, 0, :])
                                     if f < 4 else (mix2_b[:, ct * P:(ct + 1) * P], tmp_a[0:DM, 1, :]))
                        m = products(ps[:, ct, 0:HN], [(lhsT, rhs)], h1, h2, bank_free[ct])
                        m = DVE.step(lambda e, ct=ct: e.scalar_tensor_tensor(
                            dst[:, ct, :], ps[:, ct, 0:HN], V("maa_" + name, ct), sx[:, ct, :],
                            ALU.add, ALU.mult), m, free)
                        bank_free[ct] = m
                        marks.append(GP.step(lambda e, ct=ct: e.tensor_tensor(
                            seq(dst[:, ct, :]), seq(dst[:, ct, :]), xa_now[:, ct, :, :], ALU.add), m))
                    return marks

                dest = {"k": k_, "v": v_, "r": r_, "g": sx}
                got = {}

                def project(name, pair, ready, *free):
                    marks = got[name] = []
                    func = ACT.Silu if name == "g" else ACT.Copy

                    def out_of(co, src, mark):
                        marks.append(SC.step(lambda e: e.activation(dest[name][:, co, :], src, func), mark, *free))
                        return marks[-1]

                    return linear(use(unit_r(layer, name)), pair, ready, out_of, [4, 5, 6, 7])

                start_free = PE.now()
                mixed_w = mix("w", ring[0], start_free)
                mixed_k = mix("k", ring[1], start_free)
                k_split = split(pairs[0], ring[1][:, :, :], mixed_k, start_free)
                m = products(ps[0:DD, 4, 0:HN], [(dec1_w[:, ct, :], ring[0][:, ct, :]) for ct in range(CT)],
                             bank_free[4], each=mixed_w)
                w_read = m
                m = SC.step(lambda e: e.activation(tmp_a[0:DD, 2, :], ps[0:DD, 4, 0:HN], ACT.Tanh), m, affine_done)
                bank_free[4] = m
                mixed_v = mix("v", ring[2], start_free)
                v_in_split = split(pairs[1], ring[2][:, :, :], mixed_v, start_free)
                w_marks = []
                for ct in range(CT):
                    q = products(ps[:, 4 + ct, 0:HN], [(dec2_w[:, ct * P:(ct + 1) * P], tmp_a[0:DD, 2, :])],
                                 m, bank_free[4 + ct])
                    q = SC.step(lambda e, ct=ct: e.activation(
                        tmp_a[:, 3, :], ps[:, 4 + ct, 0:HN], ACT.Exp, bias=V("decay", ct)), q, w_marks, affine_done)
                    bank_free[4 + ct] = q
                    w_marks.append(SC.step(lambda e, ct=ct: e.activation(
                        w4[:, ct, :, 1:L], seq(tmp_a[:, 3, :])[:, :, 0:L - 1], ACT.Exp, scale=-1.0), q, w_zero))
                k_used = project("k", pairs[0], k_split)
                mixed_r = mix("r", ring[0], w_read)
                r_split = split(pairs[0], ring[0][:, :, :], mixed_r, k_used)
                v_used = project("v", pairs[1], v_in_split)
                mixed_g = mix("g", ring[1], k_split)
                g_split = split(pairs[1], ring[1][:, :, :], mixed_g, v_used)
                r_used = project("r", pairs[0], r_split)
                v_pair = pairs[0]
                v_split = split(v_pair, v_[:, :, :], got["v"], r_used)
                g_used = project("g", pairs[1], g_split, mixed_g)

                ring_free = [[v_in_split, g_split, r_split]] * 3
                turns = [(ct, jg) for ct in range(CT) for jg in range(HS // GJ)]
                own, y_marks, received, gathered = {}, [None] * CT, {}, {}

                def own_value(ct):
                    m = DVE.step(lambda e: e.scalar_tensor_tensor(
                        tmp_b[:, ct, :], r_[:, ct, :], V("u", ct), k_[:, ct, :], ALU.mult, ALU.mult),
                        got["r"], got["k"], h2)
                    m = products(ps[:, 7, 0:HN], [(block16[:, :], tmp_b[:, ct, :])], m, bank_free[7])
                    own[ct] = bank_free[7] = DVE.step(lambda e: e.tensor_tensor(
                        tmp_b[:, ct, :], ps[:, 7, 0:HN], v_[:, ct, :], ALU.mult), m, got["v"])

                def spread_and_scan(t):
                    ct, jg = turns[t]
                    buf, free = ring[t % 3], ring_free[t % 3]
                    buf4 = buf[:, :, :].rearrange("p j (b t) -> p j b t", b=HB)
                    st = GP.step(lambda e: e.tensor_copy(
                        buf4[:, :, :, 0], s0_t[:, ct, jg * GJ:(jg + 1) * GJ, hf * HB:(hf + 1) * HB]), free)
                    for jp in range(GJ // 2):
                        b0 = 2 * ((t * 2 + jp) % 3)
                        for q in range(2):
                            sel = pick[:, jg * GJ + jp * 2 + q, :]
                            m = products(ps[:, b0 + q, 0:HN],
                                         [(sel, v_pair[0][:, ct, :]), (sel, v_pair[1][:, ct, :])],
                                         v_split, pick_ready, bank_free[b0 + q])
                        key = seq(k_[:, ct, :])[:, :, 0:L - 1].unsqueeze(1).broadcast_to([P, 2, HB, L - 1])
                        m = DVE.step(lambda e, jp=jp, b0=b0, key=key: e.tensor_tensor(
                            buf4[:, 2 * jp:2 * jp + 2, :, 1:L],
                            ps[:, b0:b0 + 2, 0:HN].rearrange("p j (b t) -> p j b t", b=HB)[:, :, :, 0:L - 1],
                            key, ALU.mult), m, got["k"], free)
                        bank_free[b0] = bank_free[b0 + 1] = m
                    for jj in range(GJ):
                        last = DVE.step(lambda e, jj=jj: e.tensor_tensor_scan(
                            buf[:, jj, :], w_[:, ct, :], buf[:, jj, :], 0.0, ALU.mult, ALU.add), m, st, w_marks)
                    rb = r_[:, ct, :].unsqueeze(1).broadcast_to([P, GJ, HN])
                    received[t] = GP.step(lambda e: e.tensor_tensor(buf[:, :, :], buf[:, :, :], rb, ALU.mult),
                                          last, got["r"])

                def gather(t):
                    ct, jg = turns[t]
                    buf = ring[t % 3]
                    PE.wait(received[t], bank_free[6] if jg == 0 else None)
                    for jj in range(GJ):
                        j = jg * GJ + jj
                        what = lambda e, j=j, jj=jj: e.matmul(ps[:, 6, 0:HN], collect[:, HS - 1 - j:HS - 1 - j + P],
                                                              buf[:, jj, :], start=(j == 0), stop=(j == HS - 1))
                        if jj < GJ - 1:
                            PE.run(what)
                    gathered[ct] = ring_free[t % 3] = PE.step(what)

                def centre(ct):
                    m = DVE.step(lambda e: e.tensor_tensor(tmp_b[:, ct, :], tmp_b[:, ct, :], ps[:, 6, 0:HN], ALU.add),
                                 gathered[ct], own[ct])
                    bank_free[6] = m
                    m = products(ps[:, 7, 0:HN], [(centre16[:, :], tmp_b[:, ct, :])], m, bank_free[7])
                    m = SC.step(lambda e: e.activation(tmp_b[:, ct, :], ps[:, 7, 0:HN], ACT.Copy), m)
                    bank_free[7] = m
                    own[ct] = SC.step(lambda e: e.activation(tmp_a[:, ct, :], tmp_b[:, ct, :], ACT.Square), m, w_marks, h2,
                                      mixed_g)

                def deviation(ct):
                    m = products(ps[:, 7, 0:HN], [(mean16[:, :], tmp_a[:, ct, :])], own[ct], bank_free[7])
                    own[ct] = bank_free[7] = SC.step(lambda e: e.activation(
                        tmp_a[:, ct, :], ps[:, 7, 0:HN], ACT.Sqrt, bias=col("M_eps")), m)

                def finish(ct):
                    m = DVE.step(lambda e: e.reciprocal(tmp_a[:, ct, :], tmp_a[:, ct, :]), own[ct])
                    m = DVE.step(lambda e: e.tensor_tensor(tmp_b[:, ct, :], tmp_b[:, ct, :], tmp_a[:, ct, :], ALU.mult), m)
                    m = SC.step(lambda e: e.activation(tmp_b[:, ct, :], tmp_b[:, ct, :], ACT.Identity,
                                                       bias=V("gn_b", ct), scale=V("gn_w", ct)), m)
                    m = DVE.step(lambda e: e.tensor_tensor(tmp_b[:, ct, :], tmp_b[:, ct, :], sx[:, ct, :], ALU.mult),
                                 m, got["g"])
                    y_marks[ct] = split_tile(pairs[1], ct, tmp_b[:, ct, :], m, g_used)

                per = HS // GJ
                for t in range(len(turns) + 2):
                    if t < len(turns):
                        if t % per == 0:
                            own_value(t // per)
                        spread_and_scan(t)
                    if t >= 2:
                        gather(t - 2)
                        if (t - 2) % per == per - 1:
                            centre((t - 2) // per)
                        if t >= per + 2 and (t - 2) % per == 0:
                            deviation((t - 2) // per - 1)
                        if t >= per + 2 and (t - 2) % per == 1:
                            finish((t - 2) // per - 1)
                deviation(CT - 1)
                finish(CT - 1)
                x_marks = []

                def add_x(co, src, mark):
                    x_marks.append(DVE.step(lambda e: e.tensor_tensor(xh[:, co, :], xh[:, co, :], src, ALU.add), mark))
                    return x_marks[-1]

                linear_by_input(use(unit_r(layer, "o")), pairs[1], y_marks, add_x, [2, 3, 4, 5])

                xs = normalise_and_shift(layer, hf, "ln2", 0, x_marks)
                rr = tmp_a
                free = [PE.now(), GP.now()]
                k_split, r_split = [], []
                for name, dst, pair, marks in (("fmaa_k", ring[0], pairs[0], k_split), ("fmaa_r", ring[1], pairs[1], r_split)):
                    for ct in range(CT):
                        m = shifted(dst, name, ct, xs, free)
                        marks.append(split_tile(pair, ct, dst[:, ct, :], m, free))
                affine_done = SC.now()
                kk = ring[2]
                kk_marks, rr_marks = [], []

                def k_out(co, src, mark):
                    a = SC.step(lambda e: e.activation(kk[:, co, :], src, ACT.Relu), mark, free)
                    m = DVE.step(lambda e: e.tensor_tensor(kk[:, co, :], kk[:, co, :], kk[:, co, :], ALU.mult), a)
                    kk_done.append(m)
                    return a

                kk_done = []
                k_used = linear(use(unit_r(layer, "fk")), pairs[0], k_split, k_out, [4, 5, 6, 7])
                for co in range(CT):
                    kk_marks.append(split_tile(pairs[0], co, kk[:, co, :], kk_done[co], k_used))

                def r_out(co, src, mark):
                    rr_marks.append(SC.step(lambda e: e.activation(rr[:, co, :], src, ACT.Sigmoid), mark, affine_done))
                    return rr_marks[-1]

                linear(use(unit_r(layer, "fr")), pairs[1], r_split, r_out, [0, 1, 2, 3])
                x_marks = []

                def fv_out(co, src, mark):
                    m = DVE.step(lambda e: e.tensor_tensor(rr[:, co, :], rr[:, co, :], src, ALU.mult), mark, rr_marks)
                    x_marks.append(DVE.step(lambda e: e.tensor_tensor(
                        xh[:, co, :], xh[:, co, :], rr[:, co, :], ALU.add), m))
                    return m

                linear_by_input(use(unit_r(layer, "fv")), pairs[0], kk_marks, fv_out, [4, 5, 6, 7])
                x_ready[hf] = x_marks

            for layer in (0, 1):
                small_dma.load(SY, mix1_w[:, :, :], mix1[layer], PE.now())
                small_dma.load(SY, mix2_a[:, :], mix2[layer, 0:P, :])
                small_dma.load(SY, mix2_b[:, :], mix2[layer, P:P + DM, :])
                small_dma.load(SY, dec1_w[:, :, :], dec1[layer])
                small = small_dma.load(SY, dec2_w[:, :], dec2[layer])
                for hf in range(NH):
                    recurrent_half(layer, hf, small)

            barrier()

        with ExitStack() as late:
            ctx_pair = (sb(late, "ctx_hi", [P, HB, CT, SP], F32R), sb(late, "ctx_lo", [P, HB, CT, SP], F32R))
            h_pair = (sb(late, "h_hi", [P, CT, HN], F32R), sb(late, "h_lo", [P, CT, HN], F32R))
            q_pair = (sb(late, "q_hi", [P, HG, HN], F32R), sb(late, "q_lo", [P, HG, HN], F32R))
            k_pair = (sb(late, "k_hi", [P, HG, SP], F32R), sb(late, "k_lo", [P, HG, SP], F32R))
            v_pairs = [(sb(late, f"v_hi{i}", [P, 3, D], F32R), sb(late, f"v_lo{i}", [P, 3, D], F32R)) for i in range(2)]
            pt_pairs = [(sb(late, f"pt_hi{i}", [P, 3, L], F32R), sb(late, f"pt_lo{i}", [P, 3, L], F32R)) for i in range(2)]
            row_pair = sb(late, "row_pair", [1, 2, D], F32R)
            row_raw = sb(late, "row_raw", [P, 2, D])
            scratch = sb(late, "scratch", [P, T])
            soft = sb(late, "soft3", [P, 16])
            cen = scratch[:, :].rearrange("p (a b) -> p a b", a=CT)
            stage = scratch[:, 0:CT * SP].rearrange("p (a b) -> p a b", a=CT)
            probs = [scratch[0:L, i * SP:(i + 1) * SP] for i in range(3)]
            o_raw = scratch[:, 3 * SP:3 * SP + HG * L].rearrange("p (h q) -> p h q", h=HG)
            squares = [row_raw[:, i, 0:HN] for i in range(2)]
            row_dma, ctx_dma = Loads(sem("rows_loaded")), Loads(sem("late_ctx_loaded"))
            vrow_dma = [Loads(sem("vrow_moved0")), Loads(sem("vrow_moved1"))]
            out_dma = Loads(sem("stored"))
            SCALE = float(XK) ** -0.5
            BIAS_P = CH[2][1] - 1
            k_free = [None] * HG
            v_free = [None] * 2
            pt_free = [None] * 2
            p_free = [None] * 3
            turn = [0, 0]

            def minus(dst, src, hi):
                return lambda e: e.tensor_tensor(dst, src, hi.bitcast(F32), ALU.subtract)

            def load_context(hf):
                marks = []
                prior = [q.now() for q in (PE, DVE, GP, SC)]
                for bb in range(HB):
                    m = ctx_dma.load(SY, stage, ctxT[hf * HB + bb], prior if bb == 0 else marks)
                    hi = SC.step(lambda e, bb=bb: e.activation(ctx_pair[0][:, bb, :, :], stage, ACT.Copy), m, prior)
                    lo = DVE.step(minus(ctx_pair[1][:, bb, :, :], stage, ctx_pair[0][:, bb, :, :]), hi, m, prior)
                    marks += [hi, lo]
                return marks

            def norm_to_pair(hf, name, ready):
                prior = [q.now() for q in (PE, DVE, GP, SC)]
                c = layer_norm(x[:, :, hf, :], cen, squares, ready, prior, 0, 1)
                marks = []
                for ct in range(CT):
                    a = SC.step(lambda e, ct=ct: e.activation(cen[:, ct, :], cen[:, ct, :], ACT.Identity,
                                                              bias=col(name + "_ln_b", ct), scale=col(name + "_ln_w", ct)), c[ct])
                    marks += split_tile(h_pair, ct, cen[:, ct, :], a, prior)
                return marks

            def attention(hf, att, ctx_ready, x_marks):
                xh = x[:, :, hf, :]
                A = f"X{att}_"
                h_ready = norm_to_pair(hf, f"X{att}", x_marks)
                q_marks, k_marks, v_marks = [], [None] * HG, [None] * 2
                col_marks, row_marks = [None], [None, None]
                o_marks = []
                v_block, k_block = [None], [None]
                later = []
                item = [0]

                def put(lag, what):
                    later.append((item[0] + lag, what))

                def next_item(what):
                    what()
                    item[0] += 1
                    flush(item[0])

                def flush(upto):
                    due = sorted((x for x in later if x[0] <= upto), key=lambda x: x[0])
                    later[:] = [x for x in later if x[0] > upto]
                    for _, what in due:
                        what()

                def q_projection(g):
                    n = use(unit_x(att, "q", g))
                    q_marks.clear()
                    old = list(o_marks)
                    o_marks.clear()

                    def out_q(co, src, mark, g=g):
                        b = col(A + "bq", HG * g + co)
                        hi = SC.step(lambda e: e.activation(q_pair[0][:, co, :], src, ACT.Identity, bias=b), mark, old)
                        lo = DVE.step(lambda e: e.scalar_tensor_tensor(
                            q_pair[1][:, co, :], src, b, q_pair[0][:, co, :].bitcast(F32), ALU.add, ALU.subtract), hi)
                        q_marks.extend([hi, lo])
                        return [hi, lo]

                    linear(n, h_pair, h_ready, out_q, [0, 1, 2])

                def bias_slots(g):
                    kb = vec[:, COL[A + "bias_k"] + HG * g:COL[A + "bias_k"] + HG * (g + 1)]
                    hi = SC.step(lambda e: e.activation(k_pair[0][:, :, S], kb, ACT.Copy), k_free)
                    lo = DVE.step(minus(k_pair[1][:, :, S], kb, k_pair[0][:, :, S]), hi, k_free)
                    col_marks[0] = [hi, lo]

                def bias_rows(g):
                    m = row_dma.load(SY, row_raw[0:1, :, :], rows[att, g], DVE.now(), SC.now(), PE.now())
                    d = DVE.step(lambda e: e.tensor_tensor(row_raw[0:1, 0, :], row_raw[0:1, 0, :], row_raw[0:1, 1, :],
                                                           ALU.subtract), m)
                    hi = SC.step(lambda e: e.activation(row_pair[:, 0, :], row_raw[0:1, 0, :], ACT.Copy), d, row_marks)
                    lo = DVE.step(minus(row_pair[:, 1, :], row_raw[0:1, 0, :], row_pair[:, 0, :]), hi)
                    return [hi, lo]

                def move_row(i, ready):
                    for part in range(2):
                        row_marks[i] = vrow_dma[i].load(
                            SY, v_pairs[i][part][BIAS_P:BIAS_P + 1, 2, :].bitcast(F32), row_pair[:, part, :].bitcast(F32),
                            ready, v_free[i])

                def value_tile(bb, c, last):
                    i = bb % 2
                    t0, n = CH[c]
                    bank = turn[1] % 3
                    turn[1] += 1
                    blk = v_block[0]
                    s = order[blk][1]
                    terms = []
                    for ct in range(CT):
                        terms += three((ctx_pair[0][:, bb, ct, t0:t0 + n], ctx_pair[1][:, bb, ct, t0:t0 + n]),
                                       (w_hi[s][:, ct, :], w_lo[s][:, ct, :]))
                    m = products(ps[0:n, bank, :], terms, ready_of[blk], ctx_ready, bank_free[bank])
                    if last:
                        done(blk, m)
                    n = min(n, S - t0)
                    hi = SC.step(lambda e: e.activation(v_pairs[i][0][0:n, c, :], ps[0:n, bank, :], ACT.Copy), m, v_free[i])
                    lo = DVE.step(minus(v_pairs[i][1][0:n, c, :], ps[0:n, bank, :], v_pairs[i][0][0:n, c, :]), hi, v_free[i])
                    bank_free[bank] = [hi, lo]
                    v_marks[i] = [hi, lo]

                def key_tile(bb, h, g, last):
                    bank = turn[1] % 3
                    turn[1] += 1
                    blk = k_block[0]
                    s = order[blk][1]
                    terms = []
                    for ct in range(CT):
                        terms += three((w_hi[s][:, ct, h * XK:(h + 1) * XK], w_lo[s][:, ct, h * XK:(h + 1) * XK]),
                                       (ctx_pair[0][:, bb, ct, :], ctx_pair[1][:, bb, ct, :]))
                    m = products(ps[:, bank, 0:SP], terms, ready_of[blk], ctx_ready, bank_free[bank])
                    if last:
                        done(blk, m)
                    b = col(A + "bk", HG * g + h)
                    hi = SC.step(lambda e: e.activation(k_pair[0][:, h, 0:S], ps[:, bank, 0:S], ACT.Identity, bias=b),
                                 m, k_free[h])
                    lo = DVE.step(lambda e: e.scalar_tensor_tensor(
                        k_pair[1][:, h, 0:S], ps[:, bank, 0:S], b, k_pair[0][:, h, 0:S].bitcast(F32),
                        ALU.add, ALU.subtract), hi, k_free[h])
                    bank_free[bank] = [hi, lo]
                    k_marks[h] = [hi, lo]
                    put(2, lambda: scores(bb, h, g))

                def scores(bb, h, g):
                    t = turn[0]
                    turn[0] += 1
                    bank, pr, st = 3 + t % 2, probs[t % 3], soft[0:L, 4 * (t % 4):4 * (t % 4) + 4]
                    cols_b = slice(bb * L, (bb + 1) * L)
                    m = products(ps[0:L, bank, 0:SP],
                                 three((q_pair[0][:, h, cols_b], q_pair[1][:, h, cols_b]),
                                       (k_pair[0][:, h, :], k_pair[1][:, h, :])),
                                 q_marks, k_marks[h], col_marks[0], bank_free[bank])
                    k_free[h] = m
                    src = ps[0:L, bank, 0:SP]
                    m = DVE.step(lambda e: e.tensor_reduce(st[:, 0:1], src, AXX, ALU.max), m)
                    m = DVE.step(lambda e: e.tensor_scalar(st[:, 1:2], st[:, 0:1], -SCALE, None, ALU.mult), m)
                    m = SC.step(lambda e: e.activation(pr, src, ACT.Exp, bias=st[:, 1:2], scale=SCALE,
                                                       accum_out=st[:, 2:3]), m, p_free[t % 3])
                    bank_free[bank] = m
                    m = DVE.step(lambda e: e.reciprocal(st[:, 3:4], st[:, 2:3]), m)
                    m = DVE.step(lambda e: e.tensor_scalar(pr, pr, st[:, 3:4], None, ALU.mult), m)
                    put(1, lambda: turn_probs(bb, h, g, t, m))

                def turn_probs(bb, h, g, t, ready):
                    bank, pt = 5 + t % 2, pt_pairs[t % 2]
                    PE.wait(ready, bank_free[bank])
                    for c, (t0, n) in enumerate(CH):
                        m = PE.step(lambda e, c=c, t0=t0, n=n: e.transpose(
                            ps[0:n, bank, c * L:(c + 1) * L], probs[t % 3][:, t0:t0 + n], ident[0:L, 0:L]))
                    p_free[t % 3] = m
                    marks = []
                    parts = [(pt[0][0:n, c0:c1, :], pt[1][0:n, c0:c1, :],
                              ps[0:n, bank, c0 * L:c1 * L].rearrange("p (c q) -> p c q", q=L))
                             for c0, c1, n in ((0, 2, P), (2, 3, CH[2][1]))]
                    for hi, _, src in parts:
                        m = SC.step(lambda e, d=hi, s=src: e.activation(d, s, ACT.Copy), m, pt_free[t % 2])
                    marks = [m]
                    for hi, lo, src in parts:
                        marks.append(DVE.step(minus(lo, src, hi), m, pt_free[t % 2]))
                    bank_free[bank] = marks
                    put(1, lambda: weigh(bb, h, g, t, marks))

                def weigh(bb, h, g, t, ready):
                    pt, v = pt_pairs[t % 2], v_pairs[bb % 2]
                    terms = []
                    for c, (_, n) in enumerate(CH):
                        terms += three((v[0][0:n, c, h * XK:(h + 1) * XK], v[1][0:n, c, h * XK:(h + 1) * XK]),
                                       (pt[0][0:n, c, :], pt[1][0:n, c, :]))
                    m = products(ps[:, 7, h * L:(h + 1) * L], terms, ready, v_marks[bb % 2], row_marks[bb % 2],
                                 bank_free[7] if h == 0 else None)
                    pt_free[t % 2] = m
                    if h == HG - 1:
                        v_free[bb % 2] = m
                        bv = vec[:, COL[A + "bv"] + HG * g:COL[A + "bv"] + HG * (g + 1)].unsqueeze(2).broadcast_to([P, HG, L])
                        r = DVE.step(lambda e: e.tensor_tensor(
                            o_raw, ps[:, 7, 0:HG * L].rearrange("p (h q) -> p h q", h=HG), bv, ALU.add), m, GP.now())
                        bank_free[7] = r
                        dst = [q_pair[i][:, :, bb * L:(bb + 1) * L] for i in range(2)]
                        hi = SC.step(lambda e: e.activation(dst[0], o_raw, ACT.Copy), r)
                        lo = GP.step(minus(dst[1], o_raw, dst[0]), hi)
                        o_marks.extend([hi, lo])

                def out_projection(g):
                    marks = []

                    def add_x(co, src, mark):
                        if g == 0:
                            m = DVE.step(lambda e: e.scalar_tensor_tensor(
                                xh[:, co, :], src, col(A + "bo", co), xh[:, co, :], ALU.add, ALU.add), mark)
                        else:
                            m = DVE.step(lambda e: e.tensor_tensor(xh[:, co, :], xh[:, co, :], src, ALU.add), mark)
                        marks.append(m)
                        return m

                    m = linear(use(unit_x(att, "o", g)), q_pair, o_marks, add_x, [0, 1, 2])
                    o_marks[:] = [m]
                    return marks

                q_projection(0)
                for g in range(NG):
                    for bb in range(HB):
                        if bb == 0:
                            v_block[0] = use(unit_x(att, "v", g))
                            rows_ready = bias_rows(g)
                            move_row(0, rows_ready)
                        for c in range(3):
                            next_item(lambda: value_tile(bb, c, bb == HB - 1 and c == 2))
                        if bb == 0:
                            if g:
                                flush(item[0] + 9)
                                x_marks = out_projection(g - 1)
                                q_projection(g)
                            move_row(1, rows_ready)
                            bias_slots(g)
                            k_block[0] = use(unit_x(att, "k", g))
                        for h in range(HG):
                            next_item(lambda: key_tile(bb, h, g, bb == HB - 1 and h == HG - 1))
                for _ in range(4):
                    item[0] += 1
                    flush(item[0])
                return out_projection(NG - 1)

            def mlp_group(hf, g, h_ready, m):
                xh = x[:, :, hf, :]
                g_marks = []
                prior = [m, PE.now()]

                def out_g(co, src, mark):
                    a = SC.step(lambda e: e.activation(cen[:, co, :], src, ACT.Gelu, bias=col("M_b1", CT * g + co)),
                                mark, prior)
                    hi = SC.step(lambda e: e.activation(q_pair[0][:, co, :], cen[:, co, :], ACT.Copy), a, prior)
                    lo = DVE.step(minus(q_pair[1][:, co, :], cen[:, co, :], q_pair[0][:, co, :]), hi, prior)
                    g_marks.extend([hi, lo])
                    return a

                linear(use(unit_m(0, g)), h_pair, h_ready, out_g, [0, 1, 2, 3])
                x_marks = []

                def add_mlp(co, src, mark):
                    if g == 0:
                        m = DVE.step(lambda e: e.scalar_tensor_tensor(
                            xh[:, co, :], src, col("M_b2", co), xh[:, co, :], ALU.add, ALU.add), mark)
                    else:
                        m = DVE.step(lambda e: e.tensor_tensor(xh[:, co, :], xh[:, co, :], src, ALU.add), mark)
                    x_marks.append(m)
                    return m

                m = [linear(use(unit_m(1, g)), q_pair, g_marks, add_mlp, [4, 5, 6, 7]), g_marks]
                return m, x_marks

            for hf in range(NH):
                ctx_ready = load_context(hf)
                x_marks = x_ready[hf]
                for att in (0, 1):
                    x_marks = attention(hf, att, ctx_ready, x_marks)
                h_ready = norm_to_pair(hf, "M", x_marks)
                m = h_ready
                for g in range(NG):
                    m, x_marks = mlp_group(hf, g, h_ready, m)
                stored = out_dma.load(SY, out[:, :, hf, :], x[:, :, hf, :], x_marks)
            SY.wait(stored)

            with nc.Block() as block:
                @block.sync
                def _(e):
                    SY.play(e)

                @block.tensor
                def _(e):
                    PE.play(e)

                @block.vector
                def _(e):
                    DVE.play(e)

                @block.scalar
                def _(e):
                    SC.play(e)

                @block.gpsimd
                def _(e):
                    GP.play(e)


def kernel(**inputs):
    import concourse.bacc as bacc
    from concourse.bass_utils import run_bass_kernel_spmd

    get = {k: np.asarray(v) for k, v in inputs.items()}

    def tiles(w):
        return w.reshape(CT, P, w.shape[-1]).transpose(1, 0, 2)

    def column(v):
        return v.reshape(-1, P).T

    xT = tiles(get["x"].reshape(B * L, D).T).reshape(P, CT, NH, HN)
    c = get["ctx_2048"]
    ctxT = np.zeros((B, P, CT, SP), np.float32)
    ctxT[:, :, :, 0:S] = c.transpose(0, 2, 1).reshape(B, CT, P, S).transpose(0, 2, 1, 3)
    ctx_tok = np.zeros((B, 3 * P, D), np.float32)
    ctx_tok[:, 0:S] = c
    ctx_tok = ctx_tok.reshape(B, 3, P, D).transpose(0, 2, 1, 3)
    s0 = c[:, 2:2 + HS].reshape(B, CT, P // HS, HS, HS).transpose(2, 3, 1, 4, 0).reshape(P, CT, HS, B)
    shift = c[:, 0:2].reshape(B, 2, CT, P).transpose(3, 2, 1, 0)

    blocks = [get["L0_xattn_w_q"].T, get["L0_xattn_w_k"], get["L0_xattn_w_v"].T, get["L0_xattn_w_o"].T]
    r_names = [
        dict(k="Wk", v="Wv", r="Wr", g="Wg", o="Wo", fr="fWr", fk="fWk", fv="fWv", mix1="maa_w1", mix2="maa_w2",
             dec1="decay_w1", dec2="decay_w2", decay="time_decay", u="faaaa", fmaa_k="fmaa_k", fmaa_r="fmaa_r"),
        dict(k="Wk", v="Wv", r="Wr", g="Wg", o="Wo", fr="Wfr", fk="Wfk", fv="Wfv", mix1="maa_w1", mix2="maa_w2",
             dec1="td_w1", dec2="td_w2", decay="time_decay", u="u", fmaa_k="ffn_maa_k", fmaa_r="ffn_maa_r"),
    ]
    vectors, mix1, mix2, dec1, dec2 = [], [], [], [], []
    for layer, names in enumerate(r_names):
        pre = f"L{layer + 1}_xattn_"
        blocks += [get[pre + names[n]].T for n in R_ORDER]
        mix1.append(tiles(get[pre + names["mix1"]]))
        mix2.append(get[pre + names["mix2"]].reshape(5 * DM, D))
        dec1.append(tiles(get[pre + names["dec1"]]))
        dec2.append(get[pre + names["dec2"]])
        for v in R_VECS:
            if layer == 1 and v[:4] == "maa_" and v != "maa_x":
                vectors.append(column(get[pre + "maa_stack"][0, "kwvrg".index(v[4])]))
            else:
                vectors.append(column(get[pre + names.get(v, v)].reshape(D)))
    rows = []
    for att in (0, 1):
        n = str(att + 1)
        X = lambda name: get["L3_xattn_" + name + n]
        for g in range(NG):
            s = slice(g * D, (g + 1) * D)
            blocks += [X("wq")[:, s], X("wk")[:, s], X("wv")[:, s], X("wo")[s]]
        vectors += [column(get[f"L3_xattn_ln{n}_scale"]), column(get[f"L3_xattn_ln{n}_offset"])]
        vectors += [column(X("bq")), column(X("bk")), column(X("bv")), column(X("bias_k").reshape(-1)), column(X("bo"))]
        rows.append(np.stack([X("bias_v").reshape(NG, D), X("bv").reshape(NG, D)], 1)[:, None])
    w1, w2 = get["L3_xattn_w_fc1"], get["L3_xattn_w_fc2"]
    blocks += [w1[:, g * D:(g + 1) * D] for g in range(NG)] + [w2[g * D:(g + 1) * D] for g in range(NG)]
    vectors += [column(get["L3_xattn_ln_mlp_scale"]), column(get["L3_xattn_ln_mlp_offset"])]
    vectors += [column(get["L3_xattn_b_fc1"]), column(get["L3_xattn_b_fc2"])]
    vectors += [np.broadcast_to(get["L0_xattn_alpha"].reshape(1, 1), (P, 1)), np.full((P, 1), EPS, np.float32)]
    weights = np.stack([tiles(b).reshape(P, UNIT) for b in blocks])

    head = np.arange(P) // HS
    same = (head[:, None] == head[None, :]).astype(np.float32)
    collect = np.zeros((P, P + HS - 1), np.float32)
    collect[np.arange(P), HS * head + HS - 1] = 1.0
    pick = np.zeros((P, HS, P), np.float32)
    for j in range(HS):
        pick[HS * head + j, j, np.arange(P)] = 1.0
    consts = np.concatenate([np.eye(P, dtype=np.float32), np.full((P, P), 1.0 / D, np.float32), same,
                             same / np.float32(HS), np.eye(P, dtype=np.float32) - same / np.float32(HS), collect, pick.reshape(P, -1)], 1)

    arrays = {"xT": xT, "ctxT": ctxT, "ctx_tok": ctx_tok, "s0": s0, "shift": shift, "weights": weights,
              "mix1": np.stack(mix1), "mix2": np.stack(mix2), "dec1": np.stack(dec1), "dec2": np.stack(dec2),
              "cols": np.concatenate(vectors, 1), "rows": np.stack(rows), "consts": consts}
    arrays = {k: np.ascontiguousarray(v) for k, v in arrays.items()}
    nc = bacc.Bacc("TRN2", target_bir_lowering=False, num_devices=1)
    args = [nc.dram_tensor(k, v.shape, F32, kind="ExternalInput").ap() for k, v in arrays.items()]
    out = nc.dram_tensor("result", (P, CT, NH, HN), F32, kind="ExternalOutput").ap()
    build(nc, *args, out)
    got = run_bass_kernel_spmd(nc, [arrays], core_ids=[0]).results[0]["result"]
    return got.transpose(2, 3, 1, 0).reshape(B, L, D)
```

```python
from contextlib import ExitStack

import numpy as np
import concourse.bass as bass
from concourse import mybir

F32 = mybir.dt.float32
F32R = mybir.dt.float32r
ACT = mybir.ActivationFunctionType
ALU = mybir.AluOpType
AXX = mybir.AxisListType.X

P = 128
B, L, D = 8, 112, 512
S = 375
SP = S + 1
CT = D // P
NH = 2
HB = B // NH
HN = HB * L
T = CT * HN
HS = 16
GJ = 4
DM, DD = 32, 64
XH, XK = 16, 128
HG = 4
NG = XH // HG
F = 2048
CH = [(0, 128), (128, 128), (256, 120)]
UNIT = CT * D
EPS = 1e-5

U_L0 = {n: i for i, n in enumerate(["q", "k", "v", "o"])}
R_ORDER = ["k", "v", "r", "g", "o", "fk", "fr", "fv"]


def unit_r(layer, name):
    return 4 + 8 * layer + R_ORDER.index(name)


def unit_x(att, name, g):
    return 20 + 16 * att + 4 * g + ["q", "k", "v", "o"].index(name)


def unit_m(which, g):
    return 52 + 4 * which + g


N_UNITS = 60

R_VECS = ["ln1_w", "ln1_b", "ln2_w", "ln2_b", "maa_x", "maa_w", "maa_k", "maa_v", "maa_r", "maa_g",
          "decay", "u", "gn_w", "gn_b", "fmaa_k", "fmaa_r"]


def vector_columns():
    col, n = {}, 0
    for layer in (0, 1):
        for v in R_VECS:
            col[f"R{layer}_{v}"] = n
            n += CT
    for att in (0, 1):
        for v, w in (("ln_w", CT), ("ln_b", CT), ("bq", XH), ("bk", XH), ("bv", XH), ("bias_k", XH), ("bo", CT)):
            col[f"X{att}_{v}"] = n
            n += w
    for v, w in (("ln_w", CT), ("ln_b", CT), ("b1", F // P), ("b2", CT), ("alpha", 1), ("eps", 1)):
        col[f"M_{v}"] = n
        n += w
    return col, n


COL, NCOL = vector_columns()


class Queue:

    def __init__(self, sem):
        self.sem, self.count, self.todo, self.waited = sem, 0, [], {}
        self.data = 0

    def wait(self, *marks):
        for m in marks:
            if m is None:
                continue
            if isinstance(m, list):
                self.wait(*m)
                continue
            sem, value = m
            if self.waited.get(id(sem), 0) < value:
                self.waited[id(sem)] = value
                self.todo.append(lambda e, s=sem, v=value: e.wait_ge(s, v))

    def run(self, instruction, *after):
        self.wait(*after)
        self.todo.append(instruction)

    def step(self, instruction, *after):
        self.wait(*after)
        self.count += 1
        self.data = self.count
        self.todo.append(lambda e, f=instruction: f(e).then_inc(self.sem, 1))
        return (self.sem, self.count)

    def now(self):
        return (self.sem, self.data) if self.data else None

    def play(self, engine):
        for f in self.todo:
            f(engine)


class Loads:

    def __init__(self, sem):
        self.sem, self.count = sem, 0

    def load(self, queue, dst, src, *after):
        queue.wait(*after)
        self.count += 16
        queue.todo.append(lambda e: e.dma_start(dst, src).then_inc(self.sem, 16))
        return (self.sem, self.count)


def build(nc, xT, ctxT, ctx_tok, s0, shift, weights, mix1, mix2, dec1, dec2, cols, rows, consts, out):
    with ExitStack() as ctx:
        def sb(stack, name, shape, dt=F32):
            return stack.enter_context(nc.sbuf_tensor(name, shape, dt))

        def sem(name):
            return ctx.enter_context(nc.semaphore(name))

        PE, DVE, SC, GP, SY = (Queue(sem(n)) for n in ("pe_done", "dve_done", "act_done", "pool_done", "sp_done"))

        x = sb(ctx, "x", [P, CT, NH, HN])
        vec = sb(ctx, "vec", [P, NCOL])
        ident = sb(ctx, "ident", [P, P])
        ones = sb(ctx, "ones", [P, P])
        raw = sb(ctx, "raw", [P, UNIT])
        NW = 3
        w_hi = [sb(ctx, f"w_hi{i}", [P, CT, D], F32R) for i in range(NW)]
        w_lo = [sb(ctx, f"w_lo{i}", [P, CT, D], F32R) for i in range(NW)]
        std = sb(ctx, "std", [P, HN])
        ps = ctx.enter_context(nc.psum_tensor("ps", [P, 8, 512], F32))

        bank_free = [None] * 8
        std_read = [None]

        order = []

        def enter(unit, slot):
            order.append((unit, slot))
            return slot

        for unit in ([U_L0[n] for n in ("q", "k", "v", "o")] * NH
                     + [unit_r(layer, n) for layer in (0, 1) for _ in range(NH) for n in R_ORDER]):
            enter(unit, len(order) % NW)
        groups = [(hf, att, g) for hf in range(NH) for att in (0, 1) for g in range(NG)]
        spare = [(len(order) + k - 2 * NG) % NW for k in range(NW)]
        for i, (hf, att, g) in enumerate(groups):
            if att == 0 and g == 0:
                sv, sk, third = [spare[(2 * NG + k) % NW] for k in range(NW)]
                enter(unit_x(att, "v", g), sv), enter(unit_x(att, "k", g), sk), enter(unit_x(att, "q", g), third)
            if i + 1 < len(groups) and groups[i + 1][0] == hf:
                _, att1, g1 = groups[i + 1]
                enter(unit_x(att1, "v", g1), third), enter(unit_x(att1, "k", g1), sv)
                enter(unit_x(att, "o", g), sk), enter(unit_x(att1, "q", g1), sk)
                sv, sk, third = third, sv, sk
            else:
                enter(unit_x(att, "o", g), third)
                spare = [sv, sk, third]
                for m in range(2 * NG):
                    enter(unit_m(m % 2, m // 2), spare[m % NW])
        raw_dma = Loads(sem("raw_loaded"))
        raw_mark, raw_free = [None], [None]
        ready_of = [None] * len(order)
        slot_free = [None] * NW
        slot_busy = [False] * NW
        fetched, used = [0], [0]

        def load_raw(n):
            if n < len(order):
                raw_mark[0] = raw_dma.load(SY, raw[:, :], weights[order[n][0], :, :], raw_free[0])

        def fetch(upto=len(order)):
            while fetched[0] < upto and not slot_busy[order[fetched[0]][1]]:
                n = fetched[0]
                i = order[n][1]
                fetched[0] += 1
                slot_busy[i] = True
                flat_hi = w_hi[i][:, :, :].rearrange("p a b -> p (a b)")
                flat_lo = w_lo[i][:, :, :].rearrange("p a b -> p (a b)")
                free = [raw_mark[0], slot_free[i]]
                marks, data = [], [(q, q.data) for q in (SC, GP, DVE)]
                cuts = [(GP, 0, UNIT)] if unit_r(0, "k") <= order[n][0] < unit_m(0, 0) else [(GP, 0, UNIT // 2), (DVE, UNIT // 2, UNIT)]
                for engine, c0, c1 in cuts:
                    hi = SC.step(lambda e, d=flat_hi[:, c0:c1], s=raw[:, c0:c1]: e.activation(d, s, ACT.Copy), free)
                    lo = engine.step(lambda e, d=flat_lo[:, c0:c1], s=raw[:, c0:c1], h=flat_hi[:, c0:c1]: e.tensor_tensor(
                        d, s, h.bitcast(F32), ALU.subtract), free, hi)
                    marks += [hi, lo]
                for q, mark in data:
                    q.data = mark
                ready_of[n] = marks
                raw_free[0] = marks
                load_raw(n + 1)

        def use(unit):
            n = used[0]
            fetch(n + 1)
            used[0] += 1
            assert order[n][0] == unit and n < fetched[0], (n, unit, order[n])
            return n

        def done(n, mark):
            i = order[n][1]
            slot_free[i], slot_busy[i] = mark, False
            fetch()

        def products(dst, terms, *after, each=None):
            PE.wait(*after)
            for i, (lhsT, rhs) in enumerate(terms[:-1]):
                if each:
                    PE.wait(each[i])
                PE.run(lambda e, a=lhsT, b=rhs, s=(i == 0): e.matmul(dst, a, b, start=s, stop=False))
            if each:
                PE.wait(each[-1])
            a, b = terms[-1]
            return PE.step(lambda e: e.matmul(dst, a, b, start=(len(terms) == 1), stop=True))

        def three(a, b):
            return [(a[0], b[0]), (a[0], b[1]), (a[1], b[0])]

        def linear(n, pair, ready, evacuate, banks, then=lambda co: None):
            i = order[n][1]
            mark = None
            for co in range(CT):
                bank = banks[co % len(banks)]
                terms = []
                for ct in range(CT):
                    w = (w_hi[i][:, ct, co * P:(co + 1) * P], w_lo[i][:, ct, co * P:(co + 1) * P])
                    m = (pair[0][:, ct, :], pair[1][:, ct, :])
                    terms += three(w, m)
                mark = products(ps[:, bank, 0:HN], terms, ready_of[n], ready, bank_free[bank])
                bank_free[bank] = evacuate(co, ps[:, bank, 0:HN], mark)
                if co == CT - 1:
                    done(n, mark)
                then(co)
            return mark

        def linear_by_input(n, pair, ready, evacuate, banks, then=lambda co: None):
            i = order[n][1]
            marks = [None] * CT
            PE.wait(ready_of[n], [bank_free[b] for b in banks])
            for ct in range(CT):
                PE.wait(ready[ct])
                for co in range(CT):
                    dst = ps[:, banks[co], 0:HN]
                    w = (w_hi[i][:, ct, co * P:(co + 1) * P], w_lo[i][:, ct, co * P:(co + 1) * P])
                    terms = three(w, (pair[0][:, ct, :], pair[1][:, ct, :]))
                    for t, (a, b) in enumerate(terms):
                        first, last = ct == 0 and t == 0, ct == CT - 1 and t == 2
                        what = lambda e, d=dst, a=a, b=b, f=first, l=last: e.matmul(d, a, b, start=f, stop=l)
                        if last:
                            marks[co] = PE.step(what)
                        else:
                            PE.run(what)
            for co in range(CT):
                bank_free[banks[co]] = evacuate(co, ps[:, banks[co], 0:HN], marks[co])
            done(n, marks[-1])
            for co in range(CT):
                then(co)
            return marks[-1]

        def split_tile(pair, ct, src, ready, free):
            hi = SC.step(lambda e: e.activation(pair[0][:, ct, :], src, ACT.Copy), ready, free)
            lo = DVE.step(lambda e: e.tensor_tensor(pair[1][:, ct, :], src, pair[0][:, ct, :].bitcast(F32),
                                                    ALU.subtract), hi, ready, free)
            return [hi, lo]

        def split(pair, src, ready, free):
            hi = SC.step(lambda e: e.activation(pair[0][:, :, :], src, ACT.Copy), ready, free)
            lo = DVE.step(lambda e: e.tensor_tensor(pair[1][:, :, :], src, pair[0][:, :, :].bitcast(F32), ALU.subtract),
                          hi, ready, free)
            return [hi, lo]

        def col(name, i=0):
            c = COL[name] + i
            return vec[:, c:c + 1]

        def norm_parts(src, cen, sq, ready, prior, b0, b1, emit):
            m = products(ps[:, b0, 0:HN], [(ones[:, :], src[:, ct, :]) for ct in range(CT)], bank_free[b0],
                         each=ready)
            c = [DVE.step(lambda e, ct=ct: e.tensor_tensor(cen[:, ct, :], src[:, ct, :], ps[:, b0, 0:HN],
                                                           ALU.subtract), m, ready, prior) for ct in range(CT)]
            bank_free[b0] = c[-1]
            v, n = [None] * CT, len(sq)
            for first in range(0, CT, n):
                squared = [SC.step(lambda e, ct=ct: e.activation(sq[ct % n], cen[:, ct, :], ACT.Square), c[ct],
                                   prior, v[ct - n] if ct >= n else None) for ct in range(first, first + n)]
                yield
                PE.wait(bank_free[b1])
                for ct in range(first, first + n):
                    PE.wait(squared[ct - first])
                    v[ct] = PE.step(lambda e, ct=ct: e.matmul(ps[:, b1, 0:HN], ones[:, :], sq[ct % n],
                                                              start=(ct == 0), stop=(ct == CT - 1)))
            r = SC.step(lambda e: e.activation(std[:, :], ps[:, b1, 0:HN], ACT.Sqrt, bias=col("M_eps")), v[-1],
                        prior, std_read[0])
            bank_free[b1] = r
            r = DVE.step(lambda e: e.reciprocal(std[:, :], std[:, :]), r)
            for ct in range(CT):
                std_read[0] = DVE.step(lambda e, ct=ct: e.tensor_tensor(cen[:, ct, :], cen[:, ct, :], std[:, :],
                                                                        ALU.mult), r)
                emit(ct, std_read[0])

        def finish_parts(parts):
            for _ in parts:
                pass

        def barrier():
            marks = [q.now() for q in (PE, DVE, SC, GP)]
            for q in (PE, DVE, SC, GP, SY):
                q.wait(*marks)

        start = Loads(sem("start_loaded"))
        load_raw(0)
        first = start.load(SY, x[:, :, 0, :], xT[:, :, 0, :])
        first = start.load(SY, vec[:, :], cols)
        first = start.load(SY, ident[:, :], consts[:, 0:P])
        first = start.load(SY, ones[:, :], consts[:, P:2 * P])
        for q in (PE, DVE, SC, GP):
            q.wait(first)
        fetch(1)
        second = Loads(sem("second_half_loaded"))
        x_ready = [[None] * CT, None]

        with ExitStack() as early:
            def act(name, dt=F32):
                return sb(early, name, [P, CT, HN], dt)

            xa = sb(early, "xa", [P, CT, HB, L + 1])
            sx = act("sx")
            tmp_a, tmp_b = act("tmp_a"), act("tmp_b")
            pairs = [(act("p0_hi", F32R), act("p0_lo", F32R)), (act("p1_hi", F32R), act("p1_lo", F32R))]
            r_, k_, v_, w_ = act("r"), act("k"), act("v"), act("w")
            ring = [sb(early, f"ring{i}", [P, GJ, HN]) for i in range(3)]
            block16 = sb(early, "block16", [P, P])
            mean16 = sb(early, "mean16", [P, P])
            centre16 = sb(early, "centre16", [P, P])
            collect = sb(early, "collect", [P, P + HS - 1])
            pick = sb(early, "pick", [P, HS, P], F32R)
            mix1_w = sb(early, "mix1_w", [P, CT, 5 * DM])
            mix2_a = sb(early, "mix2_a", [P, D])
            mix2_b = sb(early, "mix2_b", [DM, D])
            dec1_w = sb(early, "dec1_w", [P, CT, DD])
            dec2_w = sb(early, "dec2_w", [DD, D])
            s0_t = sb(early, "s0_t", [P, CT, HS, B])
            shift_t = sb(early, "shift_t", [P, CT, 2, B])
            soft = sb(early, "soft", [P, 8])

            ctx_dma = [Loads(sem(f"ctx_loaded{i}")) for i in range(3)]
            ctx_buf = [(ring[0], ring[1]), (ring[2], k_), (r_, w_)]
            ctx_free = [None] * 3
            prob = [v_[:, i, :] for i in range(2)]
            probT = [v_[:, 2 + i, 0:3 * L].rearrange("p (c q) -> p c q", c=3) for i in range(2)]
            p_free, pt_free = [None] * 2, [None] * 2

            def cross_attention_0(hf):
                xh = x[:, :, hf, :]
                ctx_views, ctx_mark = [], []

                def load_ctx(b):
                    i = b % HB % 3
                    keyT = ctx_buf[i][0][:, :, :].rearrange("p a b -> p (a b)")[:, 0:CT * SP].rearrange(
                        "p (a b) -> p a b", a=CT)
                    tok = ctx_buf[i][1][:, :, :].rearrange("p a b -> p (a b)")[:, 0:3 * D].rearrange(
                        "p (a b) -> p a b", a=3)
                    ctx_dma[i].load(SY, keyT, ctxT[b], ctx_free[i])
                    ctx_mark.append(ctx_dma[i].load(SY, tok, ctx_tok[b]))
                    ctx_views.append((keyT, tok))

                ready = split(pairs[0], xh, x_ready[hf], PE.now())
                fetch(2)
                for bb in range(3):
                    load_ctx(hf * HB + bb)
                if hf == 0:
                    x_ready[1] = [second.load(SY, x[:, :, 1, :], xT[:, :, 1, :])] * CT

                def q_out(co, src, mark):
                    hi = SC.step(lambda e: e.activation(pairs[1][0][:, co, :], src, ACT.Copy), mark)
                    lo = DVE.step(lambda e: e.tensor_tensor(pairs[1][1][:, co, :], src,
                                                            pairs[1][0][:, co, :].bitcast(F32), ALU.subtract), hi)
                    q_marks.extend([hi, lo])
                    return [hi, lo]

                q_marks = []
                linear(use(U_L0["q"]), pairs[0], ready, q_out, [0, 1, 2, 3])
                g_marks = []

                def g_out(co, src, mark):
                    g_marks.append(SC.step(lambda e: e.activation(tmp_a[:, co, :], src, ACT.Copy), mark, PE.now()))
                    return g_marks[-1]

                linear(use(U_L0["k"]), pairs[1], q_marks, g_out, [4, 5, 6, 7])
                c_marks = []
                scale = float(D) ** -0.5

                def score(bb):
                    keyT, _ = ctx_views[bb]
                    i = bb % 2
                    sc, st, pr = ps[0:L, i, 0:SP], soft[0:L, 4 * i:4 * i + 4], prob[i]
                    m = products(sc, [(tmp_a[:, ct, bb * L:(bb + 1) * L], keyT[:, ct, :]) for ct in range(CT)],
                                 g_marks, ctx_mark[bb], bank_free[i])
                    m = DVE.step(lambda e: e.tensor_reduce(st[:, 0:1], sc[:, 0:S], AXX, ALU.max), m, p_free[i])
                    m = DVE.step(lambda e: e.tensor_scalar(st[:, 1:2], st[:, 0:1], -scale, None, ALU.mult), m)
                    m = SC.step(lambda e: e.activation(pr[0:L, 0:S], sc[:, 0:S], ACT.Exp, bias=st[:, 1:2],
                                                       scale=scale, accum_out=st[:, 2:3]), m, p_free[i])
                    bank_free[i] = m
                    m = DVE.step(lambda e: e.reciprocal(st[:, 3:4], st[:, 2:3]), m)
                    return DVE.step(lambda e: e.tensor_scalar(pr[0:L, 0:S], pr[0:L, 0:S], st[:, 3:4], None, ALU.mult), m)

                def turn(bb, ready):
                    i = bb % 2
                    pr, pt = prob[i], probT[i]
                    PE.wait(ready, bank_free[2 + i])
                    for c, (t0, n) in enumerate(CH):
                        n = min(n, S - t0)
                        m = PE.step(lambda e, c=c, t0=t0, n=n: e.transpose(
                            ps[0:n, 2 + i, c * L:(c + 1) * L], pr[0:L, t0:t0 + n], ident[0:L, 0:L]))
                    p_free[i] = m
                    a = SC.step(lambda e: e.activation(
                        pt[:, 0:2, :], ps[:, 2 + i, 0:2 * L].rearrange("p (c q) -> p c q", c=2), ACT.Copy), m, pt_free[i])
                    a = SC.step(lambda e: e.activation(
                        pt[0:S - 2 * P, 2, :], ps[0:S - 2 * P, 2 + i, 2 * L:3 * L], ACT.Copy), m, pt_free[i])
                    bank_free[2 + i] = a
                    return a

                def weigh(bb, ready):
                    i = bb % 2
                    tok, pt, dst = ctx_views[bb][1], probT[i], tmp_b[:, :, bb * L:(bb + 1) * L]
                    PE.wait(ready, bank_free[4 + i])
                    for dt in range(CT):
                        m = products(ps[:, 4 + i, dt * L:(dt + 1) * L],
                                     [(tok[0:min(n, S - t0), c, dt * P:(dt + 1) * P], pt[0:min(n, S - t0), c, :])
                                      for c, (t0, n) in enumerate(CH)])
                    ctx_free[bb % 3] = pt_free[i] = m
                    m = DVE.step(lambda e: e.tensor_copy(
                        dst, ps[:, 4 + i, 0:CT * L].rearrange("p (c q) -> p c q", c=CT)), m)
                    bank_free[4 + i] = m
                    c_marks.append(m)
                    if bb + 3 < HB:
                        load_ctx(hf * HB + bb + 3)

                scored, turned = {}, {}
                for step in range(HB + 2):
                    if step < HB:
                        scored[step] = score(step)
                    if 1 <= step <= HB:
                        turned[step - 1] = turn(step - 1, scored[step - 1])
                    if step == 1 or step == 0:
                        continue
                    weigh(step - 2, turned[step - 2])
                ready = split(pairs[0], tmp_b[:, :, :], c_marks, PE.now())
                q_marks = []
                linear(use(U_L0["v"]), pairs[0], ready, q_out, [3, 4, 5, 6])
                x_marks = []

                def o_out(co, src, mark):
                    x_marks.append(DVE.step(lambda e: e.scalar_tensor_tensor(
                        xh[:, co, :], src, col("M_alpha"), xh[:, co, :], ALU.mult, ALU.add), mark))
                    return x_marks[-1]

                linear(use(U_L0["o"]), pairs[1], q_marks, o_out, [0, 1, 2, 7])
                x_ready[hf] = x_marks

            cross_attention_0(0)
            early_dma = Loads(sem("early_loaded"))
            at = 4 * P
            halves = (xa[:, :, :, :].rearrange("p a b c -> p (a b c)")[:, 0:P * HS // 2],
                      sx[:, :, :].rearrange("p a b -> p (a b)")[:, 0:P * HS // 2])
            early_dma.load(SY, block16[:, :], consts[:, 2 * P:3 * P])
            early_dma.load(SY, mean16[:, :], consts[:, 3 * P:4 * P])
            early_dma.load(SY, centre16[:, :], consts[:, at:at + P])
            early_dma.load(SY, collect[:, :], consts[:, at + P:at + 2 * P + HS - 1])
            at += 2 * P + HS - 1
            for i, dst in enumerate(halves):
                early_dma.load(SY, dst, consts[:, at + i * P * HS // 2:at + (i + 1) * P * HS // 2])
            early_dma.load(SY, s0_t[:, :, :, :], s0)
            c_ready = early_dma.load(SY, shift_t[:, :, :, :], shift)
            cross_attention_0(1)
            for i, src in enumerate(halves):
                pick_ready = SC.step(lambda e, i=i, r=src: e.activation(
                    pick[:, i * HS // 2:(i + 1) * HS // 2, :].rearrange("p a b -> p (a b)"), r, ACT.Copy), c_ready)

            barrier()
            PE.wait(c_ready)
            DVE.wait(c_ready)
            GP.wait(c_ready)
            SC.wait(c_ready)
            w4 = w_[:, :, :].rearrange("p c (b t) -> p c b t", b=HB)
            w_zero = DVE.step(lambda e: e.memset(w4[:, :, :, 0:1], 0.0))
            small_dma = Loads(sem("small_loaded"))
            xa_now = xa[:, :, :, 1:L + 1]
            xa_prev = xa[:, :, :, 0:L]

            def seq(tile):
                return tile.rearrange("p (b t) -> p b t", b=HB)

            def normalise_and_shift(layer, hf, name, which, ready, cen, sq, marks):
                prior = [PE.now(), DVE.now(), GP.now(), SC.now()]
                st = SC.step(lambda e: e.activation(xa[:, :, :, 0], shift_t[:, :, which, hf * HB:(hf + 1) * HB],
                                                    ACT.Copy), prior)

                affine = []

                def emit(ct, m):
                    affine.append(SC.step(lambda e: e.activation(
                        xa_now[:, ct, :, :], seq(cen[:, ct, :]), ACT.Identity,
                        bias=col(f"R{layer}_{name}_b", ct), scale=col(f"R{layer}_{name}_w", ct)), m, prior))

                yield from norm_parts(x[:, :, hf, :], cen[:, :, :], [sq[:, ct, :] for ct in range(CT)], ready, prior,
                                      0, 1, emit)
                for ct in range(CT):
                    d = DVE.step(lambda e, ct=ct: e.tensor_tensor(
                        seq(sx[:, ct, :]), xa_prev[:, ct, :, :], xa_now[:, ct, :, :], ALU.subtract), affine[ct], st, prior)
                    marks.append([d, affine[ct], st])

            def recurrent_half(layer, hf, small, xs, beside):
                def V(v, ct):
                    return col(f"R{layer}_{v}", ct)

                def shifted(dst, name, ct, xs, *free):
                    return DVE.step(lambda e: e.scalar_tensor_tensor(
                        seq(dst[:, ct, :]), seq(sx[:, ct, :]), V(name, ct), xa_now[:, ct, :, :],
                        ALU.mult, ALU.add), xs[ct], *free)

                xh = x[:, :, hf, :]
                xxx = tmp_b
                m = [shifted(xxx, "maa_x", ct, xs, PE.now()) for ct in range(CT)]
                affine_done = [SC.now(), DVE.now()]
                h1 = products(ps[:, 2, 0:HN], [(mix1_w[:, ct, 0:P], xxx[:, ct, :]) for ct in range(CT)],
                              small, bank_free[2], each=m)
                h1 = SC.step(lambda e: e.activation(tmp_a[:, 0, :], ps[:, 2, 0:HN], ACT.Tanh), h1, affine_done)
                bank_free[2] = h1
                h2 = products(ps[0:DM, 3, 0:HN], [(mix1_w[:, ct, P:P + DM], xxx[:, ct, :]) for ct in range(CT)],
                              bank_free[3])
                h2 = SC.step(lambda e: e.activation(tmp_a[0:DM, 1, :], ps[0:DM, 3, 0:HN], ACT.Tanh), h2, affine_done)
                bank_free[3] = h2
                names = ["w", "k", "v", "r", "g"] if layer == 0 else ["k", "w", "v", "r", "g"]

                def mix(name, dst, free):
                    f = names.index(name)
                    marks = []
                    for ct in range(CT):
                        lhsT, rhs = ((mix2_a[f * DM:(f + 1) * DM, ct * P:(ct + 1) * P], tmp_a[f * DM:(f + 1) * DM, 0, :])
                                     if f < 4 else (mix2_b[:, ct * P:(ct + 1) * P], tmp_a[0:DM, 1, :]))
                        m = products(ps[:, ct, 0:HN], [(lhsT, rhs)], h1, h2, bank_free[ct])
                        m = DVE.step(lambda e, ct=ct: e.scalar_tensor_tensor(
                            dst[:, ct, :], ps[:, ct, 0:HN], V("maa_" + name, ct), sx[:, ct, :],
                            ALU.add, ALU.mult), m, free)
                        bank_free[ct] = m
                        marks.append(GP.step(lambda e, ct=ct: e.tensor_tensor(
                            seq(dst[:, ct, :]), seq(dst[:, ct, :]), xa_now[:, ct, :, :], ALU.add), m))
                    return marks

                dest = {"k": k_, "v": v_, "r": r_, "g": sx}
                got = {}

                def project(name, pair, ready, *free):
                    marks = got[name] = []
                    func = ACT.Silu if name == "g" else ACT.Copy

                    def out_of(co, src, mark):
                        marks.append(SC.step(lambda e: e.activation(dest[name][:, co, :], src, func), mark, *free))
                        return marks[-1]

                    return linear(use(unit_r(layer, name)), pair, ready, out_of, [4, 5, 6, 7])

                start_free = PE.now()
                mixed_w = mix("w", ring[0], start_free)
                mixed_k = mix("k", ring[1], start_free)
                k_split = split(pairs[0], ring[1][:, :, :], mixed_k, start_free)
                m = products(ps[0:DD, 4, 0:HN], [(dec1_w[:, ct, :], ring[0][:, ct, :]) for ct in range(CT)],
                             bank_free[4], each=mixed_w)
                w_read = m
                m = SC.step(lambda e: e.activation(tmp_a[0:DD, 2, :], ps[0:DD, 4, 0:HN], ACT.Tanh), m, affine_done)
                bank_free[4] = m
                mixed_v = mix("v", ring[2], start_free)
                v_in_split = split(pairs[1], ring[2][:, :, :], mixed_v, start_free)
                w_marks = []
                for ct in range(CT):
                    q = products(ps[:, 4 + ct, 0:HN], [(dec2_w[:, ct * P:(ct + 1) * P], tmp_a[0:DD, 2, :])],
                                 m, bank_free[4 + ct])
                    q = SC.step(lambda e, ct=ct: e.activation(
                        tmp_a[:, 3, :], ps[:, 4 + ct, 0:HN], ACT.Exp, bias=V("decay", ct)), q, w_marks, affine_done)
                    bank_free[4 + ct] = q
                    w_marks.append(SC.step(lambda e, ct=ct: e.activation(
                        w4[:, ct, :, 1:L], seq(tmp_a[:, 3, :])[:, :, 0:L - 1], ACT.Exp, scale=-1.0), q, w_zero))
                k_used = project("k", pairs[0], k_split)
                mixed_r = mix("r", ring[0], w_read)
                r_split = split(pairs[0], ring[0][:, :, :], mixed_r, k_used)
                v_used = project("v", pairs[1], v_in_split)
                mixed_g = mix("g", ring[1], k_split)
                next_small = load_small(layer + 1) if layer == 0 and hf == NH - 1 else None
                g_split = split(pairs[1], ring[1][:, :, :], mixed_g, v_used)
                r_used = project("r", pairs[0], r_split)
                v_pair = pairs[0]
                v_split = split(v_pair, v_[:, :, :], got["v"], r_used)
                g_used = project("g", pairs[1], g_split, mixed_g)

                per = HS // 2
                turns = [(ct, jp) for ct in range(CT) for jp in range(per)]
                bufs = [ring[i // (GJ // 2)][:, i % (GJ // 2) * 2:i % (GJ // 2) * 2 + 2, :] for i in range(3 * GJ // 2)]
                buf_free = [[v_in_split, g_split, r_split]] * len(bufs)
                own, y_marks, start_marks, spread_marks, received, gathered = {}, [None] * CT, {}, {}, {}, {}

                def own_value(ct):
                    m = DVE.step(lambda e: e.scalar_tensor_tensor(
                        tmp_b[:, ct, :], r_[:, ct, :], V("u", ct), k_[:, ct, :], ALU.mult, ALU.mult),
                        got["r"], got["k"], h2)
                    own[ct] = m

                def own_sum(ct):
                    m = products(ps[:, 6, 0:HN], [(block16[:, :], tmp_b[:, ct, :])], own[ct], bank_free[6])
                    own[ct] = bank_free[6] = DVE.step(lambda e: e.tensor_tensor(
                        tmp_b[:, ct, :], ps[:, 6, 0:HN], v_[:, ct, :], ALU.mult), m, got["v"])

                def spread(t):
                    ct, jp = turns[t]
                    b0 = 2 * (t % 2)
                    for q in range(2):
                        sel = pick[:, jp * 2 + q, :]
                        spread_marks[t] = products(ps[:, b0 + q, 0:HN],
                                                   [(sel, v_pair[0][:, ct, :]), (sel, v_pair[1][:, ct, :])],
                                                   v_split, pick_ready, bank_free[b0 + q])

                def put_start(t):
                    ct, jp = turns[t]
                    buf4 = bufs[t % len(bufs)].rearrange("p j (b t) -> p j b t", b=HB)
                    start_marks[t] = SC.step(lambda e: e.activation(
                        buf4[:, :, :, 0], s0_t[:, ct, jp * 2:jp * 2 + 2, hf * HB:(hf + 1) * HB], ACT.Copy),
                        buf_free[t % len(bufs)])

                def scan(t):
                    ct, jp = turns[t]
                    b0 = 2 * (t % 2)
                    buf, free = bufs[t % len(bufs)], buf_free[t % len(bufs)]
                    buf4 = buf.rearrange("p j (b t) -> p j b t", b=HB)
                    key = seq(k_[:, ct, :])[:, :, 0:L - 1].unsqueeze(1).broadcast_to([P, 2, HB, L - 1])
                    m = DVE.step(lambda e: e.tensor_tensor(
                        buf4[:, :, :, 1:L],
                        ps[:, b0:b0 + 2, 0:HN].rearrange("p j (b t) -> p j b t", b=HB)[:, :, :, 0:L - 1],
                        key, ALU.mult), spread_marks[t], got["k"], free)
                    bank_free[b0] = bank_free[b0 + 1] = m
                    for q in range(2):
                        last = DVE.step(lambda e, q=q: e.tensor_tensor_scan(
                            buf[:, q, :], w_[:, ct, :], buf[:, q, :], 0.0, ALU.mult, ALU.add), m, start_marks[t], w_marks)
                    rb = r_[:, ct, :].unsqueeze(1).broadcast_to([P, 2, HN])
                    received[t] = GP.step(lambda e: e.tensor_tensor(buf, buf, rb, ALU.mult), last, got["r"])

                def gather(t):
                    ct, jp = turns[t]
                    buf = bufs[t % len(bufs)]
                    bank = 4 + ct % 2
                    PE.wait(received[t], bank_free[bank] if jp == 0 else None)
                    for q in range(2):
                        j = 2 * jp + q
                        what = lambda e, j=j, q=q: e.matmul(ps[:, bank, 0:HN], collect[:, HS - 1 - j:HS - 1 - j + P],
                                                            buf[:, q, :], start=(j == 0), stop=(j == HS - 1))
                        if q == 0:
                            PE.run(what)
                    gathered[ct] = buf_free[t % len(bufs)] = PE.step(what)

                def add_own(ct):
                    bank = 4 + ct % 2
                    own[ct] = bank_free[bank] = DVE.step(lambda e: e.tensor_tensor(
                        tmp_b[:, ct, :], tmp_b[:, ct, :], ps[:, bank, 0:HN], ALU.add), gathered[ct], own[ct])

                def centre(ct):
                    m = products(ps[:, 7, 0:HN], [(centre16[:, :], tmp_b[:, ct, :])], own[ct], bank_free[7])
                    m = SC.step(lambda e: e.activation(tmp_b[:, ct, :], ps[:, 7, 0:HN], ACT.Copy), m)
                    bank_free[7] = m
                    own[ct] = SC.step(lambda e: e.activation(tmp_a[:, ct, :], tmp_b[:, ct, :], ACT.Square), m, w_marks, h2,
                                      mixed_g)

                def deviation(ct):
                    m = products(ps[:, 7, 0:HN], [(mean16[:, :], tmp_a[:, ct, :])], own[ct], bank_free[7])
                    own[ct] = bank_free[7] = SC.step(lambda e: e.activation(
                        tmp_a[:, ct, :], ps[:, 7, 0:HN], ACT.Sqrt, bias=col("M_eps")), m)

                def invert(ct):
                    own[ct] = DVE.step(lambda e: e.reciprocal(tmp_a[:, ct, :], tmp_a[:, ct, :]), own[ct])

                def finish(ct):
                    m = GP.step(lambda e: e.tensor_tensor(tmp_b[:, ct, :], tmp_b[:, ct, :], tmp_a[:, ct, :], ALU.mult), own[ct])
                    m = SC.step(lambda e: e.activation(tmp_b[:, ct, :], tmp_b[:, ct, :], ACT.Identity,
                                                       bias=V("gn_b", ct), scale=V("gn_w", ct)), m)
                    own[ct] = GP.step(lambda e: e.tensor_tensor(tmp_b[:, ct, :], tmp_b[:, ct, :], sx[:, ct, :], ALU.mult),
                                      m, got["g"])

                def split_y(ct):
                    hi = SC.step(lambda e: e.activation(pairs[1][0][:, ct, :], tmp_b[:, ct, :], ACT.Copy), own[ct], g_used)
                    lo = GP.step(lambda e: e.tensor_tensor(pairs[1][1][:, ct, :], tmp_b[:, ct, :],
                                                           pairs[1][0][:, ct, :].bitcast(F32), ALU.subtract), hi, g_used)
                    y_marks[ct] = [hi, lo]

                LAG = 4
                parts = {1: add_own, 2: centre, 3: deviation, 5: invert, 6: finish, 7: split_y}
                put_start(0)
                put_start(1)
                spread(0)
                for t in range(len(turns) + LAG):
                    if t % per == 0 and t < len(turns):
                        own_value(t // per)
                    if t % per == 1 and t < len(turns):
                        own_sum(t // per)
                    if t < len(turns):
                        scan(t)
                    if t >= LAG:
                        gather(t - LAG)
                    if t + 2 < len(turns):
                        put_start(t + 2)
                    if t + 1 < len(turns):
                        spread(t + 1)
                    g = t - LAG - (per - 1)
                    if g >= 0 and g % per in parts:
                        parts[g % per](g // per)
                for part in (add_own, centre, deviation, invert, finish, split_y):
                    part(CT - 1)
                x_marks = []

                def add_x(co, src, mark):
                    x_marks.append(DVE.step(lambda e: e.tensor_tensor(xh[:, co, :], xh[:, co, :], src, ALU.add), mark))
                    return x_marks[-1]

                linear_by_input(use(unit_r(layer, "o")), pairs[1], y_marks, add_x, [2, 3, 4, 5])

                xs = []
                finish_parts(normalise_and_shift(layer, hf, "ln2", 0, x_marks, tmp_a, tmp_b, xs))
                rr = tmp_a
                free = [PE.now(), GP.now()]
                k_split, r_split = [], []
                for name, dst, pair, marks in (("fmaa_k", ring[0], pairs[0], k_split), ("fmaa_r", ring[1], pairs[1], r_split)):
                    his = []
                    for ct in range(CT + 1):
                        if ct < CT:
                            m = shifted(dst, name, ct, xs, free)
                            his.append(SC.step(lambda e, p=pair, d=dst, ct=ct: e.activation(
                                p[0][:, ct, :], d[:, ct, :], ACT.Copy), m, free))
                        if ct:
                            lo = DVE.step(lambda e, p=pair, d=dst, ct=ct - 1: e.tensor_tensor(
                                p[1][:, ct, :], d[:, ct, :], p[0][:, ct, :].bitcast(F32), ALU.subtract), his[ct - 1], free)
                            marks.append([his[ct - 1], lo])
                affine_done = SC.now()
                kk = ring[2]
                kk_marks, rr_marks = [], []

                def k_out(co, src, mark):
                    a = SC.step(lambda e: e.activation(kk[:, co, :], src, ACT.Relu), mark, free)
                    m = DVE.step(lambda e: e.tensor_tensor(kk[:, co, :], kk[:, co, :], kk[:, co, :], ALU.mult), a)
                    kk_done.append(m)
                    return a

                kk_done = []
                norm = beside()
                next(norm)
                k_used = linear_by_input(use(unit_r(layer, "fk")), pairs[0], k_split, k_out, [4, 5, 6, 7])
                for co in range(CT):
                    kk_marks.append(split_tile(pairs[0], co, kk[:, co, :], kk_done[co], k_used))

                def r_out(co, src, mark):
                    rr_marks.append(SC.step(lambda e: e.activation(rr[:, co, :], src, ACT.Sigmoid), mark, affine_done))
                    return rr_marks[-1]

                finish_parts(norm)
                linear(use(unit_r(layer, "fr")), pairs[1], r_split, r_out, [2, 3, 0, 1])
                x_marks = []

                def fv_out(co, src, mark):
                    m = DVE.step(lambda e: e.tensor_tensor(rr[:, co, :], rr[:, co, :], src, ALU.mult), mark, rr_marks)
                    x_marks.append(DVE.step(lambda e: e.tensor_tensor(
                        xh[:, co, :], xh[:, co, :], rr[:, co, :], ALU.add), m))
                    return m

                linear_by_input(use(unit_r(layer, "fv")), pairs[0], kk_marks, fv_out, [4, 5, 6, 7])
                x_ready[hf] = x_marks
                return next_small

            def next_norm(layer, hf):
                return normalise_and_shift(layer, hf, "ln1", 1, x_ready[hf], v_, k_, xs_next[0])

            stages = [[t[:, :, :].rearrange("p a b -> p (a b)")[:, 0:CT * SP].rearrange("p (a b) -> p a b", a=CT), None]
                      for t in (r_, k_, v_, w_)]
            stage_dma = [Loads(sem(f"late_ctx_loaded{i}")) for i in range(HB)]
            normed = ring[1]

            def first_of_l3(marks):
                prior = [q.now() for q in (PE, DVE, GP, SC)]
                for bb, stage in enumerate(stages):
                    stage[1] = stage_dma[bb].load(SY, stage[0], ctxT[bb], prior)

                def emit(ct, m):
                    marks.append(SC.step(lambda e: e.activation(
                        normed[:, ct, :], normed[:, ct, :], ACT.Identity, bias=col("X0_ln_b", ct),
                        scale=col("X0_ln_w", ct)), m))

                return norm_parts(x[:, :, 0, :], normed[:, :, :], [ring[0][:, i, :] for i in range(CT)], x_ready[0], prior,
                                  0, 1, emit)

            def load_small(layer):
                small_dma.load(SY, mix1_w[:, :, :], mix1[layer], PE.now())
                small_dma.load(SY, mix2_a[:, :], mix2[layer, 0:P, :])
                small_dma.load(SY, mix2_b[:, :], mix2[layer, P:P + DM, :])
                small_dma.load(SY, dec1_w[:, :, :], dec1[layer])
                return small_dma.load(SY, dec2_w[:, :], dec2[layer])

            xs_next = [[]]
            small = load_small(0)
            finish_parts(next_norm(0, 0))
            for layer in (0, 1):
                for hf in range(NH):
                    xs = xs_next[0]
                    xs_next[0] = []
                    if hf + 1 < NH:
                        beside = lambda: next_norm(layer, hf + 1)
                    elif layer == 0:
                        beside = lambda: next_norm(layer + 1, 0)
                    else:
                        beside = lambda: first_of_l3(xs_next[0])
                    next_small = recurrent_half(layer, hf, small, xs, beside)
                small = next_small

            barrier()

        with ExitStack() as late:
            ctx_pair = (sb(late, "ctx_hi", [P, HB, CT, SP], F32R), sb(late, "ctx_lo", [P, HB, CT, SP], F32R))
            v_pairs = [(sb(late, f"v_hi{i}", [P, 3, D], F32R), sb(late, f"v_lo{i}", [P, 3, D], F32R)) for i in range(2)]
            q_pair = (sb(late, "q_hi", [P, HG, HN], F32R), sb(late, "q_lo", [P, HG, HN], F32R))
            k_pair = (sb(late, "k_hi", [P, HG, SP], F32R), sb(late, "k_lo", [P, HG, SP], F32R))
            pt_both = [sb(late, f"pt{i}", [P, 3, 2, L], F32R) for i in range(2)]
            h_pair = (sb(late, "h_hi", [P, CT, HN], F32R), sb(late, "h_lo", [P, CT, HN], F32R))
            row_pair = sb(late, "row_pair", [1, 2, D], F32R)
            row_raw = sb(late, "row_raw", [P, 2, D])
            scratch = sb(late, "scratch", [P, T])
            soft = sb(late, "soft3", [P, 16])
            cen = scratch[:, :].rearrange("p (a b) -> p a b", a=CT)
            probs = [scratch[0:L, i * SP:(i + 1) * SP] for i in range(3)]
            o_raw = scratch[:, 3 * SP:3 * SP + HG * L].rearrange("p (h q) -> p h q", h=HG)
            squares = [row_raw[:, i, 0:HN] for i in range(2)]
            row_dma = Loads(sem("rows_loaded"))
            vrow_dma = [Loads(sem("vrow_moved0")), Loads(sem("vrow_moved1"))]
            out_dma = Loads(sem("stored"))
            SCALE = float(XK) ** -0.5
            BIAS_P = CH[2][1] - 1
            p_free = [None] * 3
            q_marks, k_marks, v_marks = [None] * HG, [None] * HG, [None] * 2
            col_marks, row_marks, row_ready = [None], [None, None], [None]
            o_marks, o_read = [], [None]
            blocks = {}
            later, item = [], [0]
            turn = [0, 0]

            def minus(dst, src, hi):
                return lambda e: e.tensor_tensor(dst, src, hi.bitcast(F32), ALU.subtract)

            ctx_ready, h_ready = [None] * HB, []

            def load_rows(att, g):
                row_ready[0] = row_dma.load(SY, row_raw[0:1, :, :], rows[att, g], DVE.now(), SC.now(), PE.now())

            def split_context(bb):
                stage, m = stages[bb]
                hi = SC.step(lambda e: e.activation(ctx_pair[0][:, bb, :, :], stage, ACT.Copy), m)
                lo = DVE.step(minus(ctx_pair[1][:, bb, :, :], stage, ctx_pair[0][:, bb, :, :]), hi, m)
                ctx_ready[bb] = [hi, lo]

            load_rows(0, 0)
            split_context(0)
            for ct in range(CT):
                h_ready.append(split_tile(h_pair, ct, normed[:, ct, :], xs_next[0][ct], None))
            for bb in range(1, HB):
                split_context(bb)
            k_free, v_free, pt_free, q_free = [list(h_ready)] * HG, [list(ctx_ready)] * 2, [list(h_ready)] * 2, [list(ctx_ready)]

            def next_context(hf, free):
                pieces = [(bb, ct) for bb in range(HB) for ct in range(CT)]
                loaded, read = [None] * len(pieces), [[PE.now(), DVE.now(), SC.now()]] * 2

                def load(n):
                    if n < len(pieces):
                        bb, ct = pieces[n]
                        loaded[n] = stage_dma[n % 2].load(SY, row_raw[:, n % 2, 0:SP], ctxT[hf * HB + bb, :, ct, :],
                                                          read[n % 2])

                load(0)
                load(1)
                for n, (bb, ct) in enumerate(pieces):
                    yield
                    src = row_raw[:, n % 2, 0:SP]
                    dst = [ctx_pair[i][:, bb, ct, :] for i in range(2)]
                    hi = SC.step(lambda e, d=dst[0], s=src: e.activation(d, s, ACT.Copy), loaded[n], free)
                    lo = DVE.step(minus(dst[1], src, dst[0]), hi, loaded[n], free)
                    read[n % 2] = [hi, lo]
                    load(n + 2)
                    if n == len(pieces) - 1:
                        ctx_ready[:] = [[hi, lo]] * HB

            def norm_to_pair(hf, name, ready, marks):
                prior = [q.now() for q in (PE, DVE, GP, SC)]

                his = []

                def emit(ct, m):
                    a = SC.step(lambda e: e.activation(cen[:, ct, :], cen[:, ct, :], ACT.Identity,
                                                       bias=col(name + "_ln_b", ct), scale=col(name + "_ln_w", ct)), m)
                    his.append([SC.step(lambda e: e.activation(h_pair[0][:, ct, :], cen[:, ct, :], ACT.Copy), a, prior), a])

                yield from norm_parts(x[:, :, hf, :], cen, squares, ready, prior, 3, 4, emit)
                for ct in range(CT):
                    lo = DVE.step(minus(h_pair[1][:, ct, :], cen[:, ct, :], h_pair[0][:, ct, :]), his[ct], prior)
                    marks.append([his[ct], lo])

            WEIGH, TURN, SCORE = range(3)

            def put(lag, rank, what):
                later.append((item[0] + lag, rank, what))

            def next_item(what):
                if what is not None:
                    what()
                item[0] += 1
                due = sorted((x for x in later if x[0] <= item[0]), key=lambda x: x[:2])
                later[:] = [x for x in later if x[0] > item[0]]
                for _, _, step in due:
                    step()

            def items(whats, norm=None):
                for what in whats:
                    next_item(what)
                    if norm is not None:
                        next(norm, None)

            def q_projection(group, h_ready):
                _, att, g = group

                def then(co):
                    put(2, SCORE, lambda: scores(group, 0, co))
                    next_item(None)

                def out_q(co, src, mark):
                    b = col(f"X{att}_bq", HG * g + co)
                    hi = SC.step(lambda e: e.activation(q_pair[0][:, co, :], src, ACT.Identity, bias=b), mark, q_free[0])
                    lo = DVE.step(lambda e: e.scalar_tensor_tensor(
                        q_pair[1][:, co, :], src, b, q_pair[0][:, co, :].bitcast(F32), ALU.add, ALU.subtract),
                        hi, q_free[0])
                    q_marks[co] = [hi, lo]
                    return [hi, lo]

                if g == 0:
                    linear_by_input(use(unit_x(att, "q", g)), h_pair, h_ready, out_q, [0, 1, 2, 7], then)
                else:
                    linear(use(unit_x(att, "q", g)), h_pair, h_ready, out_q, [0, 1, 2], then)

            def bias_slots(att, g):
                at = COL[f"X{att}_bias_k"] + HG * g
                kb = vec[:, at:at + HG]
                hi = SC.step(lambda e: e.activation(k_pair[0][:, :, S], kb, ACT.Copy), k_free)
                lo = DVE.step(minus(k_pair[1][:, :, S], kb, k_pair[0][:, :, S]), hi, k_free)
                col_marks[0] = [hi, lo]

            def bias_rows():
                d = DVE.step(lambda e: e.tensor_tensor(row_raw[0:1, 0, :], row_raw[0:1, 0, :], row_raw[0:1, 1, :],
                                                       ALU.subtract), row_ready[0])
                hi = SC.step(lambda e: e.activation(row_pair[:, 0, :], row_raw[0:1, 0, :], ACT.Copy), d, row_marks)
                lo = DVE.step(minus(row_pair[:, 1, :], row_raw[0:1, 0, :], row_pair[:, 0, :]), hi, row_marks)
                row_ready[0] = [hi, lo]

            def move_row(i):
                for part in range(2):
                    row_marks[i] = vrow_dma[i].load(
                        SY, v_pairs[i][part][BIAS_P:BIAS_P + 1, 2, :].bitcast(F32), row_pair[:, part, :].bitcast(F32),
                        row_ready[0], v_free[i])

            def value_tile(bb, c):
                i = bb % 2
                t0, n = CH[c]
                bank = turn[1] % 3
                turn[1] += 1
                blk = blocks["v"]
                s = order[blk][1]
                terms = []
                for ct in range(CT):
                    terms += three((ctx_pair[0][:, bb, ct, t0:t0 + n], ctx_pair[1][:, bb, ct, t0:t0 + n]),
                                   (w_hi[s][:, ct, :], w_lo[s][:, ct, :]))
                m = products(ps[0:n, bank, :], terms, ready_of[blk], ctx_ready[bb], bank_free[bank])
                if bb == HB - 1 and c == 2:
                    done(blk, m)
                n = min(n, S - t0)
                hi = SC.step(lambda e: e.activation(v_pairs[i][0][0:n, c, :], ps[0:n, bank, :], ACT.Copy), m, v_free[i])
                lo = DVE.step(minus(v_pairs[i][1][0:n, c, :], ps[0:n, bank, :], v_pairs[i][0][0:n, c, :]), hi, v_free[i])
                bank_free[bank] = [hi, lo]
                v_marks[i] = [hi, lo]

            def key_tile(group, bb, h, lag):
                _, att, g = group
                bank = turn[1] % 3
                turn[1] += 1
                blk = blocks["k"]
                s = order[blk][1]
                terms = []
                for ct in range(CT):
                    terms += three((w_hi[s][:, ct, h * XK:(h + 1) * XK], w_lo[s][:, ct, h * XK:(h + 1) * XK]),
                                   (ctx_pair[0][:, bb, ct, :], ctx_pair[1][:, bb, ct, :]))
                m = products(ps[:, bank, 0:SP], terms, ready_of[blk], ctx_ready[bb], bank_free[bank])
                if bb == HB - 1 and h == HG - 1:
                    done(blk, m)
                b = col(f"X{att}_bk", HG * g + h)
                hi = SC.step(lambda e: e.activation(k_pair[0][:, h, 0:S], ps[:, bank, 0:S], ACT.Identity, bias=b),
                             m, k_free[h])
                lo = DVE.step(lambda e: e.scalar_tensor_tensor(
                    k_pair[1][:, h, 0:S], ps[:, bank, 0:S], b, k_pair[0][:, h, 0:S].bitcast(F32),
                    ALU.add, ALU.subtract), hi, k_free[h])
                bank_free[bank] = [hi, lo]
                k_marks[h] = [hi, lo]
                if lag is not None:
                    put(lag, SCORE, lambda: scores(group, bb, h))

            def scores(group, bb, h):
                t = turn[0]
                turn[0] += 1
                bank, pr, st = 3 + t % 2, probs[t % 3], soft[0:L, 4 * (t % 4):4 * (t % 4) + 4]
                cols_b = slice(bb * L, (bb + 1) * L)
                m = products(ps[0:L, bank, 0:SP],
                             three((q_pair[0][:, h, cols_b], q_pair[1][:, h, cols_b]),
                                   (k_pair[0][:, h, :], k_pair[1][:, h, :])),
                             q_marks[h], k_marks[h], col_marks[0], bank_free[bank])
                k_free[h] = m
                src = ps[0:L, bank, 0:SP]
                m = DVE.step(lambda e: e.tensor_reduce(st[:, 0:1], src, AXX, ALU.max), m)
                m = DVE.step(lambda e: e.tensor_scalar(st[:, 1:2], st[:, 0:1], -SCALE, None, ALU.mult), m)
                m = SC.step(lambda e: e.activation(pr, src, ACT.Exp, bias=st[:, 1:2], scale=SCALE,
                                                   accum_out=st[:, 2:3]), m, p_free[t % 3])
                bank_free[bank] = m
                m = DVE.step(lambda e: e.reciprocal(st[:, 3:4], st[:, 2:3]), m)
                m = DVE.step(lambda e: e.tensor_scalar(pr, pr, st[:, 3:4], None, ALU.mult), m)
                put(2, TURN, lambda: turn_probs(group, bb, h, t, m))

            def turn_probs(group, bb, h, t, ready):
                bank, pt = 5 + t % 2, pt_both[t % 2]
                PE.wait(ready, bank_free[bank])
                for c, (t0, n) in enumerate(CH):
                    m = PE.step(lambda e, c=c, t0=t0, n=n: e.transpose(
                        ps[0:n, bank, c * L:(c + 1) * L], probs[t % 3][:, t0:t0 + n], ident[0:L, 0:L]))
                p_free[t % 3] = m
                parts = [(pt[0:n, c0:c1, 0, :], pt[0:n, c0:c1, 1, :],
                          ps[0:n, bank, c0 * L:c1 * L].rearrange("p (c q) -> p c q", q=L))
                         for c0, c1, n in ((0, 2, P), (2, 3, CH[2][1]))]
                for hi, _, src in parts:
                    m = SC.step(lambda e, d=hi, s=src: e.activation(d, s, ACT.Copy), m, pt_free[t % 2])
                marks = [m]
                for hi, lo, src in parts:
                    marks.append(DVE.step(minus(lo, src, hi), m, pt_free[t % 2]))
                bank_free[bank] = marks
                put(1, WEIGH, lambda: weigh(group, bb, h, t, marks))

            def weigh(group, bb, h, t, ready):
                _, att, g = group
                pt, v = pt_both[t % 2], v_pairs[bb % 2]
                PE.wait(ready, v_marks[bb % 2], row_marks[bb % 2], bank_free[7])
                for c, (_, n) in enumerate(CH):
                    hs = slice(h * XK, (h + 1) * XK)
                    both = lambda e, c=c, n=n: e.matmul(
                        ps[:, 7, 0:2 * L], v[0][0:n, c, hs], pt[0:n, c, :, :].rearrange("p a b -> p (a b)"),
                        start=(c == 0), stop=(c == 2))
                    single = lambda e, c=c, n=n: e.matmul(ps[:, 7, 0:L], v[1][0:n, c, hs], pt[0:n, c, 0, :],
                                                          start=False, stop=False)
                    if c < 2:
                        PE.run(both)
                        PE.run(single)
                    else:
                        PE.run(single)
                        m = PE.step(both)
                pt_free[t % 2] = m
                r = SC.step(lambda e: e.activation(o_raw[:, h, :], ps[:, 7, 0:L], ACT.Identity,
                                                   bias=col(f"X{att}_bv", HG * g + h)), m, o_read[0])
                r = DVE.step(lambda e: e.tensor_tensor(o_raw[:, h, :], o_raw[:, h, :], ps[:, 7, L:2 * L], ALU.add), r)
                bank_free[7] = r
                if h == HG - 1:
                    v_free[bb % 2] = m
                    dst = [q_pair[i][:, :, bb * L:(bb + 1) * L] for i in range(2)]
                    hi = SC.step(lambda e: e.activation(dst[0], o_raw, ACT.Copy), r)
                    lo = DVE.step(minus(dst[1], o_raw, dst[0]), hi)
                    o_read[0] = [hi, lo]
                    o_marks.extend([hi, lo])
                    if bb >= HB - 2 and group != groups[-1]:
                        move_row(bb % 2)

            def out_projection(group):
                hf, att, g = group
                xh, marks = x[:, :, hf, :], []

                def add_x(co, src, mark):
                    if g == 0:
                        m = DVE.step(lambda e: e.scalar_tensor_tensor(
                            xh[:, co, :], src, col(f"X{att}_bo", co), xh[:, co, :], ALU.add, ALU.add), mark)
                    else:
                        m = DVE.step(lambda e: e.tensor_tensor(xh[:, co, :], xh[:, co, :], src, ALU.add), mark)
                    marks.append(m)
                    return m

                q_free[0] = linear(use(unit_x(att, "o", g)), q_pair, list(o_marks), add_x, [0, 1, 2])
                o_marks.clear()
                return marks

            def mlp(hf, h_ready, following):
                xh = x[:, :, hf, :]
                context = next_context(hf + 1, PE.now()) if hf + 1 < NH else iter(())
                g_marks = []
                for g in range(NG):
                    prior = [PE.now(), list(g_marks)] if g else [q.now() for q in (PE, DVE, SC, GP)]
                    g_marks.clear()

                    def out_g(co, src, mark, g=g, prior=prior):
                        a = SC.step(lambda e: e.activation(cen[:, co, :], src, ACT.Gelu, bias=col("M_b1", CT * g + co)),
                                    mark, prior)
                        hi = SC.step(lambda e: e.activation(q_pair[0][:, co, :], cen[:, co, :], ACT.Copy), a, prior)
                        lo = DVE.step(minus(q_pair[1][:, co, :], cen[:, co, :], q_pair[0][:, co, :]), hi, prior)
                        g_marks.append([hi, lo])
                        next(context, None)
                        return a

                    (linear if g else linear_by_input)(use(unit_m(0, g)), h_pair, h_ready, out_g, [0, 1, 2, 3])
                    if g == NG - 1:
                        norm = following()

                    def add_mlp(co, src, mark, g=g):
                        if g == 0:
                            m = DVE.step(lambda e: e.scalar_tensor_tensor(
                                xh[:, co, :], src, col("M_b2", co), xh[:, co, :], ALU.add, ALU.add), mark)
                        else:
                            m = DVE.step(lambda e: e.tensor_tensor(xh[:, co, :], xh[:, co, :], src, ALU.add), mark)
                        if g == NG - 1:
                            out_dma.load(SY, out[:, co, hf, :], xh[:, co, :], m)
                        else:
                            next(context, None)
                        return m

                    q_free[0] = linear_by_input(use(unit_m(1, g)), q_pair, g_marks, add_mlp, [4, 5, 6, 7])
                return norm

            def values(group, bb):
                if bb == 0:
                    blocks["v"] = use(unit_x(group[1], "v", group[2]))
                return [lambda c=c: value_tile(bb, c) for c in range(3)]

            def keys(group, bb, lag):
                if bb == 0:
                    blocks["k"] = use(unit_x(group[1], "k", group[2]))
                return [lambda h=h: key_tile(group, bb, h, lag) for h in range(HG)]

            items(values(groups[0], 0))
            items(keys(groups[0], 0, None))
            bias_rows()
            move_row(0)
            move_row(1)
            items(values(groups[0], 1))

            for i, group in enumerate(groups):
                hf, att, g = group
                bias_slots(att, g)
                q_projection(group, h_ready)
                items(keys(group, 1, 2))
                after = groups[i + 1] if i + 1 < len(groups) else None
                if after:
                    load_rows(after[1], after[2])
                items(values(group, 2))
                if after:
                    bias_rows()
                for bb in range(2, HB):
                    items(keys(group, bb, 2))
                    if bb + 1 < HB:
                        items(values(group, bb + 1))
                if after and after[0] == hf:
                    items(values(after, 0))
                    K0 = keys(after, 0, None)
                    if after[1] == att:
                        items(K0)
                        out_projection(group)
                        items(values(after, 1))
                    else:
                        items(K0[:2])
                        x_marks = out_projection(group)
                        h_ready = []
                        norm = norm_to_pair(hf, f"X{after[1]}", x_marks, h_ready)
                        items(K0[2:], norm)
                        items(values(after, 1), norm)
                        finish_parts(norm)
                else:
                    items([None] * 5)
                    x_marks = out_projection(group)
                    h_ready = []
                    finish_parts(norm_to_pair(hf, "M", x_marks, h_ready))
                    if after:
                        h_next = []
                        norm = mlp(hf, h_ready, lambda: norm_to_pair(hf + 1, "X0", x_ready[hf + 1], h_next))
                        h_ready = h_next
                        items(values(after, 0), norm)
                        items(keys(after, 0, None), norm)
                        items(values(after, 1), norm)
                        finish_parts(norm)
                    else:
                        mlp(hf, h_ready, lambda: None)
            SY.wait((out_dma.sem, out_dma.count))

            with nc.Block() as block:
                @block.sync
                def _(e):
                    SY.play(e)

                @block.tensor
                def _(e):
                    PE.play(e)

                @block.vector
                def _(e):
                    DVE.play(e)

                @block.scalar
                def _(e):
                    SC.play(e)

                @block.gpsimd
                def _(e):
                    GP.play(e)


def kernel(**inputs):
    import concourse.bacc as bacc
    from concourse.bass_utils import run_bass_kernel_spmd

    get = {k: np.asarray(v) for k, v in inputs.items()}

    def tiles(w):
        return w.reshape(CT, P, w.shape[-1]).transpose(1, 0, 2)

    def column(v):
        return v.reshape(-1, P).T

    xT = tiles(get["x"].reshape(B * L, D).T).reshape(P, CT, NH, HN)
    c = get["ctx_2048"]
    ctxT = np.zeros((B, P, CT, SP), np.float32)
    ctxT[:, :, :, 0:S] = c.transpose(0, 2, 1).reshape(B, CT, P, S).transpose(0, 2, 1, 3)
    ctx_tok = np.zeros((B, 3 * P, D), np.float32)
    ctx_tok[:, 0:S] = c
    ctx_tok = ctx_tok.reshape(B, 3, P, D).transpose(0, 2, 1, 3)
    s0 = c[:, 2:2 + HS].reshape(B, CT, P // HS, HS, HS).transpose(2, 3, 1, 4, 0).reshape(P, CT, HS, B)
    shift = c[:, 0:2].reshape(B, 2, CT, P).transpose(3, 2, 1, 0)

    blocks = [get["L0_xattn_w_q"].T, get["L0_xattn_w_k"], get["L0_xattn_w_v"].T, get["L0_xattn_w_o"].T]
    r_names = [
        dict(k="Wk", v="Wv", r="Wr", g="Wg", o="Wo", fr="fWr", fk="fWk", fv="fWv", mix1="maa_w1", mix2="maa_w2",
             dec1="decay_w1", dec2="decay_w2", decay="time_decay", u="faaaa", fmaa_k="fmaa_k", fmaa_r="fmaa_r"),
        dict(k="Wk", v="Wv", r="Wr", g="Wg", o="Wo", fr="Wfr", fk="Wfk", fv="Wfv", mix1="maa_w1", mix2="maa_w2",
             dec1="td_w1", dec2="td_w2", decay="time_decay", u="u", fmaa_k="ffn_maa_k", fmaa_r="ffn_maa_r"),
    ]
    vectors, mix1, mix2, dec1, dec2 = [], [], [], [], []
    for layer, names in enumerate(r_names):
        pre = f"L{layer + 1}_xattn_"
        blocks += [get[pre + names[n]].T for n in R_ORDER]
        mix1.append(tiles(get[pre + names["mix1"]]))
        mix2.append(get[pre + names["mix2"]].reshape(5 * DM, D))
        dec1.append(tiles(get[pre + names["dec1"]]))
        dec2.append(get[pre + names["dec2"]])
        for v in R_VECS:
            if layer == 1 and v[:4] == "maa_" and v != "maa_x":
                vectors.append(column(get[pre + "maa_stack"][0, "kwvrg".index(v[4])]))
            else:
                vectors.append(column(get[pre + names.get(v, v)].reshape(D)))
    rows = []
    for att in (0, 1):
        n = str(att + 1)
        X = lambda name: get["L3_xattn_" + name + n]
        for g in range(NG):
            s = slice(g * D, (g + 1) * D)
            blocks += [X("wq")[:, s], X("wk")[:, s], X("wv")[:, s], X("wo")[s]]
        vectors += [column(get[f"L3_xattn_ln{n}_scale"]), column(get[f"L3_xattn_ln{n}_offset"])]
        vectors += [column(X("bq")), column(X("bk")), column(X("bv")), column(X("bias_k").reshape(-1)), column(X("bo"))]
        rows.append(np.stack([X("bias_v").reshape(NG, D), X("bv").reshape(NG, D)], 1)[:, None])
    w1, w2 = get["L3_xattn_w_fc1"], get["L3_xattn_w_fc2"]
    blocks += [w1[:, g * D:(g + 1) * D] for g in range(NG)] + [w2[g * D:(g + 1) * D] for g in range(NG)]
    vectors += [column(get["L3_xattn_ln_mlp_scale"]), column(get["L3_xattn_ln_mlp_offset"])]
    vectors += [column(get["L3_xattn_b_fc1"]), column(get["L3_xattn_b_fc2"])]
    vectors += [np.broadcast_to(get["L0_xattn_alpha"].reshape(1, 1), (P, 1)), np.full((P, 1), EPS, np.float32)]
    weights = np.stack([tiles(b).reshape(P, UNIT) for b in blocks])

    head = np.arange(P) // HS
    same = (head[:, None] == head[None, :]).astype(np.float32)
    collect = np.zeros((P, P + HS - 1), np.float32)
    collect[np.arange(P), HS * head + HS - 1] = 1.0
    pick = np.zeros((P, HS, P), np.float32)
    for j in range(HS):
        pick[HS * head + j, j, np.arange(P)] = 1.0
    consts = np.concatenate([np.eye(P, dtype=np.float32), np.full((P, P), 1.0 / D, np.float32), same,
                             same / np.float32(HS), np.eye(P, dtype=np.float32) - same / np.float32(HS), collect, pick.reshape(P, -1)], 1)

    arrays = {"xT": xT, "ctxT": ctxT, "ctx_tok": ctx_tok, "s0": s0, "shift": shift, "weights": weights,
              "mix1": np.stack(mix1), "mix2": np.stack(mix2), "dec1": np.stack(dec1), "dec2": np.stack(dec2),
              "cols": np.concatenate(vectors, 1), "rows": np.stack(rows), "consts": consts}
    arrays = {k: np.ascontiguousarray(v) for k, v in arrays.items()}
    nc = bacc.Bacc("TRN2", target_bir_lowering=False, num_devices=1)
    args = [nc.dram_tensor(k, v.shape, F32, kind="ExternalInput").ap() for k, v in arrays.items()]
    out = nc.dram_tensor("result", (P, CT, NH, HN), F32, kind="ExternalOutput").ap()
    build(nc, *args, out)
    got = run_bass_kernel_spmd(nc, [arrays], core_ids=[0]).results[0]["result"]
    return got.transpose(2, 3, 1, 0).reshape(B, L, D)
```
